# Optimizing a Trainium2 kernel written in Bass

```python
import numpy as np
import jax
import jax.numpy as jnp

def _softmax(x, axis=-1):
    return jax.nn.softmax(x, axis=axis)

def _gelu(x):
    return jax.nn.gelu(x, approximate=True)

def _silu(x):
    return jax.nn.silu(x)

def _sigmoid(x):
    return jax.nn.sigmoid(x)

def _layernorm(x, axis=-1, eps=1e-05):
    m = jnp.mean(x, axis=axis, keepdims=True)
    v = jnp.var(x, axis=axis, keepdims=True)
    return (x - m) / jnp.sqrt(v + eps)

def _scatter_add(tgt, idx, src, axis=0):
    return tgt.at[idx].add(src)

def _segment_sum(src, seg, n):
    return jax.ops.segment_sum(src, seg, n)
kernel_name = 'mk_seq_postln_d2_jaxref_r8_37ae21'

def setup_inputs(seed: int=0):
    np.random.seed(seed)
    _w = jnp.asarray

    def _L0_attn_setup():
        import jax, jax.numpy as jnp
        import numpy as np
        key = jax.random.key(seed)
        kx, kt = jax.random.split(key)
        b, n, d = (4, 512, 128)
        x = jax.random.normal(kx, (b, n, d), dtype=jnp.float32)
        t = jax.random.normal(kt, (n, d), dtype=jnp.float32)
        return {'x': x, 't': t}
    _L0_attn_in = _L0_attn_setup()

    def _L0_ffn_setup():
        import jax, jax.numpy as jnp
        import numpy as np
        B, T, C, H, E, K = (4, 128, 128, 128, 8, 2)

        def _swiglu(x):
            a, b = jnp.split(x, 2, axis=-1)
            return jax.nn.silu(a) * b
        key = jax.random.key(seed)
        ks = jax.random.split(key, 6)
        s = 0.02
        x = jax.random.normal(ks[0], (B, T, C), jnp.float32)
        w_shared_in = jax.random.normal(ks[1], (C, 2 * H), jnp.float32) * s
        w_shared_out = jax.random.normal(ks[2], (H, C), jnp.float32) * s
        w1_shared = jax.random.normal(ks[3], (C, 2 * H), jnp.float32) * s
        w2 = jax.random.normal(ks[4], (E, H, C), jnp.float32) * s
        w_gate = jax.random.normal(ks[5], (C, E), jnp.float32) * s
        gate_bias = jnp.zeros((E,), jnp.float32)
        return {'x': x, 'w_shared_in': w_shared_in, 'w_shared_out': w_shared_out, 'w1_shared': w1_shared, 'w2': w2, 'w_gate': w_gate, 'gate_bias': gate_bias}
    _L0_ffn_in = _L0_ffn_setup()

    def _L1_attn_setup():
        import jax, jax.numpy as jnp
        import numpy as np
        key = jax.random.key(seed)
        k1, k2, k3, k4, k5 = jax.random.split(key, 5)
        B, L, D = (4, 512, 128)
        return {'x': jax.random.normal(k1, (B, L, D), dtype=jnp.float32), 'phazor': jax.random.normal(k2, (D, 2), dtype=jnp.float32), 'phazor_init': jax.random.normal(k3, (D, 2), dtype=jnp.float32), 'last_conv_re': jax.random.normal(k4, (D,), dtype=jnp.float32), 'last_conv_im': jax.random.normal(k5, (D,), dtype=jnp.float32)}
    _L1_attn_in = _L1_attn_setup()

    def _L1_ffn_setup():
        import jax, jax.numpy as jnp
        import numpy as np
        B, T, C, H, E, K = (4, 128, 128, 128, 8, 2)

        def _swiglu(x):
            a, b = jnp.split(x, 2, axis=-1)
            return jax.nn.silu(a) * b
        key = jax.random.key(seed)
        ks = jax.random.split(key, 6)
        s = 0.02
        x = jax.random.normal(ks[0], (B, T, C), jnp.float32)
        w_shared_in = jax.random.normal(ks[1], (C, 2 * H), jnp.float32) * s
        w_shared_out = jax.random.normal(ks[2], (H, C), jnp.float32) * s
        w1_shared = jax.random.normal(ks[3], (C, 2 * H), jnp.float32) * s
        w2 = jax.random.normal(ks[4], (E, H, C), jnp.float32) * s
        w_gate = jax.random.normal(ks[5], (C, E), jnp.float32) * s
        gate_bias = jnp.zeros((E,), jnp.float32)
        return {'x': x, 'w_shared_in': w_shared_in, 'w_shared_out': w_shared_out, 'w1_shared': w1_shared, 'w2': w2, 'w_gate': w_gate, 'gate_bias': gate_bias}
    _L1_ffn_in = _L1_ffn_setup()
    _d = {'L0_attn_x': _L0_attn_in['x'], 'L0_attn_t': _L0_attn_in['t'], 'L0_ffn_w_shared_in': _L0_ffn_in['w_shared_in'], 'L0_ffn_w_shared_out': _L0_ffn_in['w_shared_out'], 'L0_ffn_w1_shared': _L0_ffn_in['w1_shared'], 'L0_ffn_w2': _L0_ffn_in['w2'], 'L0_ffn_w_gate': _L0_ffn_in['w_gate'], 'L0_ffn_gate_bias': _L0_ffn_in['gate_bias'], 'L1_attn_phazor': _L1_attn_in['phazor'], 'L1_attn_phazor_init': _L1_attn_in['phazor_init'], 'L1_attn_last_conv_re': _L1_attn_in['last_conv_re'], 'L1_attn_last_conv_im': _L1_attn_in['last_conv_im'], 'L1_ffn_w_shared_in': _L1_ffn_in['w_shared_in'], 'L1_ffn_w_shared_out': _L1_ffn_in['w_shared_out'], 'L1_ffn_w1_shared': _L1_ffn_in['w1_shared'], 'L1_ffn_w2': _L1_ffn_in['w2'], 'L1_ffn_w_gate': _L1_ffn_in['w_gate'], 'L1_ffn_gate_bias': _L1_ffn_in['gate_bias']}
    _x0 = _d['L0_attn_x']
    _d['L0_attn_x'] = jax.random.normal(jax.random.fold_in(jax.random.key(seed), 1), (4, 1024, 128), dtype=_x0.dtype)
    del _x0
    return _d

def reference(L0_attn_x, L0_attn_t, L0_ffn_w_shared_in, L0_ffn_w_shared_out, L0_ffn_w1_shared, L0_ffn_w2, L0_ffn_w_gate, L0_ffn_gate_bias, L1_attn_phazor, L1_attn_phazor_init, L1_attn_last_conv_re, L1_attn_last_conv_im, L1_ffn_w_shared_in, L1_ffn_w_shared_out, L1_ffn_w1_shared, L1_ffn_w2, L1_ffn_w_gate, L1_ffn_gate_bias):

    def _L0_attn_ref(x, t):
        import jax, jax.numpy as jnp
        import numpy as np
        b, n, d = x.shape
        L = 2 * n
        xf = jnp.fft.rfft(x.astype(jnp.float32), n=L, axis=1)
        tf = jnp.fft.rfft(t.astype(jnp.float32), n=L, axis=0)
        y = jnp.fft.irfft(xf * tf[None], n=L, axis=1)[:, :n, :]
        return y.astype(x.dtype)

    def _L0_ffn_ref(x, w_shared_in, w_shared_out, w1_shared, w2, w_gate, gate_bias):
        import jax, jax.numpy as jnp
        import numpy as np
        B, T, C, H, E, K = (4, 128, 128, 128, 8, 2)

        def _swiglu(x):
            a, b = jnp.split(x, 2, axis=-1)
            return jax.nn.silu(a) * b
        Bx, Tx, Cx = x.shape
        S = Bx * Tx
        fx = x.reshape(S, Cx)
        shared_out = _swiglu(fx @ w_shared_in) @ w_shared_out
        logits = fx @ w_gate + gate_bias
        probs = jax.nn.softmax(logits, axis=-1)
        top_val, top_idx = jax.lax.top_k(probs, K)
        wdense = jnp.zeros((S, E), probs.dtype).at[jnp.arange(S)[:, None], top_idx].add(top_val)
        hid = _swiglu(fx @ w1_shared)
        routed_out = jnp.zeros_like(shared_out)
        for e in range(E):
            routed_out = routed_out + wdense[:, e:e + 1] * (hid @ w2[e])
        return (shared_out + routed_out).reshape(Bx, Tx, Cx)

    def _L1_attn_ref(x, phazor, phazor_init, last_conv_re, last_conv_im):
        import jax, jax.numpy as jnp
        import numpy as np
        B, L, D = x.shape
        in_dtype = x.dtype
        x = x.astype(jnp.float32)
        ph = jax.lax.complex(phazor[:, 0], phazor[:, 1])
        ph_init = jax.lax.complex(phazor_init[:, 0], phazor_init[:, 1])
        last_conv = jax.lax.complex(last_conv_re, last_conv_im)
        mag = jnp.abs(ph)
        ph = ph / mag * jnp.exp(-mag)
        t = jnp.arange(L)[:, None]
        prog = ph[None, :] ** t
        filt = prog * ph_init[None, :]
        filt_fft = jnp.fft.fft(filt, n=2 * L, axis=0)
        x_fft = jnp.fft.fft(x, n=2 * L, axis=1)
        conv = jnp.fft.ifft(filt_fft[None, :, :] * x_fft, axis=1)[:, :L, :]
        conv_with_past = conv + last_conv[None, None, :] * prog[None, :, :] * ph[None, None, :]
        return conv_with_past.real.astype(in_dtype)

    def _L1_ffn_ref(x, w_shared_in, w_shared_out, w1_shared, w2, w_gate, gate_bias):
        import jax, jax.numpy as jnp
        import numpy as np
        B, T, C, H, E, K = (4, 128, 128, 128, 8, 2)

        def _swiglu(x):
            a, b = jnp.split(x, 2, axis=-1)
            return jax.nn.silu(a) * b
        Bx, Tx, Cx = x.shape
        S = Bx * Tx
        fx = x.reshape(S, Cx)
        shared_out = _swiglu(fx @ w_shared_in) @ w_shared_out
        logits = fx @ w_gate + gate_bias
        probs = jax.nn.softmax(logits, axis=-1)
        top_val, top_idx = jax.lax.top_k(probs, K)
        wdense = jnp.zeros((S, E), probs.dtype).at[jnp.arange(S)[:, None], top_idx].add(top_val)
        hid = _swiglu(fx @ w1_shared)
        routed_out = jnp.zeros_like(shared_out)
        for e in range(E):
            routed_out = routed_out + wdense[:, e:e + 1] * (hid @ w2[e])
        return (shared_out + routed_out).reshape(Bx, Tx, Cx)
    x = L0_attn_x
    x = _layernorm(x + _L0_attn_ref(x, L0_attn_t), axis=-1)
    x = _layernorm(x + _L0_ffn_ref(x, L0_ffn_w_shared_in, L0_ffn_w_shared_out, L0_ffn_w1_shared, L0_ffn_w2, L0_ffn_w_gate, L0_ffn_gate_bias), axis=-1)
    x = _layernorm(x + _L1_attn_ref(x, L1_attn_phazor, L1_attn_phazor_init, L1_attn_last_conv_re, L1_attn_last_conv_im), axis=-1)
    x = _layernorm(x + _L1_ffn_ref(x, L1_ffn_w_shared_in, L1_ffn_w_shared_out, L1_ffn_w1_shared, L1_ffn_w2, L1_ffn_w_gate, L1_ffn_gate_bias), axis=-1)
    return x

_drawn_inputs = setup_inputs


def setup_inputs(seed=0):
    import zlib

    import numpy as np

    out = dict(_drawn_inputs(seed))
    spreads = {'L0_ffn_gate_bias': (0.0, 0.8), 'L1_ffn_gate_bias': (0.0, 0.8)}
    factors = {'L0_ffn_w_shared_in': 8.0,
     'L0_ffn_w_shared_out': 8.0,
     'L0_ffn_w1_shared': 8.0,
     'L0_ffn_w2': 8.0,
     'L0_ffn_w_gate': 8.0,
     'L1_attn_last_conv_re': 7.005,
     'L1_attn_last_conv_im': 7.283,
     'L1_ffn_w_shared_in': 8.0,
     'L1_ffn_w_shared_out': 8.0,
     'L1_ffn_w1_shared': 8.0,
     'L1_ffn_w2': 8.0,
     'L1_ffn_w_gate': 8.0}
    for name, (base, spread) in spreads.items():
        noise = np.random.default_rng([zlib.crc32(name.encode()), seed]).standard_normal(out[name].shape)
        drawn = base * np.exp(spread * noise) if base else spread * noise
        out[name] = jnp.asarray(drawn.astype(out[name].dtype))
    for name, factor in factors.items():
        out[name] = (out[name] * factor).astype(out[name].dtype)
    return out
```

```python
import numpy as np
import concourse.bass as bass
from concourse import mybir
from contextlib import ExitStack

F32 = mybir.dt.float32
BF16 = mybir.dt.bfloat16
ALU = mybir.AluOpType
ACT = mybir.ActivationFunctionType
AX = mybir.AxisListType
ADD, SUB, MUL = ALU.add, ALU.subtract, ALU.mult

P = 128
BATCH, TIME = 4, 1024
TAPS = 512
CHUNKS = TIME // P
WIDE = BATCH * P
GROUP = 512
TILES = GROUP // P
EXPERTS = 8
EPS = 1e-5
FFT = 1536
BLOCKS = 6
ORDER = [1, 5, 3, 2, 4, 0]
ROOT = float(np.sqrt(3.0) / 2)
POOL_EXPERTS = (2, 5)
TAB_STEPS = 77


def dve_rank(e):
    return e - sum(p < e for p in POOL_EXPERTS)


def forward_matrices():
    m = np.zeros((BLOCKS, 4, P, P))
    n2, k2 = np.arange(P)[:, None], np.arange(P)[None, :]
    q_scale = {1: -1, 2: -ROOT, 3: -1, 4: -ROOT, 5: -1}
    for k1 in range(1, 6):
        angle = -2 * np.pi * (k1 + 12 * k2) * n2 / FFT
        c, s, q = np.cos(angle), np.sin(angle), q_scale[k1]
        m[k1] = c, -q * s, s, q * c
    j = np.arange(64)[None, :]
    at0, at6 = -2 * np.pi * 12 * j * n2 / FFT, -2 * np.pi * (6 + 12 * j) * n2 / FFT
    m[0, 0, :, :64], m[0, 2, :, :64] = np.cos(at0), np.sin(at0)
    m[0, 1, :, 64:], m[0, 3, :, 64:] = np.cos(at6), np.sin(at6)
    m[0, 2, :, 0] = np.cos(np.pi * n2[:, 0])
    return m.astype(np.float32)


def inverse_matrices():
    m = np.zeros((BLOCKS, 4, P, P))
    n2, k2 = np.arange(P)[None, :], np.arange(P)[:, None]
    s_scale = {1: 1, 2: ROOT, 3: 1, 4: ROOT, 5: 1}
    for k1 in range(1, 6):
        angle = 2 * np.pi * (k1 + 12 * k2) * n2 / FFT
        c, s, q = np.cos(angle) * 2 / FFT, np.sin(angle) * 2 / FFT, s_scale[k1]
        m[k1] = c, -s, -s * q, -c * q
    j = np.arange(64)[:, None]
    at0, at6 = 2 * np.pi * 12 * j * n2 / FFT, 2 * np.pi * (6 + 12 * j) * n2 / FFT
    m[0, 0, :64], m[0, 1, :64] = np.cos(at0) * 2 / FFT, -np.sin(at0) * 2 / FFT
    m[0, 0, 0] /= 2
    m[0, 1, 0] = np.cos(np.pi * n2[0]) / FFT
    m[0, 2, 64:], m[0, 3, 64:] = np.cos(at6) * 2 / FFT, -np.sin(at6) * 2 / FFT
    return m.astype(np.float32)


def constants():
    select = np.zeros((3 * EXPERTS, EXPERTS, P), np.float32)
    for e in range(EXPERTS):
        select[e::EXPERTS, e, :] = 1.0
    bin0 = np.zeros((P, 2), np.float32)
    bin0[0, 0] = 1.0
    bin0[1:, 1] = 1.0
    return {
        "fwd": np.ascontiguousarray(forward_matrices().transpose(2, 0, 1, 3)),
        "inv": np.ascontiguousarray(inverse_matrices().transpose(2, 0, 1, 3)),
        "ident": np.eye(P, dtype=np.float32),
        "select": select,
        "bin0": bin0,
        "rank": np.tile(np.arange(EXPERTS, 0, -1, dtype=np.float32), (P, 2 * TILES, 1)),
    }


def build(nc, d, out):
    ctx = ExitStack()
    with ctx:
        def sb(name, shape, dt=F32):
            return ctx.enter_context(nc.sbuf_tensor(name, shape, dt))

        def sem(name):
            return ctx.enter_context(nc.semaphore(name))

        slots = sb("slots", [P, 56, WIDE])
        x_in = [slots[:, n, :] for n in range(8)]
        y_all = slots[:, 0:8, :].rearrange("p n (b c) -> p n b c", b=BATCH)
        u = [[slots[:, 8 + 2 * k + i, :] for i in range(2)] for k in range(BLOCKS)]
        z = u
        work = [slots[:, 20 + n, :] for n in range(16)]
        spec = [[slots[:, 36 + 2 * k + i, :] for i in range(2)] for k in range(BLOCKS)]
        prod = [[slots[:, 48 + 4 * r + i, :] for i in range(4)] for r in range(2)]
        fwd = sb("fwd", [P, BLOCKS, 4, P])
        inv = sb("inv", [P, BLOCKS, 4, P])
        t_in = sb("t_in", [P, TAPS // P, P])
        t_u = sb("t_u", [P, BLOCKS, 2, P])
        t_w = sb("t_w", [P, 10, P])
        t_spec = sb("t_spec", [P, BLOCKS, 2, P])
        t_spec0 = sb("t_spec0", [P, 2, P])
        bin0 = sb("bin0", [P, 2])
        ident = sb("ident", [P, P])
        ident16 = sb("ident16", [P, P], BF16)
        select = sb("select", [3 * EXPERTS, EXPERTS, P], BF16)
        rank = sb("rank", [P, 2 * TILES, EXPERTS])
        w_sin = [sb(f"w_sin{l}", [P, 2 * P]) for l in range(2)]
        w_rin = [sb(f"w_rin{l}", [P, 2 * P]) for l in range(2)]
        w_sout = [sb(f"w_sout{l}", [P, P]) for l in range(2)]
        w_exp = [sb(f"w_exp{l}", [P, EXPERTS, P]) for l in range(2)]
        w_gate = [sb(f"w_gate{l}", [P, EXPERTS]) for l in range(2)]
        bias = [sb(f"bias{l}", [P, EXPERTS]) for l in range(2)]
        tok1 = sb("tok1", [P, 2, TILES, P])
        x1T = sb("x1T", [P, 2, GROUP])
        select_wide = x1T[0:3 * EXPERTS].rearrange("p g (e c) -> p (g e) c", c=P)
        tok2 = fwd[:, 0:2, :, :]
        tok3 = fwd[:, 2:4, :, :]
        tok4 = fwd[:, 4:6, :, :]
        x2T = inv[:, 0:2, :, :].rearrange("p a b c -> p a (b c)")
        x3T = inv[:, 2:4, :, :].rearrange("p a b c -> p a (b c)")
        y1T, zT, y2T = slots[:, 8:10, :], slots[:, 10:12, :], slots[:, 12:14, :]
        sil = slots[:, 14:16, :]
        h_shared = [slots[:, 16:18, :], slots[:, 38:40, :]]
        h_routed = [slots[:, 18:20, :], slots[:, 40:42, :]]
        scaled = slots[:, 20:28, :]
        wide_w = slots[:, 28:30, :]
        drive = [slots[:, 30 + 2 * i:32 + 2 * i, :].rearrange("p a b -> p (a b)") for i in range(2)]
        state = [slots[:, 34 + 2 * i:36 + 2 * i, :].rearrange("p a b -> p (a b)") for i in range(2)]
        wT = [sb(f"wT{l}", [3 * EXPERTS, 2, GROUP], BF16) for l in range(2)]
        NT = 2 * TILES
        logit, expo, prob, key, rest = (sb(n, [P, NT, EXPERTS]) for n in ("logit", "expo", "prob", "key", "rest"))
        pick = [sb(f"pick{i}", [P, NT, EXPERTS]) for i in range(2)]
        peak, total, rtotal, top, peak2 = (sb(n, [P, NT]) for n in ("peak", "total", "rtotal", "top", "peak2"))
        gate_w, left1, left2 = (sb(n, [P, NT, EXPERTS]) for n in ("gate_w", "left1", "left2"))
        parts = sb("parts", [P, NT, 3, EXPERTS], BF16)
        NB = [sb(f"bn{i}", [P, TILES, 6]) for i in range(2)]
        SM = [sb(f"sm{i}", [P, TILES, 2]) for i in range(2)]
        VE, NM, RS, SH, DM, QM, VR = ([sb(f"{n}{i}", [P, TILES]) for i in range(2)]
                                      for n in ("ve", "nm", "rs", "shift", "dm", "qm", "vr"))
        eps = sb("eps", [P, TILES])
        half_neg, half_pos = sb("half_neg", [P, TILES]), sb("half_pos", [P, TILES])
        euler = sb("euler", [P, NT * EXPERTS])
        phazor, phazor_init, last = sb("phazor", [P, 2]), sb("phazor_init", [P, 2]), sb("last", [P, 2])
        col = sb("col", [P, 16])
        powers = sb("powers", [P, 10, 4])
        cosT, sinT, in_re, in_im = (sb(n, [P, TIME]) for n in ("cosT", "sinT", "in_re", "in_im"))

        table_tmp = tok1[:].rearrange("p a t c -> p (a t c)")

        ps = [ctx.enter_context(nc.psum_tensor(f"ps{i}", [P, GROUP], F32)) for i in range(8)]
        x_ps = [[ps[2 * r], ps[2 * r + 1]] for r in range(3)]
        t_ps = [ps[6], ps[7]]
        to_tok, to_ch, route_ps, acc = ps[0], ps[1], ps[2], ps[5]
        w_ps = [ps[3], ps[4]]
        wT_ps = ps[2][0:3 * EXPERTS, :].bitcast(BF16)
        gate_ps, up_ps = ps[6], ps[7]

        x_loaded = [sem(f"x_loaded{n}") for n in range(CHUNKS)]
        t_loaded, param_loaded = sem("t_loaded"), sem("param_loaded")
        fwd_loaded = [sem(f"fwd_loaded{i}") for i in range(3)]
        inv_loaded, const_loaded = sem("inv_loaded"), sem("const_loaded")
        weights_loaded = [sem(f"weights_loaded{l}") for l in range(2)]
        set_up = sem("set_up")
        dve_t, dve_fwd, pool_fwd = sem("dve_t"), sem("dve_fwd"), sem("pool_fwd")
        t_block, x_block, t_kept = sem("t_block"), sem("x_block"), sem("t_kept")
        dve_t0 = sem("dve_t0")
        products, spectra, z_block, z_kept = sem("products"), sem("spectra"), sem("z_block"), sem("z_kept")
        dve_inv, pool_inv = sem("dve_inv"), sem("pool_inv")
        pool_col, dve_tab = sem("pool_col"), sem("dve_tab")
        dve_ln = [sem(f"dve_ln{i}") for i in range(2)]
        pool_ln = [sem(f"pool_ln{i}") for i in range(2)]
        normed = [sem(f"normed{i}") for i in range(2)]
        tok_ready, ch_ready, ch_copied = sem("tok_ready"), sem("ch_ready"), sem("ch_copied")
        logits_done, dve_gate, exp_done, wT_ready, wT_copied = (
            sem(n) for n in ("logits_done", "dve_gate", "exp_done", "wT_ready", "wT_copied"))
        gate_done, up_done, silu_done, h_done = (sem(n) for n in ("gate_done", "up_done", "silu_done", "h_done"))
        w_wide, w_kept, dve_scaled, pool_scaled = (sem(n) for n in ("w_wide", "w_kept", "dve_scaled", "pool_scaled"))
        expert_mm, acc_done, ffn_out = sem("expert_mm"), sem("acc_done"), sem("ffn_out")
        driven, scanned, turned, added = sem("driven"), sem("scanned"), sem("turned"), sem("added")
        cast = sem("cast")
        summed, dve_split = sem("summed"), sem("dve_split")
        tok4_free = [sem(f"tok4_free{g}") for g in range(2)]

        x_dram = d["L0_attn_x"].rearrange("b (n p) c -> p n b c", p=P)
        out_dram = out.rearrange("b (g n p) c -> p b g n c", p=P, g=2)

        T_DVE = ["delta", "re3", "V3", "A", "re1", "re5", "C", "V1", "V5", "Em", "Ep", "Fm", "Fp", "re2", "re4",
                 "k0", "k6"]
        FWD_DVE = ["d06", "d24", "s15", "d15", "A", "B", "H", "re1", "re5", "C", "V1", "V5", "F", "re3", "V3",
                   "G", "V2", "V4", "re2", "re4"]
        FWD_POOL = ["D", "E", "Em", "Ep", "Fm", "Fp", "k0", "k6"]
        INV_DVE = ["a", "rm", "cc", "sm", "t2", "r", "g", "v", "gv", "s", "um", "m", "o", "q", "t1", "y3",
                   "f", "w", "y2", "y4", "qr", "qm", "y1", "y5", "y7"]
        INV_POOL = ["aR", "p", "u", "e", "ep", "y0", "y6"]

        def after(steps, name):
            return steps.index(name) + 1

        GATE_STEPS = 22
        LN_STEPS = 9

        def s_next(i):
            return i * 2 + 1

        def s_mid(i):
            return i * 2

        def ch_use(i):
            if isinstance(i, int) and i == BATCH - 1:
                return {2: i * 6 + 2, 3: i * 6 + 4}
            return {1: i * 6 + 2, 2: i * 6 + 4, 3: i * 6 + 6}

        def tok_use(i):
            if isinstance(i, int) and i == 0:
                return {2: 0, 3: 2}
            return {2: i * 6 - 2, 3: i * 6, 4: i * 6 + 2}

        block = ctx.enter_context(nc.Block())

        @block.sync
        def _(sp):
            sp.dma_start(t_in[:], d["L0_attn_t"].rearrange("(n p) c -> p n c", p=P)).then_inc(t_loaded, 16)
            for n in (0, 6, 2, 4, 1, 5, 3, 7):
                sp.dma_start(x_in[n].rearrange("p (b c) -> p b c", b=BATCH), x_dram[:, n]).then_inc(x_loaded[n], 16)
            sp.dma_start(inv[:], d["inv"]).then_inc(inv_loaded, 16)
            for l in range(2):
                w = f"L{l}_ffn_"
                sp.dma_start(w_sin[l][:], d[w + "w_shared_in"]).then_inc(weights_loaded[l], 16)
                sp.dma_start(w_rin[l][:], d[w + "w1_shared"]).then_inc(weights_loaded[l], 16)
                sp.dma_start(w_sout[l][:], d[w + "w_shared_out"]).then_inc(weights_loaded[l], 16)
                sp.dma_start(w_exp[l][:], d[w + "w2"].rearrange("e h c -> h e c")).then_inc(weights_loaded[l], 16)
                sp.dma_start(w_gate[l][:], d[w + "w_gate"]).then_inc(weights_loaded[l], 16)
                sp.dma_start(bias[l][:], d[w + "gate_bias"].partition_broadcast(P)).then_inc(weights_loaded[l], 16)

            for g in range(2):
                sp.sem_inc(tok4_free[g], 16)

            def store(b, n):
                for g in range(2):
                    sp.wait_ge(normed[1], n + g + 1)
                    sp.dma_start(out_dram[:, b, g], tok4[:, g]).then_inc(tok4_free[g], 16)

            with sp.Fori(1, BATCH) as i:
                store(i - 1, tok_use(i)[4])
            store(BATCH - 1, tok_use(BATCH - 1)[4] + 2)
            for g in range(2):
                sp.wait_ge(tok4_free[g], 16 * (BATCH + 1))

        @block.tensor
        def _(pe):
            mm = nc.tensor.matmul

            u_ready = {1: ("re1", "V1", None), 5: ("re5", "V5", None), 3: ("re3", "V3", None),
                       2: ("re2", "V2", None), 4: ("re4", "V4", None), 0: (None, None, "k6")}
            pe.wait_ge(dve_t, len(T_DVE))
            for i, k in enumerate(ORDER):
                pe.wait_ge(fwd_loaded[i // 2], 16)
                if i >= 2:
                    pe.wait_ge(t_kept, i - 1)
                for o in range(2):
                    for q in range(2):
                        last = mm(t_ps[i % 2][:, o * P:(o + 1) * P], fwd[:, k, 2 * o + q, :], t_u[:, k, q, :],
                                  start=(q == 0), stop=(q == 1))
                last.then_inc(t_block, 1)
                names = [n for n in u_ready[k][:2] if n]
                if names:
                    pe.wait_ge(dve_fwd, max(after(FWD_DVE, n) for n in names))
                if u_ready[k][2]:
                    pe.wait_ge(pool_fwd, after(FWD_POOL, u_ready[k][2]))
                if i >= 3:
                    pe.wait_ge(products, 4 * (i - 2))
                for o in range(2):
                    for q in range(2):
                        last = mm(x_ps[i % 3][o][:], fwd[:, k, 2 * o + q, :], u[k][q], start=(q == 0), stop=(q == 1))
                last.then_inc(x_block, 1)
            pe.wait_ge(inv_loaded, 16)
            for i, k in enumerate(ORDER):
                pe.wait_ge(spectra, 2 * (i + 1))
                if i < 3:
                    pe.wait_ge(products, 4 * (i + 4))
                else:
                    pe.wait_ge(z_kept, 2 * (i - 2))
                for o in range(2):
                    for q in range(2):
                        last = mm(x_ps[i % 3][o][:], inv[:, k, 2 * o + q, :], spec[k][q], start=(q == 0), stop=(q == 1))
                last.then_inc(z_block, 1)

            def to_channels(tok, g, stage, norms, use, first=False):
                pe.wait_ge(normed[stage], norms + 1)
                if not first:
                    pe.wait_ge(ch_copied, use)
                for t in range(TILES):
                    last = nc.tensor.transpose(to_ch[:, t * P:(t + 1) * P], tok[:, g, t, :], ident[:])
                last.then_inc(ch_ready, 1)

            def to_tokens(yT, g, n, ready, count, first=False):
                pe.wait_ge(ready, count)
                if not first:
                    pe.wait_ge(normed[1], n)
                for t in range(TILES):
                    last = nc.tensor.transpose(to_tok[:, t * P:(t + 1) * P], yT[:, g, t * P:(t + 1) * P], ident[:])
                last.then_inc(tok_ready, 1)

            def logits(s, l, xT, use, first=False):
                pe.wait_ge(ch_copied, use)
                if not first:
                    pe.wait_ge(wT_copied, s)
                for t in range(2 * TILES):
                    last = mm(route_ps[:, t * EXPERTS:(t + 1) * EXPERTS],
                              xT[:, t // TILES, (t % TILES) * P:(t % TILES + 1) * P], w_gate[l][:],
                              start=True, stop=True)
                last.then_inc(logits_done, 1)

            def hidden(s, l, xT, unit, use, first=False):
                g, kind = unit // 2, unit % 2
                w = (w_sin[l], w_rin[l])[kind]
                pe.wait_ge(ch_copied, use)
                if not (first and unit == 0):
                    pe.wait_ge(h_done, s * 4 + unit)
                mm(gate_ps[:], w[:, 0:P], xT[:, g, :], start=True, stop=True).then_inc(gate_done, 1)
                mm(up_ps[:], w[:, P:2 * P], xT[:, g, :], start=True, stop=True).then_inc(up_done, 1)

            def turn_weights(s, l):
                pe.wait_ge(dve_gate, (s + 1) * GATE_STEPS)
                for t in range(2 * TILES):
                    last = nc.tensor.transpose(wT_ps[:, t * P:(t + 1) * P],
                                               parts[:, t].rearrange("p a e -> p (a e)"), ident16[:])
                last.then_inc(wT_ready, 1)

            def experts(s, l, hooks, first=False):
                def spread(g, e):
                    if e >= 2:
                        if e - 2 in POOL_EXPERTS:
                            pe.wait_ge(w_kept, (s * 2 + g) * 2 + POOL_EXPERTS.index(e - 2) + 1)
                        else:
                            pe.wait_ge(dve_scaled, (s * 2 + g) * 6 + dve_rank(e - 2) + 1)
                    elif not (first and g == 0):
                        pe.wait_ge(dve_scaled, (s * 2 + g) * 6 - 1 + e)
                    mm(w_ps[e % 2][:], select[:, e, :], wT[l][:, g, :], start=True, stop=True).then_inc(w_wide, 1)

                pe.wait_ge(wT_copied, s + 1)
                for g in range(2):
                    spread(g, 0)
                    spread(g, 1)
                    if not (first and g == 0):
                        pe.wait_ge(ffn_out, s * 2 + g)
                    pe.wait_ge(h_done, s * 4 + 2 * g + 2)
                    mm(acc[:], w_sout[l][:], h_shared[l][:, g, :], start=True, stop=False)
                    for e in range(EXPERTS):
                        if g == 1 and e in hooks:
                            hooks[e]()
                        if e in POOL_EXPERTS:
                            pe.wait_ge(pool_scaled, (s * 2 + g) * 2 + POOL_EXPERTS.index(e) + 1)
                        else:
                            pe.wait_ge(dve_scaled, (s * 2 + g) * 6 + dve_rank(e) + 1)
                        if e + 2 < EXPERTS:
                            spread(g, e + 2)
                        last = mm(acc[:], w_exp[l][:, e, :], scaled[:, e, :], start=False, stop=(e == EXPERTS - 1))
                        last.then_inc(expert_mm, 1)

            def body(i, s0, s1, started=True, mid=True, more=True):
                ch, tk = ch_use(i), tok_use(i)

                hooks = {1: lambda: to_tokens(y1T, 0, tk[2], ffn_out, s0 * 2 + 1, first=not mid)}
                if more:
                    hooks[3] = lambda: to_channels(tok1, 0, 0, (i + 1) * 2, ch[1])
                if mid:
                    hooks[5] = lambda: turn_weights(s_mid(i), 1)
                experts(s0, 0, hooks, first=not mid)
                if more:
                    hidden(s_next(i), 0, x1T, 0, ch[1] + 1)
                to_tokens(y1T, 1, tk[2] + 1, ffn_out, s0 * 2 + 2)
                if more:
                    to_channels(tok1, 1, 0, (i + 1) * 2 + 1, ch[1] + 1)
                    hidden(s_next(i), 0, x1T, 1, ch[1] + 1)
                to_channels(tok2, 0, 1, tk[2], ch[2])
                if more:
                    logits(s_next(i), 0, x1T, ch[1] + 2)
                    hidden(s_next(i), 0, x1T, 2, ch[1] + 2)
                to_channels(tok2, 1, 1, tk[2] + 1, ch[2] + 1)
                if more:
                    hidden(s_next(i), 0, x1T, 3, ch[1] + 2)

                def norm3():
                    to_channels(tok3, 0, 1, tk[3], ch[3])
                    if more:
                        turn_weights(s_next(i), 0)
                    to_tokens(zT, 1, tk[3] + 1, added, i * 2 + 2)

                if mid:
                    experts(s_mid(i), 1, {1: lambda: to_tokens(zT, 0, tk[3], added, i * 2 + 1), 5: norm3})
                else:
                    to_tokens(zT, 0, tk[3], added, i * 2 + 1)
                    norm3()
                hidden(s1, 1, x3T, 0, ch[3] + 1)
                hidden(s1, 1, x3T, 1, ch[3] + 1)
                to_channels(tok3, 1, 1, tk[3] + 1, ch[3] + 1)
                if mid:
                    to_tokens(y2T, 0, tk[4], ffn_out, s_mid(i) * 2 + 1)
                logits(s1, 1, x3T, ch[3] + 2)
                hidden(s1, 1, x3T, 2, ch[3] + 2)
                if mid:
                    to_tokens(y2T, 1, tk[4] + 1, ffn_out, s_mid(i) * 2 + 2)
                hidden(s1, 1, x3T, 3, ch[3] + 2)

            pe.wait_ge(const_loaded, 16 * 4)
            pe.wait_ge(cast, 2)
            to_channels(tok1, 0, 0, 0, 0, first=True)
            to_channels(tok1, 1, 0, 1, 1)
            pe.wait_ge(weights_loaded[0], 16 * 6)
            logits(0, 0, x1T, 2, first=True)
            for unit in range(4):
                hidden(0, 0, x1T, unit, 2, first=True)
            turn_weights(0, 0)
            pe.wait_ge(weights_loaded[1], 16 * 6)
            body(0, 0, 2, mid=False)
            with pe.Fori(1, BATCH - 1) as i:
                body(i, i * 2 - 1, i * 2 + 2)
            body(BATCH - 1, 2 * BATCH - 3, 2 * BATCH - 1, more=False)
            turn_weights(2 * BATCH - 1, 1)
            n = tok_use(BATCH - 1)[4] + 2
            experts(2 * BATCH - 1, 1, {1: lambda: to_tokens(y2T, 0, n, ffn_out, 4 * BATCH - 1)})
            to_tokens(y2T, 1, n + 1, ffn_out, 4 * BATCH)

        @block.scalar
        def _(act):
            act.dma_start(fwd[:, 1:6:4], d["fwd"][:, 1:6:4]).then_inc(fwd_loaded[0], 16)
            act.dma_start(fwd[:, 2:4], d["fwd"][:, 2:4]).then_inc(fwd_loaded[1], 16)
            act.dma_start(fwd[:, 0:5:4], d["fwd"][:, 0:5:4]).then_inc(fwd_loaded[2], 16)
            act.dma_start(bin0[:], d["bin0"]).then_inc(const_loaded, 16)
            act.dma_start(ident[:], d["ident"]).then_inc(const_loaded, 16)
            act.dma_start(select_wide, d["select"]).then_inc(const_loaded, 16)
            act.dma_start(rank[:], d["rank"]).then_inc(const_loaded, 16)
            act.dma_start(phazor[:], d["L1_attn_phazor"]).then_inc(param_loaded, 16)
            act.dma_start(phazor_init[:], d["L1_attn_phazor_init"]).then_inc(param_loaded, 16)
            act.dma_start(last[:, 0:1], d["L1_attn_last_conv_re"].rearrange("(p o) -> p o", o=1)).then_inc(param_loaded, 16)
            act.dma_start(last[:, 1:2], d["L1_attn_last_conv_im"].rearrange("(p o) -> p o", o=1)).then_inc(param_loaded, 16)

            for i, k in enumerate(ORDER[:-1]):
                act.wait_ge(t_block, i + 1)
                nc.scalar.activation(t_spec[:, k], t_ps[i % 2][:, 0:2 * P].rearrange("p (a c) -> p a c", a=2),
                                     ACT.Copy).then_inc(t_kept, 1)
            for i, k in enumerate(ORDER):
                act.wait_ge(z_block, i + 1)
                for o in range(2):
                    nc.scalar.activation(z[k][o], x_ps[i % 3][o][:], ACT.Copy).then_inc(z_kept, 1)

            def normalise(stage, n, source, tok, g):
                act.wait_ge(pool_ln[stage], (n + 1) * 3)
                for t in range(TILES):
                    last = nc.scalar.activation(tok[:, g, t, :], source(t), ACT.Identity,
                                                bias=SH[stage][:, t:t + 1], scale=RS[stage][:, t:t + 1])
                last.then_inc(normed[stage], 1)

            def norm1(b, g):
                normalise(0, b * 2 + g, lambda t: y_all[:, 4 * g + t, b, :], tok1, g)

            def norm_in(n, tok, g):
                normalise(1, n, lambda t: to_tok[:, t * P:(t + 1) * P], tok, g)

            def copy_channels(xT, g, use):
                act.wait_ge(ch_ready, use + 1)
                nc.scalar.activation(xT[:, g, :], to_ch[:], ACT.Copy).then_inc(ch_copied, 1)

            def silu(s, unit, first=False):
                act.wait_ge(gate_done, s * 4 + unit + 1)
                if not (first and unit < 2):
                    act.wait_ge(h_done, s * 4 + unit - 1)
                nc.scalar.activation(sil[:, unit % 2, :], gate_ps[:], ACT.Silu).then_inc(silu_done, 1)

            def exponentials(s):
                act.wait_ge(dve_gate, s * GATE_STEPS + 3)
                nc.scalar.activation(expo[:], logit[:], ACT.Exp).then_inc(exp_done, 1)

            def copy_weights(s, l):
                act.wait_ge(wT_ready, s + 1)
                nc.scalar.activation(wT[l][:].rearrange("p a c -> p (a c)"), wT_ps, ACT.Copy).then_inc(wT_copied, 1)

            def keep(s, g, first=False):
                for i, e in enumerate(POOL_EXPERTS):
                    act.wait_ge(w_wide, (s * 2 + g) * 8 + e + 1)
                    if not (first and g == 0):
                        act.wait_ge(pool_scaled, (s * 2 + g) * 2 + i - 1)
                    nc.scalar.activation(wide_w[:, i, :], w_ps[e % 2][:], ACT.Copy).then_inc(w_kept, 1)

            def body(i, s0, s1, mid=True, more=True):
                ch, tk = ch_use(i), tok_use(i)
                keep(s0, 0, first=not mid)
                if more:
                    norm1(i + 1, 0)
                    norm1(i + 1, 1)
                keep(s0, 1)
                if more:
                    act.wait_ge(ffn_out, s0 * 2 + 1)
                    copy_channels(x1T, 0, ch[1])
                norm_in(tk[2], tok2, 0)
                if mid:
                    copy_weights(s_mid(i), 1)
                if more:
                    silu(s_next(i), 0)
                norm_in(tk[2] + 1, tok2, 1)
                if more:
                    act.wait_ge(ffn_out, s0 * 2 + 2)
                    copy_channels(x1T, 1, ch[1] + 1)
                    silu(s_next(i), 1)
                copy_channels(x2T, 0, ch[2])
                if more:
                    silu(s_next(i), 2)
                    exponentials(s_next(i))
                copy_channels(x2T, 1, ch[2] + 1)
                if more:
                    silu(s_next(i), 3)
                if mid:
                    keep(s_mid(i), 0)
                    keep(s_mid(i), 1)
                norm_in(tk[3], tok3, 0)
                if mid:
                    act.wait_ge(ffn_out, s_mid(i) * 2 + 1)
                copy_channels(x3T, 0, ch[3])
                if more:
                    copy_weights(s_next(i), 0)
                silu(s1, 0)
                norm_in(tk[3] + 1, tok3, 1)
                silu(s1, 1)
                if mid:
                    act.wait_ge(ffn_out, s_mid(i) * 2 + 2)
                copy_channels(x3T, 1, ch[3] + 1)
                if mid:
                    act.wait_ge(tok4_free[0], i * 16)
                    norm_in(tk[4], tok4, 0)
                silu(s1, 2)
                exponentials(s1)
                if mid:
                    act.wait_ge(tok4_free[1], i * 16)
                    norm_in(tk[4] + 1, tok4, 1)
                silu(s1, 3)

            norm1(0, 0)
            norm1(0, 1)
            copy_channels(x1T, 0, 0)
            copy_channels(x1T, 1, 1)
            silu(0, 0, first=True)
            silu(0, 1, first=True)
            exponentials(0)
            silu(0, 2)
            silu(0, 3)
            copy_weights(0, 0)
            body(0, 0, 2, mid=False)
            with act.Fori(1, BATCH - 1) as i:
                body(i, i * 2 - 1, i * 2 + 2)
            body(BATCH - 1, 2 * BATCH - 3, 2 * BATCH - 1, more=False)
            s, n = 2 * BATCH - 1, tok_use(BATCH - 1)[4] + 2
            copy_weights(s, 1)
            keep(s, 0)
            keep(s, 1)
            for g in range(2):
                act.wait_ge(tok4_free[g], 16 * BATCH)
                norm_in(n + g, tok4, g)

        @block.gpsimd
        def _(pool):
            tt, ts_ = nc.gpsimd.tensor_tensor, nc.gpsimd.tensor_scalar
            nc.gpsimd.memset(half_neg[:], -0.5).then_inc(set_up, 1)
            nc.gpsimd.memset(eps[:], EPS).then_inc(set_up, 1)
            nc.gpsimd.memset(half_pos[:], 0.5).then_inc(set_up, 1)
            nc.gpsimd.memset(euler[:], float(np.e)).then_inc(set_up, 1)
            pool.wait_ge(param_loaded, 16 * 4)
            pool.wait_ge(set_up, 4)

            def step(ins, n):
                ins.then_inc(pool_col, 1)
                pool.wait_ge(pool_col, n)

            step(tt(col[:, 0:2], phazor[:], phazor[:], MUL), 1)
            step(tt(col[:, 2:3], col[:, 0:1], col[:, 1:2], ADD), 2)
            step(tt(col[:, 3:4], col[:, 2:3], half_pos[:, 0:1], ALU.pow), 3)
            step(tt(col[:, 4:5], col[:, 2:3], half_neg[:, 0:1], ALU.pow), 4)
            step(ts_(powers[:, 0, 0:2], phazor[:], col[:, 4:5], None, MUL), 5)
            step(ts_(col[:, 5:6], col[:, 3:4], -1.0, None, MUL), 6)
            step(tt(col[:, 6:7], euler[:, 0:1], col[:, 5:6], ALU.pow), 7)

            D, E, Em, Ep, Fm, Fp = (work[i] for i in (0, 1, 2, 3, 4, 5))
            F = work[12]
            x = x_in
            pool.wait_ge(x_loaded[2], 16)
            pool.wait_ge(x_loaded[4], 16)
            tt(D, x[2], x[4], ADD).then_inc(pool_fwd, 1)
            pool.wait_ge(x_loaded[0], 16)
            pool.wait_ge(x_loaded[6], 16)
            tt(E, x[0], x[6], ADD).then_inc(pool_fwd, 1)
            pool.wait_ge(x_loaded[3], 16)
            pool.wait_ge(pool_fwd, after(FWD_POOL, "E"))
            tt(Em, E, x[3], SUB).then_inc(pool_fwd, 1)
            tt(Ep, E, x[3], ADD).then_inc(pool_fwd, 1)
            pool.wait_ge(dve_fwd, after(FWD_DVE, "F"))
            tt(Fm, F, D, SUB).then_inc(pool_fwd, 1)
            tt(Fp, F, D, ADD).then_inc(pool_fwd, 1)
            pool.wait_ge(pool_fwd, after(FWD_POOL, "Fp"))
            tt(u[0][0], Ep, Fp, ADD).then_inc(pool_fwd, 1)
            tt(u[0][1], Em, Fm, SUB).then_inc(pool_fwd, 1)
            for i, k in enumerate(ORDER):
                pool.wait_ge(products, 4 * (i + 1))
                tt(spec[k][0], prod[i % 2][0], prod[i % 2][1], SUB).then_inc(spectra, 1)
                tt(spec[k][1], prod[i % 2][2], prod[i % 2][3], ADD).then_inc(spectra, 1)
            (R0, R6), (R1, S1), (R2, S2), (R3, S3), (R4, S4), (R5, S5) = z
            a, aR, p, uu, e, ep = work[0], work[10], work[4], work[6], work[8], work[11]
            pool.wait_ge(dve_inv, after(INV_DVE, "a"))
            pool.wait_ge(z_kept, 6)
            tt(aR, a, R3, ADD).then_inc(pool_inv, 1)
            pool.wait_ge(z_kept, 10)
            tt(p, R2, R4, ADD).then_inc(pool_inv, 1)
            tt(uu, S2, S4, ADD).then_inc(pool_inv, 1)
            pool.wait_ge(z_kept, 12)
            tt(e, R0, R6, ADD).then_inc(pool_inv, 1)
            pool.wait_ge(pool_inv, after(INV_POOL, "e"))
            tt(ep, e, p, ADD).then_inc(pool_inv, 1)
            pool.wait_ge(pool_inv, after(INV_POOL, "ep"))
            tt(x[0], ep, aR, ADD).then_inc(pool_inv, 1)
            tt(x[6], ep, aR, SUB).then_inc(pool_inv, 1)

            def scale_shift(stage, n, first=False):
                if not first:
                    pool.wait_ge(normed[stage], n)
                pool.wait_ge(dve_ln[stage], (n + 1) * LN_STEPS)
                tt(VE[stage][:], VR[stage][:], eps[:], ADD).then_inc(pool_ln[stage], 1)
                pool.wait_ge(pool_ln[stage], n * 3 + 1)
                tt(RS[stage][:], VE[stage][:], half_neg[:], ALU.pow).then_inc(pool_ln[stage], 1)
                pool.wait_ge(pool_ln[stage], n * 3 + 2)
                tt(SH[stage][:], NM[stage][:], RS[stage][:], MUL).then_inc(pool_ln[stage], 1)

            def scale_hidden(s, l, g, i, first=False):
                e = POOL_EXPERTS[i]
                pool.wait_ge(w_kept, (s * 2 + g) * 2 + i + 1)
                pool.wait_ge(h_done, s * 4 + 2 * g + 2)
                if not (first and g == 0):
                    pool.wait_ge(expert_mm, (s * 2 + g) * 8 - 7 + e)
                tt(scaled[:, e, :], wide_w[:, i, :], h_routed[l][:, g, :], MUL).then_inc(pool_scaled, 1)

            def drive_state(i, g, use, first=False):
                lo, hi = g * GROUP, (g + 1) * GROUP
                pool.wait_ge(ch_copied, use)
                if first:
                    pool.wait_ge(dve_tab, TAB_STEPS)
                else:
                    pool.wait_ge(added, i * 2)
                tt(drive[0][:, lo:hi], x2T[:, g, :], in_re[:, lo:hi], MUL).then_inc(driven, 1)
                tt(drive[1][:, lo:hi], x2T[:, g, :], in_im[:, lo:hi], MUL).then_inc(driven, 1)

            def body(i, s0, s1, mid=True, more=True):
                ch, tk = ch_use(i), tok_use(i)
                scale_hidden(s0, 0, 0, 0, first=not mid)
                scale_hidden(s0, 0, 0, 1, first=not mid)
                if more:
                    scale_shift(0, i * 2 + 2)
                    scale_shift(0, i * 2 + 3)
                scale_hidden(s0, 0, 1, 0)
                scale_shift(1, tk[2], first=not mid)
                scale_hidden(s0, 0, 1, 1)
                scale_shift(1, tk[2] + 1)
                drive_state(i, 0, ch[2] + 1, first=not mid)
                drive_state(i, 1, ch[2] + 2, first=not mid)
                if mid:
                    scale_hidden(s_mid(i), 1, 0, 0)
                    scale_hidden(s_mid(i), 1, 0, 1)
                    scale_hidden(s_mid(i), 1, 1, 0)
                scale_shift(1, tk[3])
                if mid:
                    scale_hidden(s_mid(i), 1, 1, 1)
                scale_shift(1, tk[3] + 1)
                if mid:
                    scale_shift(1, tk[4])
                    scale_shift(1, tk[4] + 1)

            scale_shift(0, 0, first=True)
            scale_shift(0, 1)
            body(0, 0, 2, mid=False)
            with pool.Fori(1, BATCH - 1) as i:
                body(i, i * 2 - 1, i * 2 + 2)
            body(BATCH - 1, 2 * BATCH - 3, 2 * BATCH - 1, more=False)
            s, n = 2 * BATCH - 1, tok_use(BATCH - 1)[4] + 2
            scale_hidden(s, 1, 0, 0)
            scale_hidden(s, 1, 0, 1)
            scale_hidden(s, 1, 1, 0)
            scale_shift(1, n)
            scale_hidden(s, 1, 1, 1)
            scale_shift(1, n + 1)

        @block.vector
        def _(dve):
            tt, ts_, stt = nc.vector.tensor_tensor, nc.vector.tensor_scalar, nc.vector.scalar_tensor_tensor

            t = [t_in[:, n, :] for n in range(4)]
            A, C, Em, Ep = (t_w[:, i, :] for i in range(4))
            U = [[t_u[:, k, i, :] for i in range(2)] for k in range(BLOCKS)]
            dve.wait_ge(t_loaded, 16)
            ts_(t[0][0:1, :], t[0][0:1, :], 1.0, None, ADD).then_inc(dve_t, 1)
            dve.wait_ge(dve_t, after(T_DVE, "delta"))
            tt(U[3][0], t[0], t[2], SUB).then_inc(dve_t, 1)
            tt(U[3][1], t[1], t[3], SUB).then_inc(dve_t, 1)
            stt(A, t[2], 0.5, t[0], MUL, ADD).then_inc(dve_t, 1)
            dve.wait_ge(dve_t, after(T_DVE, "A"))
            stt(U[1][0], t[1], ROOT, A, MUL, ADD).then_inc(dve_t, 1)
            stt(U[5][0], t[1], -ROOT, A, MUL, ADD).then_inc(dve_t, 1)
            stt(C, t[1], 0.5, t[3], MUL, ADD).then_inc(dve_t, 1)
            dve.wait_ge(dve_t, after(T_DVE, "C"))
            stt(U[1][1], t[2], ROOT, C, MUL, ADD).then_inc(dve_t, 1)
            stt(U[5][1], t[2], -ROOT, C, MUL, ADD).then_inc(dve_t, 1)
            tt(Em, t[0], t[3], SUB).then_inc(dve_t, 1)
            tt(Ep, t[0], t[3], ADD).then_inc(dve_t, 1)
            tt(U[4][1], t[1], t[2], SUB).then_inc(dve_t, 1)
            tt(U[2][1], t[1], t[2], ADD).then_inc(dve_t, 1)
            dve.wait_ge(dve_t, after(T_DVE, "Fp"))
            stt(U[2][0], U[4][1], 0.5, Em, MUL, ADD).then_inc(dve_t, 1)
            stt(U[4][0], U[2][1], -0.5, Ep, MUL, ADD).then_inc(dve_t, 1)
            tt(U[0][0], Ep, U[2][1], ADD).then_inc(dve_t, 1)
            tt(U[0][1], Em, U[4][1], SUB).then_inc(dve_t, 1)

            x = x_in
            D, E, Em, Ep, Fm, Fp, d06, d24, s15, d15, A, B, F, G, H, C = work

            def have(*chunks):
                for n in chunks:
                    dve.wait_ge(x_loaded[n], 16)

            def own(name):
                dve.wait_ge(dve_fwd, after(FWD_DVE, name))

            def pools(name):
                dve.wait_ge(pool_fwd, after(FWD_POOL, name))

            have(0, 6)
            tt(d06, x[0], x[6], SUB).then_inc(dve_fwd, 1)
            have(2, 4)
            tt(d24, x[2], x[4], SUB).then_inc(dve_fwd, 1)
            have(1, 5)
            tt(s15, x[1], x[5], ADD).then_inc(dve_fwd, 1)
            tt(d15, x[1], x[5], SUB).then_inc(dve_fwd, 1)
            own("d24")
            stt(A, d24, 0.5, d06, MUL, ADD).then_inc(dve_fwd, 1)
            have(3, 7)
            own("d15")
            tt(B, d15, x[7], SUB).then_inc(dve_fwd, 1)
            tt(H, s15, x[7], SUB).then_inc(dve_fwd, 1)
            own("B")
            stt(u[1][0], B, ROOT, A, MUL, ADD).then_inc(dve_fwd, 1)
            stt(u[5][0], B, -ROOT, A, MUL, ADD).then_inc(dve_fwd, 1)
            own("H")
            stt(C, H, 0.5, x[3], MUL, ADD).then_inc(dve_fwd, 1)
            own("C")
            pools("D")
            stt(u[1][1], D, ROOT, C, MUL, ADD).then_inc(dve_fwd, 1)
            stt(u[5][1], D, -ROOT, C, MUL, ADD).then_inc(dve_fwd, 1)
            tt(F, s15, x[7], ADD).then_inc(dve_fwd, 1)
            tt(u[3][0], d06, d24, SUB).then_inc(dve_fwd, 1)
            tt(u[3][1], H, x[3], SUB).then_inc(dve_fwd, 1)
            tt(G, d15, x[7], ADD).then_inc(dve_fwd, 1)
            own("G")
            tt(u[2][1], G, d24, ADD).then_inc(dve_fwd, 1)
            tt(u[4][1], G, d24, SUB).then_inc(dve_fwd, 1)
            pools("Fp")
            stt(u[2][0], Fm, 0.5, Em, MUL, ADD).then_inc(dve_fwd, 1)
            stt(u[4][0], Fp, -0.5, Ep, MUL, ADD).then_inc(dve_fwd, 1)

            def wide(ap):
                return ap.unsqueeze(1).to_broadcast([P, BATCH, P])

            for i, k in enumerate(ORDER):
                if k == 0:
                    dve.wait_ge(t_block, i + 1)
                    dve.wait_ge(const_loaded, 16 * 4)
                    tr, ti = t_ps[i % 2][:, 0:P], t_ps[i % 2][:, P:2 * P]
                    nc.vector.tensor_copy(t_spec[:, 0, 0, :], tr).then_inc(dve_t0, 1)
                    ts_(t_spec[:, 0, 1, :], ti, bin0[:, 1:2], None, MUL).then_inc(dve_t0, 1)
                    ts_(t_spec0[:, 1, :], ti, bin0[:, 0:1], None, MUL).then_inc(dve_t0, 1)
                    dve.wait_ge(dve_t0, 3)
                    stt(t_spec0[:, 0, :], tr, bin0[:, 1:2], t_spec0[:, 1, :], MUL, ADD).then_inc(dve_t0, 1)
                    dve.wait_ge(dve_t0, 4)
                else:
                    dve.wait_ge(t_kept, i + 1)
                dve.wait_ge(x_block, i + 1)
                if i >= 2:
                    dve.wait_ge(spectra, 2 * (i - 1))
                xr, xi = (x_ps[i % 3][o][:].rearrange("p (b c) -> p b c", b=BATCH) for o in range(2))
                tr, ti = wide(t_spec[:, k, 0, :]), wide(t_spec[:, k, 1, :])
                t4 = wide(t_spec0[:, 0, :]) if k == 0 else tr
                pr = [q.rearrange("p (b c) -> p b c", b=BATCH) for q in prod[i % 2]]
                tt(pr[0], xr, tr, MUL).then_inc(products, 1)
                tt(pr[1], xi, ti, MUL).then_inc(products, 1)
                tt(pr[2], xr, ti, MUL).then_inc(products, 1)
                tt(pr[3], xi, t4, MUL).then_inc(products, 1)

            dve.wait_ge(const_loaded, 16 * 4)
            nc.vector.tensor_copy(ident16[:], ident[:]).then_inc(cast, 1)
            nc.vector.tensor_copy(select[:], select_wide).then_inc(cast, 1)

            tab = [0]

            def tick(ins):
                tab[0] += 1
                ins.then_inc(dve_tab, 1)
                return tab[0]

            def at(n):
                dve.wait_ge(dve_tab, n)

            tmp = table_tmp
            dve.wait_ge(pool_col, 7)
            nc.vector.memset(cosT[:, 0:1], 1.0).then_inc(dve_tab, 1)
            nc.vector.memset(sinT[:, 0:1], 0.0).then_inc(dve_tab, 1)
            tab[0] = 2
            for j in range(10):
                n = 1 << j
                zr, zi = powers[:, j, 0:1], powers[:, j, 1:2]
                at(tab[0])
                tick(ts_(tmp[:, 0:n], sinT[:, 0:n], zi, None, MUL))
                tick(ts_(tmp[:, 512:512 + n], sinT[:, 0:n], zr, None, MUL))
                if j < 9:
                    tick(ts_(powers[:, j, 2:3], zi, zi, None, MUL))
                    tick(stt(powers[:, j + 1, 1:2], zr, 2.0, zi, MUL, MUL))
                at(tab[0])
                tick(stt(cosT[:, n:2 * n], cosT[:, 0:n], zr, tmp[:, 0:n], MUL, SUB))
                tick(stt(sinT[:, n:2 * n], cosT[:, 0:n], zi, tmp[:, 512:512 + n], MUL, ADD))
                if j < 9:
                    tick(stt(powers[:, j + 1, 0:1], zr, zr, powers[:, j, 2:3], MUL, SUB))
            pr_, pi_ = phazor_init[:, 0:1], phazor_init[:, 1:2]
            at(tab[0])
            tick(ts_(tmp[:, 0:1024], sinT[:], pi_, None, MUL))
            at(tab[0])
            tick(stt(in_re[:], cosT[:], pr_, tmp[:, 0:1024], MUL, ADD))
            at(tab[0])
            tick(ts_(tmp[:, 0:1024], sinT[:], pr_, None, MUL))
            at(tab[0])
            tick(stt(in_im[:], cosT[:], pi_, tmp[:, 0:1024], MUL, SUB))
            tick(ts_(col[:, 8:9], last[:, 1:2], powers[:, 0, 1:2], None, MUL))
            tick(ts_(col[:, 9:10], last[:, 1:2], powers[:, 0, 0:1], None, MUL))
            at(tab[0])
            tick(stt(col[:, 10:11], last[:, 0:1], powers[:, 0, 0:1], col[:, 8:9], MUL, SUB))
            tick(stt(col[:, 11:12], last[:, 0:1], powers[:, 0, 1:2], col[:, 9:10], MUL, ADD))
            assert tab[0] == TAB_STEPS, tab[0]

            (R0, R6), (R1, S1), (R2, S2), (R3, S3), (R4, S4), (R5, S5) = z
            a, rm, cc, sm, p, m, uu, v, e, o, aR, ep, t1, t2, f, g_ = work
            w, gv, q, r, qr, s_, qm, um = prod[0] + prod[1]

            def own(name):
                dve.wait_ge(dve_inv, after(INV_DVE, name))

            def pools(name):
                dve.wait_ge(pool_inv, after(INV_POOL, name))

            dve.wait_ge(z_kept, 4)
            tt(a, R1, R5, ADD).then_inc(dve_inv, 1)
            tt(rm, R1, R5, SUB).then_inc(dve_inv, 1)
            tt(cc, S1, S5, ADD).then_inc(dve_inv, 1)
            tt(sm, S1, S5, SUB).then_inc(dve_inv, 1)
            dve.wait_ge(z_kept, 6)
            dve.wait_ge(spectra, 2 * BLOCKS)
            own("cc")
            tt(t2, cc, S3, SUB).then_inc(dve_inv, 1)
            stt(r, cc, 0.5, S3, MUL, ADD).then_inc(dve_inv, 1)
            stt(g_, a, 0.5, R3, MUL, SUB).then_inc(dve_inv, 1)
            dve.wait_ge(z_kept, 10)
            tt(v, S2, S4, SUB).then_inc(dve_inv, 1)
            own("v")
            tt(gv, g_, v, ADD).then_inc(dve_inv, 1)
            pools("u")
            stt(s_, rm, ROOT, uu, MUL, ADD).then_inc(dve_inv, 1)
            stt(um, rm, -ROOT, uu, MUL, ADD).then_inc(dve_inv, 1)
            tt(m, R2, R4, SUB).then_inc(dve_inv, 1)
            dve.wait_ge(z_kept, 12)
            tt(o, R0, R6, SUB).then_inc(dve_inv, 1)
            own("o")
            stt(q, m, 0.5, o, MUL, ADD).then_inc(dve_inv, 1)
            tt(t1, o, m, SUB).then_inc(dve_inv, 1)
            own("t1")
            tt(x[3], t1, t2, ADD).then_inc(dve_inv, 1)
            pools("e")
            stt(f, p, -0.5, e, MUL, ADD).then_inc(dve_inv, 1)
            own("f")
            stt(w, sm, ROOT, f, MUL, ADD).then_inc(dve_inv, 1)
            own("w")
            tt(x[2], w, gv, ADD).then_inc(dve_inv, 1)
            tt(x[4], w, gv, SUB).then_inc(dve_inv, 1)
            tt(qr, q, r, ADD).then_inc(dve_inv, 1)
            tt(qm, q, r, SUB).then_inc(dve_inv, 1)
            own("qm")
            tt(x[1], qr, s_, ADD).then_inc(dve_inv, 1)
            tt(x[5], qr, s_, SUB).then_inc(dve_inv, 1)
            tt(x[7], qm, um, ADD).then_inc(dve_inv, 1)

            def moments(stage, n, source, first):
                for t_ in range(TILES):
                    nc.vector.bn_stats(NB[stage][:, t_, :], source(t_)).then_inc(dve_ln[stage], 1)
                done = n * LN_STEPS
                even, odd = NB[stage][:, :, 1:3], NB[stage][:, :, 4:6]
                dve.wait_ge(dve_ln[stage], done + 4)
                tt(SM[stage][:], even, odd, ADD).then_inc(dve_ln[stage], 1)
                tt(DM[stage][:], even[:, :, 0], odd[:, :, 0], SUB).then_inc(dve_ln[stage], 1)
                if not first:
                    dve.wait_ge(pool_ln[stage], n * 3)
                dve.wait_ge(dve_ln[stage], done + 5)
                ts_(NM[stage][:], SM[stage][:, :, 0], -0.5, None, MUL).then_inc(dve_ln[stage], 1)
                dve.wait_ge(dve_ln[stage], done + 6)
                stt(QM[stage][:], DM[stage][:], 0.25, DM[stage][:], MUL, MUL).then_inc(dve_ln[stage], 1)
                dve.wait_ge(dve_ln[stage], done + 8)
                stt(VR[stage][:], SM[stage][:, :, 1], 1.0 / P, QM[stage][:], MUL, ADD).then_inc(dve_ln[stage], 1)

            def moments1(b, g, first=False):
                moments(0, b * 2 + g, lambda t_: y_all[:, 4 * g + t_, b, :], first)

            def moments_in(n, first=False):
                dve.wait_ge(tok_ready, n + 1)
                moments(1, n, lambda t_: to_tok[:, t_ * P:(t_ + 1) * P], first)

            def spread(ap):
                return ap.unsqueeze(2).to_broadcast([P, NT, EXPERTS])

            def route_shift(s, l):
                dve.wait_ge(logits_done, s + 1)
                tt(logit[:], route_ps[:, 0:NT * EXPERTS].rearrange("p (a e) -> p a e", a=NT),
                   bias[l][:].unsqueeze(1).to_broadcast([P, NT, EXPERTS]), ADD).then_inc(dve_gate, 1)
                dve.wait_ge(dve_gate, s * GATE_STEPS + 1)
                nc.vector.tensor_reduce(peak[:], logit[:], AX.X, ALU.max).then_inc(dve_gate, 1)
                dve.wait_ge(dve_gate, s * GATE_STEPS + 2)
                tt(logit[:], logit[:], spread(peak[:]), SUB).then_inc(dve_gate, 1)

            def route_softmax(s):
                dve.wait_ge(exp_done, s + 1)
                nc.vector.tensor_reduce(total[:], expo[:], AX.X, ADD).then_inc(dve_gate, 1)
                dve.wait_ge(dve_gate, s * GATE_STEPS + 4)
                nc.vector.reciprocal(rtotal[:], total[:]).then_inc(dve_gate, 1)
                dve.wait_ge(dve_gate, s * GATE_STEPS + 5)
                tt(prob[:], expo[:], spread(rtotal[:]), MUL).then_inc(dve_gate, 1)
                dve.wait_ge(dve_gate, s * GATE_STEPS + 6)
                nc.vector.tensor_reduce(peak2[:], prob[:], AX.X, ALU.max).then_inc(dve_gate, 1)

            def route_pick(s, i, values):
                done = s * GATE_STEPS + 7 + 6 * i
                dve.wait_ge(dve_gate, done)
                tt(key[:], values[:], spread(peak2[:]), ALU.is_equal).then_inc(dve_gate, 1)
                dve.wait_ge(dve_gate, done + 1)
                tt(key[:], key[:], rank[:], MUL).then_inc(dve_gate, 1)
                dve.wait_ge(dve_gate, done + 2)
                nc.vector.tensor_reduce(top[:], key[:], AX.X, ALU.max).then_inc(dve_gate, 1)
                dve.wait_ge(dve_gate, done + 3)
                tt(pick[i][:], key[:], spread(top[:]), ALU.is_equal).then_inc(dve_gate, 1)

            def route_rest(s):
                dve.wait_ge(dve_gate, s * GATE_STEPS + 11)
                stt(rest[:], pick[0][:], -2.0, prob[:], MUL, ADD).then_inc(dve_gate, 1)
                dve.wait_ge(dve_gate, s * GATE_STEPS + 12)
                nc.vector.tensor_reduce(peak2[:], rest[:], AX.X, ALU.max).then_inc(dve_gate, 1)

            def route_weights(s):
                dve.wait_ge(dve_gate, s * GATE_STEPS + 17)
                tt(key[:], pick[0][:], pick[1][:], ADD).then_inc(dve_gate, 1)
                dve.wait_ge(dve_gate, s * GATE_STEPS + 18)
                tt(gate_w[:], key[:], prob[:], MUL).then_inc(dve_gate, 1)

            def route_split(s, first=False):
                dve.wait_ge(dve_gate, s * GATE_STEPS + 19)
                if not first:
                    dve.wait_ge(wT_ready, s)
                nc.vector.tensor_copy(parts[:, :, 0, :], gate_w[:]).then_inc(dve_gate, 1)
                dve.wait_ge(dve_gate, s * GATE_STEPS + 20)
                tt(left1[:], gate_w[:], parts[:, :, 0, :], SUB).then_inc(dve_split, 1)
                dve.wait_ge(dve_split, s * 2 + 1)
                nc.vector.tensor_copy(parts[:, :, 1, :], left1[:]).then_inc(dve_gate, 1)
                dve.wait_ge(dve_gate, s * GATE_STEPS + 21)
                tt(left2[:], left1[:], parts[:, :, 1, :], SUB).then_inc(dve_split, 1)
                dve.wait_ge(dve_split, s * 2 + 2)
                nc.vector.tensor_copy(parts[:, :, 2, :], left2[:]).then_inc(dve_gate, 1)

            def route(s, part, first=False):
                if part == 0:
                    route_softmax(s)
                elif part == 1:
                    route_pick(s, 0, prob)
                elif part == 2:
                    route_rest(s)
                elif part == 3:
                    route_pick(s, 1, rest)
                elif part == 4:
                    route_weights(s)
                elif part == 5:
                    route_split(s, first)

            def hidden(s, l, unit):
                g, kind = unit // 2, unit % 2
                dve.wait_ge(silu_done, s * 4 + unit + 1)
                dve.wait_ge(up_done, s * 4 + unit + 1)
                dst = (h_shared, h_routed)[kind][l]
                tt(dst[:, g, :], up_ps[:], sil[:, kind, :], MUL).then_inc(h_done, 1)

            def scale_hidden(s, l, g, e, first=False):
                dve.wait_ge(w_wide, (s * 2 + g) * 8 + e + 1)
                if not (first and g == 0):
                    dve.wait_ge(expert_mm, (s * 2 + g) * 8 - 7 + e)
                tt(scaled[:, e, :], w_ps[e % 2][:], h_routed[l][:, g, :], MUL).then_inc(dve_scaled, 1)

            def residual(s, g, xT, yT):
                dve.wait_ge(expert_mm, (s * 2 + g) * 8 + 8)
                tt(yT[:, g, :], acc[:], xT[:, g, :], ADD).then_inc(ffn_out, 1)

            def scan_state(i, g):
                lo, hi = g * GROUP, (g + 1) * GROUP
                for part in range(2):
                    dve.wait_ge(driven, i * 4 + 2 * g + part + 1)
                    start = col[:, 10 + part:11 + part] if g == 0 else state[part][:, lo - 1:lo]
                    nc.vector.tensor_tensor_scan(state[part][:, lo:hi], col[:, 6:7].to_broadcast([P, GROUP]),
                                                 drive[part][:, lo:hi], start, MUL, ADD).then_inc(scanned, 1)

            def turn_state(i, g):
                lo, hi = g * GROUP, (g + 1) * GROUP
                dve.wait_ge(scanned, i * 4 + 2 * g + 2)
                tt(drive[0][:, lo:hi], state[0][:, lo:hi], cosT[:, lo:hi], MUL).then_inc(turned, 1)
                tt(drive[1][:, lo:hi], state[1][:, lo:hi], sinT[:, lo:hi], MUL).then_inc(turned, 1)

            def add_state(i, g):
                lo, hi = g * GROUP, (g + 1) * GROUP
                dve.wait_ge(turned, i * 4 + 2 * g + 2)
                tt(drive[0][:, lo:hi], drive[0][:, lo:hi], drive[1][:, lo:hi], SUB).then_inc(summed, 1)
                dve.wait_ge(summed, i * 2 + g + 1)
                tt(zT[:, g, :], drive[0][:, lo:hi], x2T[:, g, :], ADD).then_inc(added, 1)

            def body(i, s0, s1, mid=True, more=True):
                tk = tok_use(i)
                dve.wait_ge(h_done, s0 * 4 + 4)
                for e in (0, 1, 3):
                    scale_hidden(s0, 0, 0, e, first=not mid)
                    if mid:
                        route(s_mid(i), (0, 1, None, 2)[e])
                scale_hidden(s0, 0, 0, 4, first=not mid)
                if more:
                    moments1(i + 1, 0)
                scale_hidden(s0, 0, 0, 6, first=not mid)
                if more:
                    moments1(i + 1, 1)
                scale_hidden(s0, 0, 0, 7, first=not mid)
                if mid:
                    route(s_mid(i), 3)
                residual(s0, 0, x1T, y1T)
                scale_hidden(s0, 0, 1, 0)
                if mid:
                    route(s_mid(i), 4)
                scale_hidden(s0, 0, 1, 1)
                moments_in(tk[2], first=not mid)
                if mid:
                    route(s_mid(i), 5)
                for e in (3, 4, 6, 7):
                    scale_hidden(s0, 0, 1, e)
                residual(s0, 1, x1T, y1T)
                if more:
                    hidden(s_next(i), 0, 0)
                moments_in(tk[2] + 1)
                if more:
                    hidden(s_next(i), 0, 1)
                    route_shift(s_next(i), 0)
                    hidden(s_next(i), 0, 2)
                    hidden(s_next(i), 0, 3)
                if mid:
                    scale_hidden(s_mid(i), 1, 0, 0)
                    scale_hidden(s_mid(i), 1, 0, 1)
                scan_state(i, 0)
                if mid:
                    scale_hidden(s_mid(i), 1, 0, 3)
                turn_state(i, 0)
                if mid:
                    scale_hidden(s_mid(i), 1, 0, 4)
                add_state(i, 0)
                if more:
                    route(s_next(i), 0)
                if mid:
                    scale_hidden(s_mid(i), 1, 0, 6)
                if more:
                    route(s_next(i), 1)
                if mid:
                    scale_hidden(s_mid(i), 1, 0, 7)
                scan_state(i, 1)
                if more:
                    route(s_next(i), 2)
                if mid:
                    residual(s_mid(i), 0, x3T, y2T)
                    scale_hidden(s_mid(i), 1, 1, 0)
                turn_state(i, 1)
                if more:
                    route(s_next(i), 3)
                if mid:
                    scale_hidden(s_mid(i), 1, 1, 1)
                add_state(i, 1)
                moments_in(tk[3])
                if more:
                    route(s_next(i), 4)
                if mid:
                    scale_hidden(s_mid(i), 1, 1, 3)
                if more:
                    route(s_next(i), 5)
                if mid:
                    for e in (4, 6, 7):
                        scale_hidden(s_mid(i), 1, 1, e)
                if mid:
                    residual(s_mid(i), 1, x3T, y2T)
                hidden(s1, 1, 0)
                moments_in(tk[3] + 1)
                hidden(s1, 1, 1)
                if mid:
                    moments_in(tk[4])
                route_shift(s1, 1)
                hidden(s1, 1, 2)
                if mid:
                    moments_in(tk[4] + 1)
                hidden(s1, 1, 3)

            dve.wait_ge(pool_inv, len(INV_POOL))
            dve.wait_ge(dve_inv, len(INV_DVE))
            moments1(0, 0, first=True)
            moments1(0, 1)
            dve.wait_ge(weights_loaded[0], 16 * 6)
            route_shift(0, 0)
            hidden(0, 0, 0)
            hidden(0, 0, 1)
            route_softmax(0)
            hidden(0, 0, 2)
            route(0, 1)
            hidden(0, 0, 3)
            for part in range(2, 6):
                route(0, part, first=True)
            dve.wait_ge(weights_loaded[1], 16 * 6)
            body(0, 0, 2, mid=False)
            with dve.Fori(1, BATCH - 1) as i:
                body(i, i * 2 - 1, i * 2 + 2)
            body(BATCH - 1, 2 * BATCH - 3, 2 * BATCH - 1, more=False)
            s, n = 2 * BATCH - 1, tok_use(BATCH - 1)[4] + 2
            for part in range(6):
                route(s, part)
            for g in range(2):
                for e in range(EXPERTS):
                    if e not in POOL_EXPERTS:
                        scale_hidden(s, 1, g, e)
                    if g == 1 and e == 1:
                        moments_in(n)
                residual(s, g, x3T, y2T)
            moments_in(n + 1)


INPUTS = ["L0_attn_x", "L0_attn_t", "L0_ffn_w_shared_in", "L0_ffn_w_shared_out", "L0_ffn_w1_shared", "L0_ffn_w2",
          "L0_ffn_w_gate", "L0_ffn_gate_bias", "L1_attn_phazor", "L1_attn_phazor_init", "L1_attn_last_conv_re",
          "L1_attn_last_conv_im", "L1_ffn_w_shared_in", "L1_ffn_w_shared_out", "L1_ffn_w1_shared", "L1_ffn_w2",
          "L1_ffn_w_gate", "L1_ffn_gate_bias"]


def kernel(**inputs):
    import concourse.bacc as bacc
    from concourse.bass_utils import run_bass_kernel_spmd

    nc = bacc.Bacc("TRN2", target_bir_lowering=False, num_devices=1)
    arrays, aps = {}, {}
    for name, value in [(n, inputs[n]) for n in INPUTS] + list(constants().items()):
        a = np.ascontiguousarray(value)
        arrays[f"in_{name}"] = a
        aps[name] = nc.dram_tensor(f"in_{name}", a.shape, mybir.dt.from_np(a.dtype), kind="ExternalInput").ap()
    out = nc.dram_tensor("out_0", (BATCH, TIME, P), F32, kind="ExternalOutput").ap()
    build(nc, aps, out)
    r = run_bass_kernel_spmd(nc, [arrays], core_ids=[0])
    return r.results[0]["out_0"]
```

```python
import numpy as np
import concourse.bass as bass
from concourse import mybir
from contextlib import ExitStack

F32 = mybir.dt.float32
BF16 = mybir.dt.bfloat16
ALU = mybir.AluOpType
ACT = mybir.ActivationFunctionType
AX = mybir.AxisListType
ADD, SUB, MUL = ALU.add, ALU.subtract, ALU.mult

P = 128
BATCH, TIME = 4, 1024
TAPS = 512
CHUNKS = TIME // P
WIDE = BATCH * P
HALF = WIDE // 2
GROUP = 512
TILES = GROUP // P
EXPERTS = 8
EPS = 1e-5
FFT = 1536
BLOCKS = 6
ORDER = [1, 5, 3, 2, 4, 0]
ROOT = float(np.sqrt(3.0) / 2)
HEADS = EXPERTS // 2
UNITS = 2 + 4 * TILES
SCALAR_PAIRS = (0, 1, 2)
SMALL_TABLES = 7
TAB_STEPS = 110


def vector_pair(pair):
    return 2 + 2 * HEADS * sum(1 if p in SCALAR_PAIRS else 2 for p in range(pair))


def vector_ops(pair, half, tile):
    return vector_pair(pair) + 2 * HEADS * (half + 1) - 2 + tile + 1


def scalar_ops(pair, tile):
    return 2 * HEADS * SCALAR_PAIRS.index(pair) + HEADS * (tile + 1)


VECTOR_OPS = vector_pair(TILES)
SCALAR_OPS = 2 * HEADS * len(SCALAR_PAIRS)


def forward_matrices():
    m = np.zeros((BLOCKS, 4, P, P))
    n2, k2 = np.arange(P)[:, None], np.arange(P)[None, :]
    q_scale = {1: -1, 2: -ROOT, 3: -1, 4: -ROOT, 5: -1}
    for k1 in range(1, 6):
        angle = -2 * np.pi * (k1 + 12 * k2) * n2 / FFT
        c, s, q = np.cos(angle), np.sin(angle), q_scale[k1]
        m[k1] = c, -q * s, s, q * c
    j = np.arange(64)[None, :]
    at0, at6 = -2 * np.pi * 12 * j * n2 / FFT, -2 * np.pi * (6 + 12 * j) * n2 / FFT
    m[0, 0, :, :64], m[0, 2, :, :64] = np.cos(at0), np.sin(at0)
    m[0, 1, :, 64:], m[0, 3, :, 64:] = np.cos(at6), np.sin(at6)
    m[0, 2, :, 0] = np.cos(np.pi * n2[:, 0])
    return m.astype(np.float32)


def inverse_matrices():
    m = np.zeros((BLOCKS, 4, P, P))
    n2, k2 = np.arange(P)[None, :], np.arange(P)[:, None]
    s_scale = {1: 1, 2: ROOT, 3: 1, 4: ROOT, 5: 1}
    for k1 in range(1, 6):
        angle = 2 * np.pi * (k1 + 12 * k2) * n2 / FFT
        c, s, q = np.cos(angle) * 2 / FFT, np.sin(angle) * 2 / FFT, s_scale[k1]
        m[k1] = c, -s, -s * q, -c * q
    j = np.arange(64)[:, None]
    at0, at6 = 2 * np.pi * 12 * j * n2 / FFT, 2 * np.pi * (6 + 12 * j) * n2 / FFT
    m[0, 0, :64], m[0, 1, :64] = np.cos(at0) * 2 / FFT, -np.sin(at0) * 2 / FFT
    m[0, 0, 0] /= 2
    m[0, 1, 0] = np.cos(np.pi * n2[0]) / FFT
    m[0, 2, 64:], m[0, 3, 64:] = np.cos(at6) * 2 / FFT, -np.sin(at6) * 2 / FFT
    return m.astype(np.float32)


def constants():
    bin0 = np.zeros((P, 2), np.float32)
    bin0[0, 0] = 1.0
    bin0[1:, 1] = 1.0
    return {
        "fwd": np.ascontiguousarray(forward_matrices().transpose(2, 0, 1, 3)),
        "inv": np.ascontiguousarray(inverse_matrices().transpose(2, 0, 1, 3)),
        "ident": np.eye(P, dtype=np.float32),
        "bin0": bin0,
        "rank": np.tile(np.arange(EXPERTS, 0, -1, dtype=np.float32), (P, 2 * TILES, 1)),
    }


def build(nc, d, out):
    ctx = ExitStack()
    with ctx:
        def sb(name, shape, dt=F32):
            return ctx.enter_context(nc.sbuf_tensor(name, shape, dt))

        def sem(name):
            return ctx.enter_context(nc.semaphore(name))

        xy = sb("xy", [P, CHUNKS, WIDE])
        y_all = xy[:].rearrange("p n (b c) -> p n b c", b=BATCH)
        conv = sb("conv", [P, 48, HALF])
        u = [[conv[:, 2 * k + i, :] for i in range(2)] for k in range(BLOCKS)]
        z = u
        work = [conv[:, 12 + n, :] for n in range(16)]
        spec = [[conv[:, 28 + 2 * k + i, :] for i in range(2)] for k in range(BLOCKS)]
        prod = [[conv[:, 40 + 4 * r + i, :] for i in range(4)] for r in range(2)]
        late = [conv[:, 4 * n:4 * n + 4, :].rearrange("p a c -> p (a c)") for n in range(3)]
        fwd = sb("fwd", [P, BLOCKS, 4, P])
        inv = sb("inv", [P, BLOCKS, 4, P])
        filt = sb("filt", [P, 20, P])
        t_in = filt[:, 0:TAPS // P]
        t_u = filt[:, 4:16].rearrange("p (k i) c -> p k i c", k=BLOCKS)
        t_w = filt[:, 16:20]
        tok3 = filt[:, 0:8].rearrange("p (g t) c -> p g t c", g=2)
        x3T = filt[:, 8:16].rearrange("p (g t) c -> p g (t c)", g=2)
        t_spec = sb("t_spec", [P, BLOCKS, 2, P])
        t_spec0 = sb("t_spec0", [P, 2, P])
        bin0 = sb("bin0", [P, 2])
        ident = sb("ident", [P, P])
        rank = sb("rank", [P, 2 * TILES, EXPERTS])
        w_sin = [sb(f"w_sin{l}", [P, 2 * P]) for l in range(2)]
        w_rin = [sb(f"w_rin{l}", [P, 2 * P]) for l in range(2)]
        w_sout = [sb(f"w_sout{l}", [P, P]) for l in range(2)]
        w_exp = [sb(f"w_exp{l}", [P, EXPERTS, P]) for l in range(2)]
        w_gate = [sb(f"w_gate{l}", [P, EXPERTS]) for l in range(2)]
        bias = [sb(f"bias{l}", [P, EXPERTS]) for l in range(2)]
        tok1 = sb("tok1", [P, 2, TILES, P])
        x1T = sb("x1T", [P, 2, GROUP])
        tok2 = sb("tok2", [P, 2, TILES, P])
        tok4 = late[0].rearrange("p (g t c) -> p g t c", g=2, t=TILES)
        x2T = sb("x2T", [P, 2, GROUP])
        y = sb("y", [P, 2, TILES, P])
        part = sb("part", [P, 2, HEADS, 2, P])
        zT, sil = sb("zT", [P, 2, GROUP]), sb("sil", [P, 2, GROUP])
        h_shared = [sb("h_shared0", [P, 2, GROUP])[:], late[1].rearrange("p (g c) -> p g c", g=2)]
        h_routed = [sb("h_routed0", [P, 2, GROUP])[:], late[2].rearrange("p (g c) -> p g c", g=2)]
        drive = [sb(f"drive{i}", [P, TIME]) for i in range(2)]
        state = [sb(f"state{i}", [P, TIME]) for i in range(2)]
        NT = 2 * TILES
        logit, expo, prob, key, rest = (sb(n, [P, NT, EXPERTS]) for n in ("logit", "expo", "prob", "key", "rest"))
        pick = [sb(f"pick{i}", [P, NT, EXPERTS]) for i in range(2)]
        peak, total, rtotal, top, peak2 = (sb(n, [P, NT]) for n in ("peak", "total", "rtotal", "top", "peak2"))
        gate_w = [sb(f"gate_w{l}", [P, NT, EXPERTS]) for l in range(2)]
        NB = [sb(f"bn{i}", [P, TILES, 6]) for i in range(2)]
        SM = [sb(f"sm{i}", [P, TILES, 2]) for i in range(2)]
        VE, NM, RS, SH, DM, QM, VR = ([sb(f"{n}{i}", [P, TILES]) for i in range(2)]
                                      for n in ("ve", "nm", "rs", "shift", "dm", "qm", "vr"))
        eps = sb("eps", [P, TILES])
        half_neg, half_pos = sb("half_neg", [P, TILES]), sb("half_pos", [P, TILES])
        euler = sb("euler", [P, NT * EXPERTS])
        phazor, phazor_init, last = sb("phazor", [P, 2]), sb("phazor_init", [P, 2]), sb("last", [P, 2])
        col = sb("col", [P, 16])
        powers = sb("powers", [P, 10, 4])
        cosT, sinT, in_re, in_im = (sb(n, [P, TIME]) for n in ("cosT", "sinT", "in_re", "in_im"))

        table_tmp = state[0][:]

        ps = [ctx.enter_context(nc.psum_tensor(f"ps{i}", [P, GROUP], F32)) for i in range(8)]
        half_ps = [ps[2], ps[3], ps[4]]
        x_ps = [[b[:, 0:HALF], b[:, HALF:2 * HALF]] for b in half_ps]
        t_ps = [ps[6], ps[7]]
        to_tok, to_ch, route_ps = ps[0], ps[1], ps[0]
        o_ps = [ps[2], ps[3], ps[4], ps[5]]
        gate_ps, up_ps = ps[6], ps[7]

        x_loaded = [[sem(f"x_loaded{h}_{n}") for n in range(CHUNKS)] for h in range(2)]
        t_loaded, param_loaded = sem("t_loaded"), sem("param_loaded")
        fwd_loaded = [sem(f"fwd_loaded{i}") for i in range(3)]
        inv_loaded, const_loaded = sem("inv_loaded"), sem("const_loaded")
        weights_loaded = [sem(f"weights_loaded{l}") for l in range(2)]
        set_up = sem("set_up")
        dve_t, dve_fwd = sem("dve_t"), sem("dve_fwd")
        t_block, x_block, t_kept = sem("t_block"), sem("x_block"), sem("t_kept")
        dve_t0 = sem("dve_t0")
        products, spectra, z_block, z_kept = sem("products"), sem("spectra"), sem("z_block"), sem("z_kept")
        dve_inv, pool_inv = sem("dve_inv"), sem("pool_inv")
        pool_col, pool_tab = sem("pool_col"), sem("pool_tab")
        dve_ln = [sem(f"dve_ln{i}") for i in range(2)]
        pool_ln = [sem(f"pool_ln{i}") for i in range(2)]
        normed = [sem(f"normed{i}") for i in range(2)]
        tok_ready, ch_ready, ch_copied = sem("tok_ready"), sem("ch_ready"), sem("ch_copied")
        logits_done, dve_gate, exp_done = (sem(n) for n in ("logits_done", "dve_gate", "exp_done"))
        gate_done, up_done, silu_done, h_done = (sem(n) for n in ("gate_done", "up_done", "silu_done", "h_done"))
        o_ready, combined, weighed, part_added, y_done = (
            sem(n) for n in ("o_ready", "combined", "weighed", "part_added", "y_done"))
        driven, scanned, turned, added = sem("driven"), sem("scanned"), sem("turned"), sem("added")
        summed = sem("summed")
        tok4_free = [sem(f"tok4_free{g}") for g in range(2)]

        x_dram = d["L0_attn_x"].rearrange("b (n p) c -> p n b c", p=P)
        out_dram = out.rearrange("b (g n p) c -> p b g n c", p=P, g=2)

        T_DVE = ["delta", "re3", "V3", "A", "re1", "re5", "C", "V1", "V5", "Em", "Ep", "Fm", "Fp", "re2", "re4",
                 "k0", "k6"]
        FWD = ["d06", "E", "d24", "D", "s15", "d15", "A", "B", "H", "F", "re1", "re5", "C", "G", "V1", "V5",
               "re3", "V3", "Em", "Ep", "Fm", "Fp", "V2", "V4", "re2", "re4", "k0", "k6"]
        INV_DVE = ["a", "rm", "cc", "sm", "t2", "r", "g", "v", "gv", "s", "um", "m", "o", "q", "t1", "y3",
                   "f", "w", "y2", "y4", "qr", "qm", "y1", "y5", "y7"]
        INV_POOL = ["aR", "p", "u", "e", "ep", "y0", "y6"]

        U_READY = {1: "V1", 5: "V5", 3: "V3", 2: "re2", 4: "re4", 0: "k6"}

        def after(steps, name):
            return steps.index(name) + 1

        GATE_STEPS = 19
        LN_STEPS = 9

        def s_next(i):
            return i * 2 + 1

        def s_mid(i):
            return i * 2

        def ch_use(i):
            if isinstance(i, int) and i == BATCH - 1:
                return {2: i * 6 + 2, 3: i * 6 + 4}
            return {1: i * 6 + 2, 2: i * 6 + 4, 3: i * 6 + 6}

        def norm_use(i):
            if isinstance(i, int) and i == 0:
                return {2: 0, 3: 2}
            return {2: i * 6 - 2, 3: i * 6, 4: i * 6 + 2}

        def expert_out(odd, half, tile, e):
            return o_ps[(2 + 2 * half + tile + 2 * odd) % 4][:, e % HEADS * P:(e % HEADS + 1) * P]

        block = ctx.enter_context(nc.Block())

        @block.sync
        def _(sp):
            sp.dma_start(t_in, d["L0_attn_t"].rearrange("(n p) c -> p n c", p=P)).then_inc(t_loaded, 16)
            for half in range(2):
                b = 2 * half
                for n in (0, 6, 2, 4, 1, 5, 3, 7):
                    sp.dma_start(y_all[:, n, b:b + 2], x_dram[:, n, b:b + 2]).then_inc(x_loaded[half][n], 16)
                if half == 0:
                    sp.dma_start(inv[:], d["inv"]).then_inc(inv_loaded, 16)
                l, w = half, f"L{half}_ffn_"
                sp.dma_start(w_sin[l][:], d[w + "w_shared_in"]).then_inc(weights_loaded[l], 16)
                sp.dma_start(w_rin[l][:], d[w + "w1_shared"]).then_inc(weights_loaded[l], 16)
                sp.dma_start(w_sout[l][:], d[w + "w_shared_out"]).then_inc(weights_loaded[l], 16)
                sp.dma_start(w_exp[l][:], d[w + "w2"].rearrange("e h c -> h e c")).then_inc(weights_loaded[l], 16)
                sp.dma_start(w_gate[l][:], d[w + "w_gate"]).then_inc(weights_loaded[l], 16)
                sp.dma_start(bias[l][:], d[w + "gate_bias"].partition_broadcast(P)).then_inc(weights_loaded[l], 16)

            for g in range(2):
                sp.sem_inc(tok4_free[g], 16)

            def store(b, n):
                for g in range(2):
                    sp.wait_ge(normed[1], n + g + 1)
                    sp.dma_start(out_dram[:, b, g], tok4[:, g]).then_inc(tok4_free[g], 16)

            with sp.Fori(1, BATCH) as i:
                store(i - 1, norm_use(i)[4])
            store(BATCH - 1, norm_use(BATCH - 1)[4] + 2)
            for g in range(2):
                sp.wait_ge(tok4_free[g], 16 * (BATCH + 1))

        @block.tensor
        def _(pe):
            mm = nc.tensor.matmul

            def filter_block(i):
                k = ORDER[i]
                if i >= 2:
                    pe.wait_ge(t_kept, i - 1)
                for o in range(2):
                    for q in range(2):
                        last = mm(t_ps[i % 2][:, o * P:(o + 1) * P], fwd[:, k, 2 * o + q, :], t_u[:, k, q, :],
                                  start=(q == 0), stop=(q == 1))
                last.then_inc(t_block, 1)

            def forward_block(half, i):
                k = ORDER[i]
                pe.wait_ge(dve_fwd, half * len(FWD) + after(FWD, U_READY[k]))
                if half == 1 and i == 0:
                    pe.wait_ge(combined, VECTOR_OPS)
                    pe.wait_ge(weighed, SCALAR_OPS)
                if i >= 3:
                    pe.wait_ge(products, 24 * half + 4 * (i - 2))
                for o in range(2):
                    for q in range(2):
                        last = mm(x_ps[i % 3][o], fwd[:, k, 2 * o + q, :], u[k][q], start=(q == 0), stop=(q == 1))
                last.then_inc(x_block, 1)

            def inverse_block(half, i):
                k = ORDER[i]
                pe.wait_ge(spectra, 12 * half + 2 * (i + 1))
                if i < 3:
                    pe.wait_ge(products, 24 * half + 4 * (i + 4))
                else:
                    pe.wait_ge(z_kept, 12 * half + 2 * (i - 2))
                for o in range(2):
                    for q in range(2):
                        last = mm(x_ps[i % 3][o], inv[:, k, 2 * o + q, :], spec[k][q], start=(q == 0), stop=(q == 1))
                last.then_inc(z_block, 1)

            def to_channels(tok, g, stage, norms, use, first=False):
                pe.wait_ge(normed[stage], norms + 1)
                if not first:
                    pe.wait_ge(ch_copied, use)
                for t in range(TILES):
                    last = nc.tensor.transpose(to_ch[:, t * P:(t + 1) * P], tok[:, g, t, :], ident[:])
                last.then_inc(ch_ready, 1)

            def to_tokens(zT, g, n, ready, count, read, value):
                pe.wait_ge(ready, count)
                pe.wait_ge(read, value)
                for t in range(TILES):
                    last = nc.tensor.transpose(to_tok[:, t * P:(t + 1) * P], zT[:, g, t * P:(t + 1) * P], ident[:])
                last.then_inc(tok_ready, 1)

            def logits(s, l, xT, use, norms=None):
                pe.wait_ge(ch_copied, use)
                if norms is not None:
                    pe.wait_ge(normed[1], norms)
                for t in range(2 * TILES):
                    last = mm(route_ps[:, t * EXPERTS:(t + 1) * EXPERTS],
                              xT[:, t // TILES, (t % TILES) * P:(t % TILES + 1) * P], w_gate[l][:],
                              start=True, stop=True)
                last.then_inc(logits_done, 1)

            def hidden(s, l, xT, unit, use, first=False):
                g, kind = unit // 2, unit % 2
                w = (w_sin[l], w_rin[l])[kind]
                pe.wait_ge(ch_copied, use)
                if not (first and unit == 0):
                    pe.wait_ge(h_done, s * 4 + unit)
                mm(gate_ps[:], w[:, 0:P], xT[:, g, :], start=True, stop=True).then_inc(gate_done, 1)
                mm(up_ps[:], w[:, P:2 * P], xT[:, g, :], start=True, stop=True).then_inc(up_done, 1)

            def experts(s, l, odd, hooks, first=False):
                pe.wait_ge(h_done, s * 4 + 4)
                unit = 0

                def bank(unit):
                    if unit >= 4:
                        u, n = unit - 4, s
                    elif not first:
                        u, n = unit + UNITS - 4, s - 1
                    else:
                        return o_ps[unit]
                    if u < 2:
                        pe.wait_ge(combined, n * VECTOR_OPS + u + 1)
                    else:
                        pair, half, tile = (u - 2) // 4, (u - 2) // 2 % 2, u % 2
                        if half == 1 and pair in SCALAR_PAIRS:
                            pe.wait_ge(weighed, n * SCALAR_OPS + scalar_ops(pair, tile))
                        else:
                            pe.wait_ge(combined, n * VECTOR_OPS + vector_ops(pair, half, tile))
                    return o_ps[(unit + 2 * odd) % 4]

                for g in range(2):
                    o = bank(unit)
                    for t in range(TILES):
                        last = mm(o[:, t * P:(t + 1) * P], h_shared[l][:, g, t * P:(t + 1) * P], w_sout[l][:],
                                  start=True, stop=True)
                    last.then_inc(o_ready, 1)
                    unit += 1
                for pair in range(TILES):
                    if pair in hooks:
                        hooks[pair]()
                    for half in range(2):
                        w = w_exp[l][:, half * HEADS:(half + 1) * HEADS, :].rearrange("p e c -> p (e c)")
                        for tile in range(2):
                            g, t = pair // 2, 2 * (pair % 2) + tile
                            mm(bank(unit)[:], h_routed[l][:, g, t * P:(t + 1) * P], w,
                               start=True, stop=True).then_inc(o_ready, 1)
                            unit += 1

            def body(i, s0, s1, mid=True, more=True):
                ch, nu = ch_use(i), norm_use(i)
                hooks = {}
                if more:
                    hooks[2] = lambda: to_channels(tok1, 0, 0, (i + 1) * 2, ch[1])
                    hooks[3] = lambda: to_channels(tok1, 1, 0, (i + 1) * 2 + 1, ch[1] + 1)
                experts(s0, 0, mid, hooks, first=not mid)
                if more:
                    hidden(s_next(i), 0, x1T, 0, ch[1] + 1)
                to_channels(tok2, 0, 1, nu[2], ch[2])
                if more:
                    hidden(s_next(i), 0, x1T, 1, ch[1] + 1)
                    logits(s_next(i), 0, x1T, ch[1] + 2, norms=nu[2] if mid else None)
                    hidden(s_next(i), 0, x1T, 2, ch[1] + 2)
                    hidden(s_next(i), 0, x1T, 3, ch[1] + 2)
                to_channels(tok2, 1, 1, nu[2] + 1, ch[2] + 1)

                def tokens3(g):
                    if g == 0:
                        to_tokens(zT, 0, nu[3], added, i * 2 + 1, dve_gate,
                                  (s_next(i) if more else s_mid(i)) * GATE_STEPS + 1)
                    else:
                        to_tokens(zT, 1, nu[3] + 1, added, i * 2 + 2, normed[1], nu[3] + 1)

                def channels3(g):
                    to_channels(tok3, g, 1, nu[3] + g, ch[3] + g)

                if mid:
                    experts(s_mid(i), 1, False, {1: lambda: tokens3(0), 2: lambda: channels3(0),
                                                 3: lambda: tokens3(1)})
                else:
                    for n in range(BLOCKS):
                        forward_block(1, n)
                    tokens3(0)
                    for n in range(3):
                        inverse_block(1, n)
                    channels3(0)
                    tokens3(1)
                    for n in range(3, BLOCKS):
                        inverse_block(1, n)
                hidden(s1, 1, x3T, 0, ch[3] + 1)
                hidden(s1, 1, x3T, 1, ch[3] + 1)
                channels3(1)
                logits(s1, 1, x3T, ch[3] + 2, norms=nu[3] + 2)
                hidden(s1, 1, x3T, 2, ch[3] + 2)
                hidden(s1, 1, x3T, 3, ch[3] + 2)

            pe.wait_ge(dve_t, len(T_DVE))
            for n in range(BLOCKS):
                pe.wait_ge(fwd_loaded[n // 2], 16)
                filter_block(n)
                forward_block(0, n)
            pe.wait_ge(inv_loaded, 16)
            for n in range(BLOCKS):
                inverse_block(0, n)
            pe.wait_ge(const_loaded, 16 * 3)
            to_channels(tok1, 0, 0, 0, 0, first=True)
            to_channels(tok1, 1, 0, 1, 1)
            pe.wait_ge(weights_loaded[0], 16 * 6)
            logits(0, 0, x1T, 2)
            for unit in range(4):
                hidden(0, 0, x1T, unit, 2, first=True)
            pe.wait_ge(weights_loaded[1], 16 * 6)
            body(0, 0, 2, mid=False)
            with pe.Fori(1, BATCH - 1) as i:
                body(i, i * 2 - 1, i * 2 + 2)
            body(BATCH - 1, 2 * BATCH - 3, 2 * BATCH - 1, more=False)
            experts(2 * BATCH - 1, 1, True, {})

        @block.scalar
        def _(act):
            act.dma_start(phazor[:], d["L1_attn_phazor"]).then_inc(param_loaded, 16)
            act.dma_start(phazor_init[:], d["L1_attn_phazor_init"]).then_inc(param_loaded, 16)
            act.dma_start(last[:, 0:1], d["L1_attn_last_conv_re"].rearrange("(p o) -> p o", o=1)).then_inc(param_loaded, 16)
            act.dma_start(last[:, 1:2], d["L1_attn_last_conv_im"].rearrange("(p o) -> p o", o=1)).then_inc(param_loaded, 16)
            act.dma_start(fwd[:, 1:6:4], d["fwd"][:, 1:6:4]).then_inc(fwd_loaded[0], 16)
            act.dma_start(fwd[:, 2:4], d["fwd"][:, 2:4]).then_inc(fwd_loaded[1], 16)
            act.dma_start(fwd[:, 0:5:4], d["fwd"][:, 0:5:4]).then_inc(fwd_loaded[2], 16)
            act.dma_start(bin0[:], d["bin0"]).then_inc(const_loaded, 16)
            act.dma_start(ident[:], d["ident"]).then_inc(const_loaded, 16)
            act.dma_start(rank[:], d["rank"]).then_inc(const_loaded, 16)

            for i, k in enumerate(ORDER[:-1]):
                act.wait_ge(t_block, i + 1)
                nc.scalar.activation(t_spec[:, k], t_ps[i % 2][:, 0:2 * P].rearrange("p (a c) -> p a c", a=2),
                                     ACT.Copy).then_inc(t_kept, 1)
            def keep_inverse(half, i):
                act.wait_ge(z_block, 6 * half + i + 1)
                for o in range(2):
                    nc.scalar.activation(z[ORDER[i]][o], x_ps[i % 3][o], ACT.Copy).then_inc(z_kept, 1)

            def normalise(stage, n, source, tok, g):
                act.wait_ge(pool_ln[stage], (n + 1) * 3)
                for t in range(TILES):
                    last = nc.scalar.activation(tok[:, g, t, :], source(t), ACT.Identity,
                                                bias=SH[stage][:, t:t + 1], scale=RS[stage][:, t:t + 1])
                last.then_inc(normed[stage], 1)

            def norm1(b, g):
                normalise(0, b * 2 + g, lambda t: y_all[:, 4 * g + t, b, :], tok1, g)

            def norm_out(n, tok, g):
                normalise(1, n, lambda t: y[:, g, t, :], tok, g)

            def norm3(n, g):
                normalise(1, n, lambda t: to_tok[:, t * P:(t + 1) * P], tok3, g)

            def copy_channels(xT, g, use):
                act.wait_ge(ch_ready, use + 1)
                nc.scalar.activation(xT[:, g, :], to_ch[:], ACT.Copy).then_inc(ch_copied, 1)

            def silu(s, unit, first=False):
                act.wait_ge(gate_done, s * 4 + unit + 1)
                if not (first and unit < 2):
                    act.wait_ge(h_done, s * 4 + unit - 1)
                nc.scalar.activation(sil[:, unit % 2, :], gate_ps[:], ACT.Silu).then_inc(silu_done, 1)

            def exponentials(s):
                act.wait_ge(dve_gate, s * GATE_STEPS + 3)
                nc.scalar.activation(expo[:], logit[:], ACT.Exp).then_inc(exp_done, 1)

            def weigh(s, l, odd, pair, first=False):
                turn = SCALAR_PAIRS.index(pair)
                act.wait_ge(dve_gate, (s + 1) * GATE_STEPS)
                if not (first and turn < 2):
                    act.wait_ge(y_done, s * len(SCALAR_PAIRS) + turn - 1)
                for tile in range(2):
                    act.wait_ge(o_ready, s * UNITS + 2 + 4 * pair + 2 + tile + 1)
                    for e in range(HEADS, EXPERTS):
                        nc.scalar.activation(part[:, (turn + odd) % 2, e - HEADS, tile, :],
                                             expert_out(odd, 1, tile, e), ACT.Copy,
                                             scale=gate_w[l][:, 2 * pair + tile, e:e + 1]).then_inc(weighed, 1)

            def body(i, s0, s1, mid=True, more=True):
                ch, nu = ch_use(i), norm_use(i)
                weigh(s0, 0, mid, 0, first=not mid)
                if more:
                    norm1(i + 1, 0)
                weigh(s0, 0, mid, 1, first=not mid)
                if more:
                    norm1(i + 1, 1)
                weigh(s0, 0, mid, 2)
                if more:
                    copy_channels(x1T, 0, ch[1])
                if more:
                    copy_channels(x1T, 1, ch[1] + 1)
                norm_out(nu[2], tok2, 0)
                if more:
                    silu(s_next(i), 0)
                copy_channels(x2T, 0, ch[2])
                if more:
                    silu(s_next(i), 1)
                norm_out(nu[2] + 1, tok2, 1)
                if more:
                    silu(s_next(i), 2)
                    silu(s_next(i), 3)
                copy_channels(x2T, 1, ch[2] + 1)
                if more:
                    exponentials(s_next(i))
                if mid:
                    weigh(s_mid(i), 1, False, 0)
                    weigh(s_mid(i), 1, False, 1)
                    norm3(nu[3], 0)
                    weigh(s_mid(i), 1, False, 2)
                    copy_channels(x3T, 0, ch[3])
                    norm3(nu[3] + 1, 1)
                else:
                    for n in range(3):
                        keep_inverse(1, n)
                    norm3(nu[3], 0)
                    copy_channels(x3T, 0, ch[3])
                    for n in range(3, BLOCKS):
                        keep_inverse(1, n)
                    norm3(nu[3] + 1, 1)
                silu(s1, 0)
                silu(s1, 1)
                copy_channels(x3T, 1, ch[3] + 1)
                if mid:
                    act.wait_ge(tok4_free[0], i * 16)
                    norm_out(nu[4], tok4, 0)
                silu(s1, 2)
                silu(s1, 3)
                exponentials(s1)
                if mid:
                    act.wait_ge(tok4_free[1], i * 16)
                    norm_out(nu[4] + 1, tok4, 1)

            for n in range(BLOCKS):
                keep_inverse(0, n)
            norm1(0, 0)
            norm1(0, 1)
            copy_channels(x1T, 0, 0)
            copy_channels(x1T, 1, 1)
            silu(0, 0, first=True)
            silu(0, 1, first=True)
            exponentials(0)
            silu(0, 2)
            silu(0, 3)
            body(0, 0, 2, mid=False)
            with act.Fori(1, BATCH - 1) as i:
                body(i, i * 2 - 1, i * 2 + 2)
            body(BATCH - 1, 2 * BATCH - 3, 2 * BATCH - 1, more=False)
            s, n = 2 * BATCH - 1, norm_use(BATCH - 1)[4] + 2
            for pair in SCALAR_PAIRS:
                weigh(s, 1, True, pair)
            for g in range(2):
                act.wait_ge(tok4_free[g], 16 * BATCH)
                norm_out(n + g, tok4, g)

        @block.gpsimd
        def _(pool):
            tt, ts_ = nc.gpsimd.tensor_tensor, nc.gpsimd.tensor_scalar
            nc.gpsimd.memset(half_neg[:], -0.5).then_inc(set_up, 1)
            nc.gpsimd.memset(eps[:], EPS).then_inc(set_up, 1)
            nc.gpsimd.memset(half_pos[:], 0.5).then_inc(set_up, 1)
            nc.gpsimd.memset(euler[:], float(np.e)).then_inc(set_up, 1)
            pool.wait_ge(param_loaded, 16 * 4)
            pool.wait_ge(set_up, 4)

            def step(ins, n):
                ins.then_inc(pool_col, 1)
                pool.wait_ge(pool_col, n)

            step(tt(col[:, 0:2], phazor[:], phazor[:], MUL), 1)
            step(tt(col[:, 2:3], col[:, 0:1], col[:, 1:2], ADD), 2)
            step(tt(col[:, 3:4], col[:, 2:3], half_pos[:, 0:1], ALU.pow), 3)
            step(tt(col[:, 4:5], col[:, 2:3], half_neg[:, 0:1], ALU.pow), 4)
            step(ts_(powers[:, 0, 0:2], phazor[:], col[:, 4:5], None, MUL), 5)
            step(ts_(col[:, 5:6], col[:, 3:4], -1.0, None, MUL), 6)
            step(tt(col[:, 6:7], euler[:, 0:1], col[:, 5:6], ALU.pow), 7)

            def tick(ins):
                tab.append(ins)
                ins.then_inc(pool_tab, 1)

            tab = []
            tmp = table_tmp
            zr, zi = powers[:, :, 0], powers[:, :, 1]
            tick(nc.gpsimd.memset(cosT[:, 0:1], 1.0))
            tick(nc.gpsimd.memset(sinT[:, 0:1], 0.0))
            for j in range(9):
                pool.wait_ge(pool_tab, len(tab))
                r, i_ = zr[:, j:j + 1], zi[:, j:j + 1]
                tick(tt(powers[:, j, 2:3], r, r, MUL))
                tick(tt(powers[:, j, 3:4], i_, i_, MUL))
                tick(ts_(powers[:, j + 1, 1:2], r, i_, 2.0, MUL, MUL))
                pool.wait_ge(pool_tab, len(tab))
                tick(tt(zr[:, j + 1:j + 2], powers[:, j, 2:3], powers[:, j, 3:4], SUB))
            def double_tables(j):
                n = 1 << j
                r, i_ = zr[:, j:j + 1], zi[:, j:j + 1]
                pool.wait_ge(pool_tab, len(tab))
                tick(ts_(cosT[:, n:2 * n], cosT[:, 0:n], r, None, MUL))
                tick(ts_(tmp[:, 0:n], sinT[:, 0:n], i_, None, MUL))
                tick(ts_(sinT[:, n:2 * n], cosT[:, 0:n], i_, None, MUL))
                tick(ts_(tmp[:, 512:512 + n], sinT[:, 0:n], r, None, MUL))
                pool.wait_ge(pool_tab, len(tab))
                tick(tt(cosT[:, n:2 * n], cosT[:, n:2 * n], tmp[:, 0:n], SUB))
                tick(tt(sinT[:, n:2 * n], sinT[:, n:2 * n], tmp[:, 512:512 + n], ADD))
            for j in range(SMALL_TABLES):
                double_tables(j)
            r, i_ = zr[:, 0:1], zi[:, 0:1]
            tick(tt(col[:, 8:9], last[:, 1:2], i_, MUL))
            tick(tt(col[:, 9:10], last[:, 1:2], r, MUL))
            tick(tt(col[:, 12:13], last[:, 0:1], r, MUL))
            tick(tt(col[:, 13:14], last[:, 0:1], i_, MUL))
            pool.wait_ge(pool_tab, len(tab))
            tick(tt(col[:, 10:11], col[:, 12:13], col[:, 8:9], SUB))
            tick(tt(col[:, 11:12], col[:, 13:14], col[:, 9:10], ADD))

            def input_factors():
                tmp = table_tmp
                pr, pi = phazor_init[:, 0:1], phazor_init[:, 1:2]
                pool.wait_ge(pool_tab, len(tab))
                tick(ts_(in_re[:], cosT[:], pr, None, MUL))
                tick(ts_(tmp, sinT[:], pi, None, MUL))
                tick(ts_(in_im[:], cosT[:], pi, None, MUL))
                pool.wait_ge(pool_tab, len(tab))
                tick(tt(in_re[:], in_re[:], tmp, ADD))
                pool.wait_ge(pool_tab, len(tab))
                tick(ts_(tmp, sinT[:], pr, None, MUL))
                pool.wait_ge(pool_tab, len(tab))
                tick(tt(in_im[:], in_im[:], tmp, SUB))
                assert len(tab) == TAB_STEPS, len(tab)

            def product_sums(half, i):
                k = ORDER[i]
                pool.wait_ge(products, 24 * half + 4 * (i + 1))
                tt(spec[k][0], prod[i % 2][0], prod[i % 2][1], SUB).then_inc(spectra, 1)
                tt(spec[k][1], prod[i % 2][2], prod[i % 2][3], ADD).then_inc(spectra, 1)

            def inverse_share(half):
                (R0, R6), (R1, S1), (R2, S2), (R3, S3), (R4, S4), (R5, S5) = z
                a, aR, p, uu, e, ep = work[0], work[10], work[4], work[6], work[8], work[11]
                y = [xy[:, n, half * HALF:(half + 1) * HALF] for n in range(CHUNKS)]
                done, kept = half * len(INV_POOL), 12 * half
                pool.wait_ge(dve_inv, half * len(INV_DVE) + after(INV_DVE, "a"))
                pool.wait_ge(z_kept, kept + 6)
                tt(aR, a, R3, ADD).then_inc(pool_inv, 1)
                pool.wait_ge(z_kept, kept + 10)
                tt(p, R2, R4, ADD).then_inc(pool_inv, 1)
                tt(uu, S2, S4, ADD).then_inc(pool_inv, 1)
                pool.wait_ge(z_kept, kept + 12)
                tt(e, R0, R6, ADD).then_inc(pool_inv, 1)
                pool.wait_ge(pool_inv, done + after(INV_POOL, "e"))
                tt(ep, e, p, ADD).then_inc(pool_inv, 1)
                pool.wait_ge(pool_inv, done + after(INV_POOL, "ep"))
                tt(y[0], ep, aR, ADD).then_inc(pool_inv, 1)
                tt(y[6], ep, aR, SUB).then_inc(pool_inv, 1)

            def scale_shift(stage, n, first=False):
                if not first:
                    pool.wait_ge(normed[stage], n)
                pool.wait_ge(dve_ln[stage], (n + 1) * LN_STEPS)
                tt(VE[stage][:], VR[stage][:], eps[:], ADD).then_inc(pool_ln[stage], 1)
                pool.wait_ge(pool_ln[stage], n * 3 + 1)
                tt(RS[stage][:], VE[stage][:], half_neg[:], ALU.pow).then_inc(pool_ln[stage], 1)
                pool.wait_ge(pool_ln[stage], n * 3 + 2)
                tt(SH[stage][:], NM[stage][:], RS[stage][:], MUL).then_inc(pool_ln[stage], 1)

            def add_parts(s, odd, pair):
                turn = SCALAR_PAIRS.index(pair)
                p, done = part[:, (turn + odd) % 2], (s * len(SCALAR_PAIRS) + turn) * 2
                pool.wait_ge(weighed, s * SCALAR_OPS + scalar_ops(pair, 1))
                tt(p[:, 0:2], p[:, 0:2], p[:, 2:4], ADD).then_inc(part_added, 1)
                pool.wait_ge(part_added, done + 1)
                tt(p[:, 0], p[:, 0], p[:, 1], ADD).then_inc(part_added, 1)
                pool.wait_ge(part_added, done + 2)
                pool.wait_ge(combined, s * VECTOR_OPS + vector_ops(pair, 0, 1))
                out_ = y[:, pair // 2, 2 * (pair % 2):2 * (pair % 2) + 2, :]
                tt(out_, out_, p[:, 0], ADD).then_inc(y_done, 1)

            def drive_state(i, g, use, first=False):
                lo, hi = g * GROUP, (g + 1) * GROUP
                pool.wait_ge(ch_copied, use)
                if first:
                    pool.wait_ge(pool_tab, TAB_STEPS)
                else:
                    pool.wait_ge(added, i * 2)
                tt(drive[0][:, lo:hi], x2T[:, g, :], in_re[:, lo:hi], MUL).then_inc(driven, 1)
                tt(drive[1][:, lo:hi], x2T[:, g, :], in_im[:, lo:hi], MUL).then_inc(driven, 1)

            def body(i, s0, s1, mid=True, more=True):
                ch, nu = ch_use(i), norm_use(i)
                if more:
                    scale_shift(0, i * 2 + 2)
                add_parts(s0, mid, 0)
                if more:
                    scale_shift(0, i * 2 + 3)
                add_parts(s0, mid, 1)
                add_parts(s0, mid, 2)
                scale_shift(1, nu[2], first=not mid)
                drive_state(i, 0, ch[2] + 1, first=not mid)
                scale_shift(1, nu[2] + 1)
                drive_state(i, 1, ch[2] + 2, first=not mid)
                if mid:
                    add_parts(s_mid(i), False, 0)
                    scale_shift(1, nu[3])
                    add_parts(s_mid(i), False, 1)
                    add_parts(s_mid(i), False, 2)
                    scale_shift(1, nu[3] + 1)
                    scale_shift(1, nu[4])
                    scale_shift(1, nu[4] + 1)
                else:
                    for n in range(BLOCKS):
                        product_sums(1, n)
                    scale_shift(1, nu[3])
                    inverse_share(1)
                    scale_shift(1, nu[3] + 1)

            for n in range(BLOCKS):
                product_sums(0, n)
            inverse_share(0)
            scale_shift(0, 0, first=True)
            scale_shift(0, 1)
            for j in range(SMALL_TABLES, 10):
                double_tables(j)
            input_factors()
            body(0, 0, 2, mid=False)
            with pool.Fori(1, BATCH - 1) as i:
                body(i, i * 2 - 1, i * 2 + 2)
            body(BATCH - 1, 2 * BATCH - 3, 2 * BATCH - 1, more=False)
            s, n = 2 * BATCH - 1, norm_use(BATCH - 1)[4] + 2
            add_parts(s, True, 0)
            add_parts(s, True, 1)
            add_parts(s, True, 2)
            scale_shift(1, n)
            scale_shift(1, n + 1)

        @block.vector
        def _(dve):
            tt, ts_, stt = nc.vector.tensor_tensor, nc.vector.tensor_scalar, nc.vector.scalar_tensor_tensor

            t = [t_in[:, n, :] for n in range(4)]
            A, C, Em, Ep = (t_w[:, i, :] for i in range(4))
            U = [[t_u[:, k, i, :] for i in range(2)] for k in range(BLOCKS)]
            dve.wait_ge(t_loaded, 16)
            ts_(t[0][0:1, :], t[0][0:1, :], 1.0, None, ADD).then_inc(dve_t, 1)
            dve.wait_ge(dve_t, after(T_DVE, "delta"))
            tt(U[3][0], t[0], t[2], SUB).then_inc(dve_t, 1)
            tt(U[3][1], t[1], t[3], SUB).then_inc(dve_t, 1)
            stt(A, t[2], 0.5, t[0], MUL, ADD).then_inc(dve_t, 1)
            dve.wait_ge(dve_t, after(T_DVE, "A"))
            stt(U[1][0], t[1], ROOT, A, MUL, ADD).then_inc(dve_t, 1)
            stt(U[5][0], t[1], -ROOT, A, MUL, ADD).then_inc(dve_t, 1)
            stt(C, t[1], 0.5, t[3], MUL, ADD).then_inc(dve_t, 1)
            dve.wait_ge(dve_t, after(T_DVE, "C"))
            stt(U[1][1], t[2], ROOT, C, MUL, ADD).then_inc(dve_t, 1)
            stt(U[5][1], t[2], -ROOT, C, MUL, ADD).then_inc(dve_t, 1)
            tt(Em, t[0], t[3], SUB).then_inc(dve_t, 1)
            tt(Ep, t[0], t[3], ADD).then_inc(dve_t, 1)
            tt(U[4][1], t[1], t[2], SUB).then_inc(dve_t, 1)
            tt(U[2][1], t[1], t[2], ADD).then_inc(dve_t, 1)
            dve.wait_ge(dve_t, after(T_DVE, "Fp"))
            stt(U[2][0], U[4][1], 0.5, Em, MUL, ADD).then_inc(dve_t, 1)
            stt(U[4][0], U[2][1], -0.5, Ep, MUL, ADD).then_inc(dve_t, 1)
            tt(U[0][0], Ep, U[2][1], ADD).then_inc(dve_t, 1)
            tt(U[0][1], Em, U[4][1], SUB).then_inc(dve_t, 1)

            def forward_transform(half, part):
                D, E, Em, Ep, Fm, Fp, d06, d24, s15, d15, A, B, F, G, H, C = work
                x = [xy[:, n, half * HALF:(half + 1) * HALF] for n in range(CHUNKS)]

                def have(*chunks):
                    for n in chunks:
                        dve.wait_ge(x_loaded[half][n], 16)

                def own(name):
                    dve.wait_ge(dve_fwd, half * len(FWD) + after(FWD, name))

                if part == 0:
                    have(0, 6)
                    tt(d06, x[0], x[6], SUB).then_inc(dve_fwd, 1)
                    tt(E, x[0], x[6], ADD).then_inc(dve_fwd, 1)
                    have(2, 4)
                    tt(d24, x[2], x[4], SUB).then_inc(dve_fwd, 1)
                    tt(D, x[2], x[4], ADD).then_inc(dve_fwd, 1)
                    have(1, 5)
                    tt(s15, x[1], x[5], ADD).then_inc(dve_fwd, 1)
                    tt(d15, x[1], x[5], SUB).then_inc(dve_fwd, 1)
                    own("d24")
                    stt(A, d24, 0.5, d06, MUL, ADD).then_inc(dve_fwd, 1)
                if part == 1:
                    have(3, 7)
                    own("d15")
                    tt(B, d15, x[7], SUB).then_inc(dve_fwd, 1)
                    tt(H, s15, x[7], SUB).then_inc(dve_fwd, 1)
                    tt(F, s15, x[7], ADD).then_inc(dve_fwd, 1)
                    own("B")
                    stt(u[1][0], B, ROOT, A, MUL, ADD).then_inc(dve_fwd, 1)
                    stt(u[5][0], B, -ROOT, A, MUL, ADD).then_inc(dve_fwd, 1)
                    own("H")
                    stt(C, H, 0.5, x[3], MUL, ADD).then_inc(dve_fwd, 1)
                    tt(G, d15, x[7], ADD).then_inc(dve_fwd, 1)
                if part == 2:
                    own("C")
                    stt(u[1][1], D, ROOT, C, MUL, ADD).then_inc(dve_fwd, 1)
                    stt(u[5][1], D, -ROOT, C, MUL, ADD).then_inc(dve_fwd, 1)
                    tt(u[3][0], d06, d24, SUB).then_inc(dve_fwd, 1)
                    tt(u[3][1], H, x[3], SUB).then_inc(dve_fwd, 1)
                    tt(Em, E, x[3], SUB).then_inc(dve_fwd, 1)
                    tt(Ep, E, x[3], ADD).then_inc(dve_fwd, 1)
                    tt(Fm, F, D, SUB).then_inc(dve_fwd, 1)
                if part == 3:
                    tt(Fp, F, D, ADD).then_inc(dve_fwd, 1)
                    own("G")
                    tt(u[2][1], G, d24, ADD).then_inc(dve_fwd, 1)
                    tt(u[4][1], G, d24, SUB).then_inc(dve_fwd, 1)
                    own("Fp")
                    stt(u[2][0], Fm, 0.5, Em, MUL, ADD).then_inc(dve_fwd, 1)
                    stt(u[4][0], Fp, -0.5, Ep, MUL, ADD).then_inc(dve_fwd, 1)
                    tt(u[0][0], Ep, Fp, ADD).then_inc(dve_fwd, 1)
                    tt(u[0][1], Em, Fm, SUB).then_inc(dve_fwd, 1)

            def keep_filter0():
                i = BLOCKS - 1
                dve.wait_ge(t_block, i + 1)
                dve.wait_ge(const_loaded, 16 * 3)
                tr, ti = t_ps[i % 2][:, 0:P], t_ps[i % 2][:, P:2 * P]
                nc.vector.tensor_copy(t_spec[:, 0, 0, :], tr).then_inc(dve_t0, 1)
                ts_(t_spec[:, 0, 1, :], ti, bin0[:, 1:2], None, MUL).then_inc(dve_t0, 1)
                ts_(t_spec0[:, 1, :], ti, bin0[:, 0:1], None, MUL).then_inc(dve_t0, 1)
                dve.wait_ge(dve_t0, 3)
                stt(t_spec0[:, 0, :], tr, bin0[:, 1:2], t_spec0[:, 1, :], MUL, ADD).then_inc(dve_t0, 1)
                dve.wait_ge(dve_t0, 4)

            def multiply_spectra(half, i):
                k = ORDER[i]

                def wide(ap):
                    return ap.unsqueeze(1).to_broadcast([P, 2, P])

                if half == 0 and k != 0:
                    dve.wait_ge(t_kept, i + 1)
                dve.wait_ge(x_block, 6 * half + i + 1)
                if half == 1 or i >= 2:
                    dve.wait_ge(spectra, 12 * half + 2 * (i - 1))
                xr, xi = (x_ps[i % 3][o].rearrange("p (b c) -> p b c", b=2) for o in range(2))
                tr, ti = wide(t_spec[:, k, 0, :]), wide(t_spec[:, k, 1, :])
                t4 = wide(t_spec0[:, 0, :]) if k == 0 else tr
                pr = [q.rearrange("p (b c) -> p b c", b=2) for q in prod[i % 2]]
                tt(pr[0], xr, tr, MUL).then_inc(products, 1)
                tt(pr[1], xi, ti, MUL).then_inc(products, 1)
                tt(pr[2], xr, ti, MUL).then_inc(products, 1)
                tt(pr[3], xi, t4, MUL).then_inc(products, 1)

            def inverse_transform(half):
                (R0, R6), (R1, S1), (R2, S2), (R3, S3), (R4, S4), (R5, S5) = z
                a, rm, cc, sm, p, m, uu, v, e, o, aR, ep, t1, t2, f, g_ = work
                w, gv, q, r, qr, s_, qm, um = prod[0] + prod[1]
                y = [xy[:, n, half * HALF:(half + 1) * HALF] for n in range(CHUNKS)]
                kept = 12 * half

                def own(name):
                    dve.wait_ge(dve_inv, half * len(INV_DVE) + after(INV_DVE, name))

                def pools(name):
                    dve.wait_ge(pool_inv, half * len(INV_POOL) + after(INV_POOL, name))

                dve.wait_ge(z_kept, kept + 4)
                tt(a, R1, R5, ADD).then_inc(dve_inv, 1)
                tt(rm, R1, R5, SUB).then_inc(dve_inv, 1)
                tt(cc, S1, S5, ADD).then_inc(dve_inv, 1)
                tt(sm, S1, S5, SUB).then_inc(dve_inv, 1)
                dve.wait_ge(z_kept, kept + 6)
                dve.wait_ge(spectra, 12 * half + 12)
                own("cc")
                tt(t2, cc, S3, SUB).then_inc(dve_inv, 1)
                stt(r, cc, 0.5, S3, MUL, ADD).then_inc(dve_inv, 1)
                stt(g_, a, 0.5, R3, MUL, SUB).then_inc(dve_inv, 1)
                dve.wait_ge(z_kept, kept + 10)
                tt(v, S2, S4, SUB).then_inc(dve_inv, 1)
                own("v")
                tt(gv, g_, v, ADD).then_inc(dve_inv, 1)
                pools("u")
                stt(s_, rm, ROOT, uu, MUL, ADD).then_inc(dve_inv, 1)
                stt(um, rm, -ROOT, uu, MUL, ADD).then_inc(dve_inv, 1)
                tt(m, R2, R4, SUB).then_inc(dve_inv, 1)
                dve.wait_ge(z_kept, kept + 12)
                tt(o, R0, R6, SUB).then_inc(dve_inv, 1)
                own("o")
                stt(q, m, 0.5, o, MUL, ADD).then_inc(dve_inv, 1)
                tt(t1, o, m, SUB).then_inc(dve_inv, 1)
                own("t1")
                tt(y[3], t1, t2, ADD).then_inc(dve_inv, 1)
                pools("e")
                stt(f, p, -0.5, e, MUL, ADD).then_inc(dve_inv, 1)
                own("f")
                stt(w, sm, ROOT, f, MUL, ADD).then_inc(dve_inv, 1)
                own("w")
                tt(y[2], w, gv, ADD).then_inc(dve_inv, 1)
                tt(y[4], w, gv, SUB).then_inc(dve_inv, 1)
                tt(qr, q, r, ADD).then_inc(dve_inv, 1)
                tt(qm, q, r, SUB).then_inc(dve_inv, 1)
                own("qm")
                tt(y[1], qr, s_, ADD).then_inc(dve_inv, 1)
                tt(y[5], qr, s_, SUB).then_inc(dve_inv, 1)
                tt(y[7], qm, um, ADD).then_inc(dve_inv, 1)

            def moments(stage, n, source, first):
                for t_ in range(TILES):
                    nc.vector.bn_stats(NB[stage][:, t_, :], source(t_)).then_inc(dve_ln[stage], 1)
                done = n * LN_STEPS
                even, odd = NB[stage][:, :, 1:3], NB[stage][:, :, 4:6]
                dve.wait_ge(dve_ln[stage], done + 4)
                tt(SM[stage][:], even, odd, ADD).then_inc(dve_ln[stage], 1)
                tt(DM[stage][:], even[:, :, 0], odd[:, :, 0], SUB).then_inc(dve_ln[stage], 1)
                if not first:
                    dve.wait_ge(pool_ln[stage], n * 3)
                dve.wait_ge(dve_ln[stage], done + 5)
                ts_(NM[stage][:], SM[stage][:, :, 0], -0.5, None, MUL).then_inc(dve_ln[stage], 1)
                dve.wait_ge(dve_ln[stage], done + 6)
                stt(QM[stage][:], DM[stage][:], 0.25, DM[stage][:], MUL, MUL).then_inc(dve_ln[stage], 1)
                dve.wait_ge(dve_ln[stage], done + 8)
                stt(VR[stage][:], SM[stage][:, :, 1], 1.0 / P, QM[stage][:], MUL, ADD).then_inc(dve_ln[stage], 1)

            def moments1(b, g, first=False):
                moments(0, b * 2 + g, lambda t_: y_all[:, 4 * g + t_, b, :], first)

            def moments_out(n, s, g, first=False):
                dve.wait_ge(y_done, s * len(SCALAR_PAIRS) + sum(p // 2 <= g for p in SCALAR_PAIRS))
                if g == 1:
                    dve.wait_ge(combined, (s + 1) * VECTOR_OPS)
                moments(1, n, lambda t_: y[:, g, t_, :], first)

            def moments3(n, i, g):
                dve.wait_ge(tok_ready, i * 2 + g + 1)
                moments(1, n, lambda t_: to_tok[:, t_ * P:(t_ + 1) * P], False)

            def spread(ap):
                return ap.unsqueeze(2).to_broadcast([P, NT, EXPERTS])

            def route_shift(s, l):
                dve.wait_ge(logits_done, s + 1)
                tt(logit[:], route_ps[:, 0:NT * EXPERTS].rearrange("p (a e) -> p a e", a=NT),
                   bias[l][:].unsqueeze(1).to_broadcast([P, NT, EXPERTS]), ADD).then_inc(dve_gate, 1)
                dve.wait_ge(dve_gate, s * GATE_STEPS + 1)
                nc.vector.tensor_reduce(peak[:], logit[:], AX.X, ALU.max).then_inc(dve_gate, 1)
                dve.wait_ge(dve_gate, s * GATE_STEPS + 2)
                tt(logit[:], logit[:], spread(peak[:]), SUB).then_inc(dve_gate, 1)

            def route_softmax(s):
                dve.wait_ge(exp_done, s + 1)
                nc.vector.tensor_reduce(total[:], expo[:], AX.X, ADD).then_inc(dve_gate, 1)
                dve.wait_ge(dve_gate, s * GATE_STEPS + 4)
                nc.vector.reciprocal(rtotal[:], total[:]).then_inc(dve_gate, 1)
                dve.wait_ge(dve_gate, s * GATE_STEPS + 5)
                tt(prob[:], expo[:], spread(rtotal[:]), MUL).then_inc(dve_gate, 1)
                dve.wait_ge(dve_gate, s * GATE_STEPS + 6)
                nc.vector.tensor_reduce(peak2[:], prob[:], AX.X, ALU.max).then_inc(dve_gate, 1)

            def route_pick(s, i, values):
                done = s * GATE_STEPS + 7 + 6 * i
                dve.wait_ge(dve_gate, done)
                tt(key[:], values[:], spread(peak2[:]), ALU.is_equal).then_inc(dve_gate, 1)
                dve.wait_ge(dve_gate, done + 1)
                tt(key[:], key[:], rank[:], MUL).then_inc(dve_gate, 1)
                dve.wait_ge(dve_gate, done + 2)
                nc.vector.tensor_reduce(top[:], key[:], AX.X, ALU.max).then_inc(dve_gate, 1)
                dve.wait_ge(dve_gate, done + 3)
                tt(pick[i][:], key[:], spread(top[:]), ALU.is_equal).then_inc(dve_gate, 1)

            def route_rest(s):
                dve.wait_ge(dve_gate, s * GATE_STEPS + 11)
                stt(rest[:], pick[0][:], -2.0, prob[:], MUL, ADD).then_inc(dve_gate, 1)
                dve.wait_ge(dve_gate, s * GATE_STEPS + 12)
                nc.vector.tensor_reduce(peak2[:], rest[:], AX.X, ALU.max).then_inc(dve_gate, 1)

            def route_weights(s, l):
                dve.wait_ge(dve_gate, s * GATE_STEPS + 17)
                tt(key[:], pick[0][:], pick[1][:], ADD).then_inc(dve_gate, 1)
                dve.wait_ge(dve_gate, s * GATE_STEPS + 18)
                tt(gate_w[l][:], key[:], prob[:], MUL).then_inc(dve_gate, 1)

            def route(s, l, part):
                if part == 0:
                    route_softmax(s)
                elif part == 1:
                    route_pick(s, 0, prob)
                elif part == 2:
                    route_rest(s)
                elif part == 3:
                    route_pick(s, 1, rest)
                elif part == 4:
                    route_weights(s, l)

            def hidden(s, l, unit):
                g, kind = unit // 2, unit % 2
                dve.wait_ge(silu_done, s * 4 + unit + 1)
                dve.wait_ge(up_done, s * 4 + unit + 1)
                dst = (h_shared, h_routed)[kind][l]
                tt(dst[:, g, :], up_ps[:], sil[:, kind, :], MUL).then_inc(h_done, 1)

            def start_sum(s, odd, g, x, norms=None):
                dve.wait_ge(o_ready, s * UNITS + g + 1)
                if norms is not None:
                    dve.wait_ge(normed[1], norms)
                tt(y[:, g], o_ps[(g + 2 * odd) % 4][:].rearrange("p (t c) -> p t c", t=TILES), x[:, g],
                   ADD).then_inc(combined, 1)

            def combine(s, l, odd, pair):
                if pair == 0:
                    dve.wait_ge(dve_gate, (s + 1) * GATE_STEPS)
                done = vector_pair(pair)
                for half in range(1 if pair in SCALAR_PAIRS else 2):
                    for e in range(half * HEADS, (half + 1) * HEADS):
                        for tile in range(2):
                            if e % HEADS == 0:
                                dve.wait_ge(o_ready, s * UNITS + 2 + 4 * pair + 2 * half + tile + 1)
                            if e == 0:
                                dve.wait_ge(combined, s * VECTOR_OPS + 2)
                            else:
                                dve.wait_ge(combined, s * VECTOR_OPS + done - 1)
                            sum_ = y[:, pair // 2, 2 * (pair % 2) + tile, :]
                            stt(sum_, expert_out(odd, half, tile, e), gate_w[l][:, 2 * pair + tile, e:e + 1], sum_,
                                MUL, ADD).then_inc(combined, 1)
                            done += 1

            def scan_state(i, g):
                lo, hi = g * GROUP, (g + 1) * GROUP
                for part in range(2):
                    dve.wait_ge(driven, i * 4 + 2 * g + part + 1)
                    start = col[:, 10 + part:11 + part] if g == 0 else state[part][:, lo - 1:lo]
                    nc.vector.tensor_tensor_scan(state[part][:, lo:hi], col[:, 6:7].to_broadcast([P, GROUP]),
                                                 drive[part][:, lo:hi], start, MUL, ADD).then_inc(scanned, 1)

            def turn_state(i, g):
                lo, hi = g * GROUP, (g + 1) * GROUP
                dve.wait_ge(scanned, i * 4 + 2 * g + 2)
                tt(drive[0][:, lo:hi], state[0][:, lo:hi], cosT[:, lo:hi], MUL).then_inc(turned, 1)
                tt(drive[1][:, lo:hi], state[1][:, lo:hi], sinT[:, lo:hi], MUL).then_inc(turned, 1)

            def add_state(i, g):
                lo, hi = g * GROUP, (g + 1) * GROUP
                dve.wait_ge(turned, i * 4 + 2 * g + 2)
                tt(drive[0][:, lo:hi], drive[0][:, lo:hi], drive[1][:, lo:hi], SUB).then_inc(summed, 1)
                dve.wait_ge(summed, i * 2 + g + 1)
                tt(zT[:, g, :], drive[0][:, lo:hi], x2T[:, g, :], ADD).then_inc(added, 1)

            def body(i, s0, s1, mid=True, more=True):
                nu = norm_use(i)
                for g in range(2):
                    start_sum(s0, mid, g, tok1, norms=nu[2] - 1 + g if mid else None)
                if more:
                    moments1(i + 1, 0)
                combine(s0, 0, mid, 0)
                if more:
                    moments1(i + 1, 1)
                combine(s0, 0, mid, 1)
                if mid:
                    route(s_mid(i), 1, 0)
                    route(s_mid(i), 1, 1)
                else:
                    forward_transform(1, 0)
                combine(s0, 0, mid, 2)
                moments_out(nu[2], s0, 0, first=not mid)
                if mid:
                    route(s_mid(i), 1, 2)
                    route(s_mid(i), 1, 3)
                else:
                    forward_transform(1, 1)
                combine(s0, 0, mid, 3)
                if mid:
                    route(s_mid(i), 1, 4)
                else:
                    forward_transform(1, 2)
                if more:
                    hidden(s_next(i), 0, 0)
                moments_out(nu[2] + 1, s0, 1)
                if more:
                    hidden(s_next(i), 0, 1)
                scan_state(i, 0)
                if more:
                    hidden(s_next(i), 0, 2)
                turn_state(i, 0)
                if more:
                    hidden(s_next(i), 0, 3)
                    route_shift(s_next(i), 0)
                add_state(i, 0)
                if mid:
                    for g in range(2):
                        start_sum(s_mid(i), False, g, tok3, norms=nu[2] + g + 1)
                    combine(s_mid(i), 1, False, 0)
                    scan_state(i, 1)
                    if more:
                        route(s_next(i), 0, 0)
                    turn_state(i, 1)
                    moments3(nu[3], i, 0)
                    combine(s_mid(i), 1, False, 1)
                    add_state(i, 1)
                    if more:
                        route(s_next(i), 0, 1)
                    combine(s_mid(i), 1, False, 2)
                    if more:
                        route(s_next(i), 0, 2)
                        route(s_next(i), 0, 3)
                    combine(s_mid(i), 1, False, 3)
                    moments3(nu[3] + 1, i, 1)
                    if more:
                        route(s_next(i), 0, 4)
                    moments_out(nu[4], s_mid(i), 0)
                else:
                    forward_transform(1, 3)
                    multiply_spectra(1, 0)
                    scan_state(0, 1)
                    multiply_spectra(1, 1)
                    turn_state(0, 1)
                    multiply_spectra(1, 2)
                    add_state(0, 1)
                    multiply_spectra(1, 3)
                    route(s_next(0), 0, 0)
                    multiply_spectra(1, 4)
                    route(s_next(0), 0, 1)
                    multiply_spectra(1, 5)
                    moments3(nu[3], 0, 0)
                    for part in range(2, 5):
                        route(s_next(0), 0, part)
                    moments3(nu[3] + 1, 0, 1)
                    inverse_transform(1)
                hidden(s1, 1, 0)
                hidden(s1, 1, 1)
                if mid:
                    moments_out(nu[4] + 1, s_mid(i), 1)
                hidden(s1, 1, 2)
                hidden(s1, 1, 3)
                route_shift(s1, 1)

            for part in range(4):
                forward_transform(0, part)
            for n in range(BLOCKS):
                if n == BLOCKS - 1:
                    keep_filter0()
                multiply_spectra(0, n)
            inverse_transform(0)
            dve.wait_ge(pool_inv, len(INV_POOL))
            dve.wait_ge(dve_inv, len(INV_DVE))
            moments1(0, 0, first=True)
            moments1(0, 1)
            dve.wait_ge(weights_loaded[0], 16 * 6)
            route_shift(0, 0)
            hidden(0, 0, 0)
            hidden(0, 0, 1)
            hidden(0, 0, 2)
            hidden(0, 0, 3)
            for part in range(5):
                route(0, 0, part)
            dve.wait_ge(weights_loaded[1], 16 * 6)
            body(0, 0, 2, mid=False)
            with dve.Fori(1, BATCH - 1) as i:
                body(i, i * 2 - 1, i * 2 + 2)
            body(BATCH - 1, 2 * BATCH - 3, 2 * BATCH - 1, more=False)
            s, n = 2 * BATCH - 1, norm_use(BATCH - 1)[4] + 2
            for part in range(5):
                route(s, 1, part)
            for g in range(2):
                start_sum(s, True, g, tok3, norms=n - 1 + g)
            combine(s, 1, True, 0)
            combine(s, 1, True, 1)
            combine(s, 1, True, 2)
            moments_out(n, s, 0)
            combine(s, 1, True, 3)
            moments_out(n + 1, s, 1)


INPUTS = ["L0_attn_x", "L0_attn_t", "L0_ffn_w_shared_in", "L0_ffn_w_shared_out", "L0_ffn_w1_shared", "L0_ffn_w2",
          "L0_ffn_w_gate", "L0_ffn_gate_bias", "L1_attn_phazor", "L1_attn_phazor_init", "L1_attn_last_conv_re",
          "L1_attn_last_conv_im", "L1_ffn_w_shared_in", "L1_ffn_w_shared_out", "L1_ffn_w1_shared", "L1_ffn_w2",
          "L1_ffn_w_gate", "L1_ffn_gate_bias"]


def kernel(**inputs):
    import concourse.bacc as bacc
    from concourse.bass_utils import run_bass_kernel_spmd

    nc = bacc.Bacc("TRN2", target_bir_lowering=False, num_devices=1)
    arrays, aps = {}, {}
    for name, value in [(n, inputs[n]) for n in INPUTS] + list(constants().items()):
        a = np.ascontiguousarray(value)
        arrays[f"in_{name}"] = a
        aps[name] = nc.dram_tensor(f"in_{name}", a.shape, mybir.dt.from_np(a.dtype), kind="ExternalInput").ap()
    out = nc.dram_tensor("out_0", (BATCH, TIME, P), F32, kind="ExternalOutput").ap()
    build(nc, aps, out)
    r = run_bass_kernel_spmd(nc, [arrays], core_ids=[0])
    return r.results[0]["out_0"]
```

```python
import numpy as np
import concourse.bass as bass
from concourse import mybir
from contextlib import ExitStack

F32 = mybir.dt.float32
ALU = mybir.AluOpType
ACT = mybir.ActivationFunctionType
AX = mybir.AxisListType
ADD, SUB, MUL = ALU.add, ALU.subtract, ALU.mult

P = 128
BATCH, TIME = 4, 1024
TAPS = 512
CHUNKS = TIME // P
WIDE = BATCH * P
HALF = WIDE // 2
GROUP = 512
TILES = GROUP // P
EXPERTS = 8
EPS = 1e-5
FFT = 1536
BLOCKS = 6
ORDER = [1, 5, 3, 2, 4, 0]
ROOT = float(np.sqrt(3.0) / 2)
HEADS = EXPERTS // 2
UNITS = 2 + 4 * TILES
SCALAR_PAIRS = (0, 1, 2, 3)
DOUBLINGS = 10
SMALL_TABLES = 3
TAB_STEPS = 2 + 4 * (DOUBLINGS - 1) + 6 * SMALL_TABLES + 6
DVE_TAB_STEPS = 6 * (DOUBLINGS - SMALL_TABLES) + 5


def vector_pair(pair):
    return 2 + 2 * HEADS * sum(1 if p in SCALAR_PAIRS else 2 for p in range(pair))


def vector_ops(pair, half, tile):
    return vector_pair(pair) + 2 * HEADS * (half + 1) - 2 + tile + 1


def scalar_ops(pair, tile):
    return 2 * HEADS * SCALAR_PAIRS.index(pair) + HEADS * (tile + 1)


VECTOR_OPS = vector_pair(TILES)
SCALAR_OPS = 2 * HEADS * len(SCALAR_PAIRS)


def forward_matrices():
    m = np.zeros((BLOCKS, 4, P, P))
    n2, k2 = np.arange(P)[:, None], np.arange(P)[None, :]
    q_scale = {1: -1, 2: -ROOT, 3: -1, 4: -ROOT, 5: -1}
    for k1 in range(1, 6):
        angle = -2 * np.pi * (k1 + 12 * k2) * n2 / FFT
        c, s, q = np.cos(angle), np.sin(angle), q_scale[k1]
        m[k1] = c, -q * s, s, q * c
    j = np.arange(64)[None, :]
    at0, at6 = -2 * np.pi * 12 * j * n2 / FFT, -2 * np.pi * (6 + 12 * j) * n2 / FFT
    m[0, 0, :, :64], m[0, 2, :, :64] = np.cos(at0), np.sin(at0)
    m[0, 1, :, 64:], m[0, 3, :, 64:] = np.cos(at6), np.sin(at6)
    m[0, 2, :, 0] = np.cos(np.pi * n2[:, 0])
    return m.astype(np.float32)


def inverse_matrices():
    m = np.zeros((BLOCKS, 4, P, P))
    n2, k2 = np.arange(P)[None, :], np.arange(P)[:, None]
    s_scale = {1: 1, 2: ROOT, 3: 1, 4: ROOT, 5: 1}
    for k1 in range(1, 6):
        angle = 2 * np.pi * (k1 + 12 * k2) * n2 / FFT
        c, s, q = np.cos(angle) * 2 / FFT, np.sin(angle) * 2 / FFT, s_scale[k1]
        m[k1] = c, -s, -s * q, -c * q
    j = np.arange(64)[:, None]
    at0, at6 = 2 * np.pi * 12 * j * n2 / FFT, 2 * np.pi * (6 + 12 * j) * n2 / FFT
    m[0, 0, :64], m[0, 1, :64] = np.cos(at0) * 2 / FFT, -np.sin(at0) * 2 / FFT
    m[0, 0, 0] /= 2
    m[0, 1, 0] = np.cos(np.pi * n2[0]) / FFT
    m[0, 2, 64:], m[0, 3, 64:] = np.cos(at6) * 2 / FFT, -np.sin(at6) * 2 / FFT
    return m.astype(np.float32)


def constants():
    bin0 = np.zeros((P, 2), np.float32)
    bin0[0, 0] = 1.0
    bin0[1:, 1] = 1.0
    return {
        "fwd": np.ascontiguousarray(forward_matrices().transpose(2, 0, 1, 3)),
        "inv": np.ascontiguousarray(inverse_matrices().transpose(2, 0, 1, 3)),
        "ident": np.eye(P, dtype=np.float32),
        "bin0": bin0,
        "rank": np.tile(np.arange(EXPERTS, 0, -1, dtype=np.float32), (P, 2 * TILES, 1)),
    }


def build(nc, d, out):
    ctx = ExitStack()
    with ctx:
        def sb(name, shape, dt=F32):
            return ctx.enter_context(nc.sbuf_tensor(name, shape, dt))

        def sem(name):
            return ctx.enter_context(nc.semaphore(name))

        xy = sb("xy", [P, CHUNKS, WIDE])
        y_all = xy[:].rearrange("p n (b c) -> p n b c", b=BATCH)
        conv = sb("conv", [P, 48, HALF])
        u = [[conv[:, 2 * k + i, :] for i in range(2)] for k in range(BLOCKS)]
        z = u
        work = [conv[:, 12 + n, :] for n in range(16)]
        spec = [[conv[:, 28 + 2 * k + i, :] for i in range(2)] for k in range(BLOCKS)]
        prod = [[conv[:, 40 + 4 * r + i, :] for i in range(4)] for r in range(2)]
        late = [conv[:, 4 * n:4 * n + 4, :].rearrange("p a c -> p (a c)") for n in range(3)]
        fwd = sb("fwd", [P, BLOCKS, 4, P])
        inv = sb("inv", [P, BLOCKS, 4, P])
        filt = sb("filt", [P, 20, P])
        t_in = filt[:, 0:TAPS // P]
        t_u = filt[:, 4:16].rearrange("p (k i) c -> p k i c", k=BLOCKS)
        t_w = filt[:, 16:20]
        tok3 = filt[:, 0:8].rearrange("p (g t) c -> p g t c", g=2)
        x3T = filt[:, 8:16].rearrange("p (g t) c -> p g (t c)", g=2)
        t_spec = sb("t_spec", [P, BLOCKS, 2, P])
        t_spec0 = sb("t_spec0", [P, 2, P])
        bin0 = sb("bin0", [P, 2])
        ident = sb("ident", [P, P])
        rank = sb("rank", [P, 2 * TILES, EXPERTS])
        w_sin = [sb(f"w_sin{l}", [P, 2 * P]) for l in range(2)]
        w_rin = [sb(f"w_rin{l}", [P, 2 * P]) for l in range(2)]
        w_sout = [sb(f"w_sout{l}", [P, P]) for l in range(2)]
        w_exp = [sb(f"w_exp{l}", [P, EXPERTS, P]) for l in range(2)]
        w_gate = [sb(f"w_gate{l}", [P, EXPERTS]) for l in range(2)]
        bias = [sb(f"bias{l}", [P, EXPERTS]) for l in range(2)]
        tok1 = sb("tok1", [P, 2, TILES, P])
        x1T = sb("x1T", [P, 2, GROUP])
        tok2 = sb("tok2", [P, 2, TILES, P])
        tok4 = late[0].rearrange("p (g t c) -> p g t c", g=2, t=TILES)
        x2T = sb("x2T", [P, 2, GROUP])
        y = [sb(f"y{l}", [P, 2, TILES, P]) for l in range(2)]
        part = sb("part", [P, 2, HEADS, 2, P])
        zT, sil = sb("zT", [P, 2, GROUP]), sb("sil", [P, 2, GROUP])
        h_shared = [sb("h_shared0", [P, 2, GROUP])[:], late[1].rearrange("p (g c) -> p g c", g=2)]
        h_routed = [sb("h_routed0", [P, 2, GROUP])[:], late[2].rearrange("p (g c) -> p g c", g=2)]
        drive = [sb(f"drive{i}", [P, TIME]) for i in range(2)]
        state = [sb(f"state{i}", [P, TIME]) for i in range(2)]
        NT = 2 * TILES
        logit, expo, prob, key, rest = (sb(n, [P, NT, EXPERTS]) for n in ("logit", "expo", "prob", "key", "rest"))
        pick = [sb(f"pick{i}", [P, NT, EXPERTS]) for i in range(2)]
        peak, total, rtotal, top, peak2 = (sb(n, [P, NT]) for n in ("peak", "total", "rtotal", "top", "peak2"))
        gate_w = [sb(f"gate_w{l}", [P, NT, EXPERTS]) for l in range(2)]
        NB = [[sb(f"bn{i}_{g}", [P, TILES, 6]) for g in range(2)] for i in range(2)]
        SM = [[sb(f"sm{i}_{g}", [P, TILES, 2]) for g in range(2)] for i in range(2)]
        VE, NM, RS, SH, DM, QM, VR = ([[sb(f"{n}{i}_{g}", [P, TILES]) for g in range(2)] for i in range(2)]
                                      for n in ("ve", "nm", "rs", "shift", "dm", "qm", "vr"))
        stats1, sums1 = sb("stats1", [P, BATCH * NT, 6]), sb("sums1", [P, BATCH * NT, 2])
        nm1, dm1, qm1, vr1, ve1, rs1, sh1 = (sb(n, [P, BATCH, NT])
                                             for n in ("nm1", "dm1", "qm1", "vr1", "ve1", "rs1", "sh1"))
        eps = sb("eps", [P, NT])
        half_neg, half_pos = sb("half_neg", [P, NT]), sb("half_pos", [P, 1])
        euler = sb("euler", [P, NT * EXPERTS])
        phazor, phazor_init, last = sb("phazor", [P, 2]), sb("phazor_init", [P, 2]), sb("last", [P, 2])
        col = sb("col", [P, 16])
        powers = sb("powers", [P, DOUBLINGS, 4])
        cosT, sinT, in_re, in_im = (sb(n, [P, TIME]) for n in ("cosT", "sinT", "in_re", "in_im"))

        table_tmp = state[0][:]

        ps = [ctx.enter_context(nc.psum_tensor(f"ps{i}", [P, GROUP], F32)) for i in range(8)]
        half_ps = [ps[2], ps[3], ps[4]]
        x_ps = [[b[:, 0:HALF], b[:, HALF:2 * HALF]] for b in half_ps]
        t_ps = [ps[6], ps[7]]
        to_tok, to_ch, route_ps = ps[0], ps[1], ps[0]
        o_ps = [ps[2], ps[3], ps[4], ps[5]]

        def hidden_ps(unit, odd):
            if unit % 2 == 0:
                return ps[6], ps[7]
            first = (2 * odd + 2 * (unit == 1)) % 4
            return o_ps[first], o_ps[first + 1]

        x_loaded = [[sem(f"x_loaded{h}_{n}") for n in range(CHUNKS)] for h in range(2)]
        t_loaded, param_loaded = sem("t_loaded"), sem("param_loaded")
        fwd_loaded = [sem(f"fwd_loaded{i}") for i in range(3)]
        inv_loaded, const_loaded = sem("inv_loaded"), sem("const_loaded")
        weights_loaded = [sem(f"weights_loaded{l}") for l in range(2)]
        set_up = sem("set_up")
        dve_t, fwd_step = sem("dve_t"), [sem(f"fwd_step{h}") for h in range(2)]
        fwd_scaled = sem("fwd_scaled")
        t_block, x_block, t_kept = sem("t_block"), sem("x_block"), sem("t_kept")
        dve_t0 = sem("dve_t0")
        products, spectra, z_block, z_kept = sem("products"), sem("spectra"), sem("z_block"), sem("z_kept")
        dve_inv, pool_inv = sem("dve_inv"), sem("pool_inv")
        pool_col, pool_tab, dve_tab = sem("pool_col"), sem("pool_tab"), sem("dve_tab")
        dve_ln = [sem(f"dve_ln_set{i}") for i in range(2)]
        pool_ln = [sem(f"pool_ln_set{i}") for i in range(2)]
        normed = [sem(f"normed_set{i}") for i in range(2)]
        normed_last = sem("normed_last")
        dve_ln1, pool_ln1, normed1 = sem("dve_ln1"), sem("pool_ln1"), sem("normed1")
        tok_ready, ch_ready, ch_copied = sem("tok_ready"), sem("ch_ready"), sem("ch_copied")
        logits_done, dve_gate, exp_done = (sem(n) for n in ("logits_done", "dve_gate", "exp_done"))
        gate_done, up_done, silu_done, h_done = (sem(n) for n in ("gate_done", "up_done", "silu_done", "h_done"))
        o_ready, combined, weighed, part_added, y_done = (
            sem(n) for n in ("o_ready", "combined", "weighed", "part_added", "y_done"))
        driven, scanned, turned, added = sem("driven"), sem("scanned"), sem("turned"), sem("added")
        summed = sem("summed")
        tok4_free = [sem(f"tok4_free{g}") for g in range(2)]

        x_dram = d["L0_attn_x"].rearrange("b (n p) c -> p n b c", p=P)
        out_dram = out.rearrange("b (g n p) c -> p b g n c", p=P, g=2)

        T_DVE = ["delta", "re3", "V3", "A", "re1", "re5", "C", "V1", "V5", "Em", "Ep", "Fm", "Fp", "re2", "re4",
                 "k0", "k6"]
        FWD = ["d06", "E", "d24", "D", "s15", "d15", "A", "B", "H", "F", "re1", "re5", "C", "G", "V1", "V5",
               "re3", "V3", "Em", "Ep", "Fm", "Fp", "V2", "V4", "re2", "re4", "k0", "k6"]
        INV_DVE = ["a", "rm", "cc", "sm", "t2", "r", "g", "v", "u", "gv", "m", "s", "um", "o", "q", "t1", "y3",
                   "f", "w", "y2", "qr", "qm", "y1", "y5"]
        INV_POOL = ["aR", "p", "e", "ep", "y0", "y6", "y4", "y7"]

        U_READY = {1: "V1", 5: "V5", 3: "V3", 2: "re2", 4: "re4", 0: "k6"}

        def after(steps, name):
            return steps.index(name) + 1

        GATE_STEPS = 19
        LN_STEPS, LN1_STEPS = TILES + 5, NT + 5

        def s_next(i):
            return i * 2 + 1

        def s_mid(i):
            return i * 2

        def ch_use(i):
            if isinstance(i, int) and i == 0:
                return {1: (2, 3), 2: (4, 5), 3: (6, 7)}
            if isinstance(i, int) and i == BATCH - 1:
                return {2: (i * 6 + 2, i * 6 + 3), 3: (i * 6 + 4, i * 6 + 5)}
            return {1: (i * 6 + 3, i * 6 + 4), 2: (i * 6 + 2, i * 6 + 5), 3: (i * 6 + 6, i * 6 + 7)}

        AHEAD = 2

        def norm_number(norm, b, g):
            return {2: (0, b * 4 + g), 3: (0, b * 4 + 2 + g), 4: (1, b * 2 + g + AHEAD)}[norm]

        def early(n):
            return isinstance(n, int) and n < 2

        def double_tables(engine, queue, done, steps, j):
            n, tmp = 1 << j, table_tmp
            r, i_ = powers[:, j, 0:1], powers[:, j, 1:2]

            def tick(ins):
                steps.append(0)
                ins.then_inc(done, 1)

            if steps:
                queue.wait_ge(done, len(steps))
            tick(engine.tensor_scalar(cosT[:, n:2 * n], cosT[:, 0:n], r, None, MUL))
            tick(engine.tensor_scalar(tmp[:, 0:n], sinT[:, 0:n], i_, None, MUL))
            tick(engine.tensor_scalar(sinT[:, n:2 * n], cosT[:, 0:n], i_, None, MUL))
            tick(engine.tensor_scalar(tmp[:, 512:512 + n], sinT[:, 0:n], r, None, MUL))
            queue.wait_ge(done, len(steps))
            tick(engine.tensor_tensor(cosT[:, n:2 * n], cosT[:, n:2 * n], tmp[:, 0:n], SUB))
            tick(engine.tensor_tensor(sinT[:, n:2 * n], sinT[:, n:2 * n], tmp[:, 512:512 + n], ADD))

        def forward_transform(engine, queue, half, part):
            tt, scaled = engine.tensor_tensor, []

            def stt(out, a, factor, b, op0, op1):
                if engine is nc.vector:
                    return engine.scalar_tensor_tensor(out, a, factor, b, op0, op1)
                k = {0: 0, 1: 1, 2: 4}[part] + len(scaled)
                scaled.append(k)
                engine.tensor_scalar(prod[k // 4][k % 4], a, factor, None, op0).then_inc(fwd_scaled, 1)
                queue.wait_ge(fwd_scaled, k + 1)
                return tt(out, prod[k // 4][k % 4], b, op1)

            D, E, Em, Ep, Fm, Fp, d06, d24, s15, d15, A, B, F, G, H, C = work
            x = [xy[:, n, half * HALF:(half + 1) * HALF] for n in range(CHUNKS)]

            def have(*chunks):
                for n in chunks:
                    queue.wait_ge(x_loaded[half][n], 16)

            def own(name):
                queue.wait_ge(fwd_step[half], after(FWD, name))

            if part == 0:
                have(0, 6)
                tt(d06, x[0], x[6], SUB).then_inc(fwd_step[half], 1)
                tt(E, x[0], x[6], ADD).then_inc(fwd_step[half], 1)
                have(2, 4)
                tt(d24, x[2], x[4], SUB).then_inc(fwd_step[half], 1)
                tt(D, x[2], x[4], ADD).then_inc(fwd_step[half], 1)
                have(1, 5)
                tt(s15, x[1], x[5], ADD).then_inc(fwd_step[half], 1)
                tt(d15, x[1], x[5], SUB).then_inc(fwd_step[half], 1)
                own("d24")
                stt(A, d24, 0.5, d06, MUL, ADD).then_inc(fwd_step[half], 1)
            if part == 1:
                have(3, 7)
                own("d15")
                tt(B, d15, x[7], SUB).then_inc(fwd_step[half], 1)
                tt(H, s15, x[7], SUB).then_inc(fwd_step[half], 1)
                tt(F, s15, x[7], ADD).then_inc(fwd_step[half], 1)
                own("B")
                stt(u[1][0], B, ROOT, A, MUL, ADD).then_inc(fwd_step[half], 1)
                stt(u[5][0], B, -ROOT, A, MUL, ADD).then_inc(fwd_step[half], 1)
                own("H")
                stt(C, H, 0.5, x[3], MUL, ADD).then_inc(fwd_step[half], 1)
                tt(G, d15, x[7], ADD).then_inc(fwd_step[half], 1)
            if part == 2:
                own("C")
                stt(u[1][1], D, ROOT, C, MUL, ADD).then_inc(fwd_step[half], 1)
                stt(u[5][1], D, -ROOT, C, MUL, ADD).then_inc(fwd_step[half], 1)
                tt(u[3][0], d06, d24, SUB).then_inc(fwd_step[half], 1)
                tt(u[3][1], H, x[3], SUB).then_inc(fwd_step[half], 1)
                tt(Em, E, x[3], SUB).then_inc(fwd_step[half], 1)
                tt(Ep, E, x[3], ADD).then_inc(fwd_step[half], 1)
                tt(Fm, F, D, SUB).then_inc(fwd_step[half], 1)
            if part == 3:
                if half == 1:
                    own("Fm")
                tt(Fp, F, D, ADD).then_inc(fwd_step[half], 1)
                own("G")
                tt(u[2][1], G, d24, ADD).then_inc(fwd_step[half], 1)
                tt(u[4][1], G, d24, SUB).then_inc(fwd_step[half], 1)
                own("Fp")
                stt(u[2][0], Fm, 0.5, Em, MUL, ADD).then_inc(fwd_step[half], 1)
                stt(u[4][0], Fp, -0.5, Ep, MUL, ADD).then_inc(fwd_step[half], 1)
                tt(u[0][0], Ep, Fp, ADD).then_inc(fwd_step[half], 1)
                tt(u[0][1], Em, Fm, SUB).then_inc(fwd_step[half], 1)


        def expert_out(odd, half, tile, e):
            return o_ps[(2 + 2 * half + tile + 2 * odd) % 4][:, e % HEADS * P:(e % HEADS + 1) * P]

        block = ctx.enter_context(nc.Block())

        @block.sync
        def _(sp):
            sp.dma_start(t_in, d["L0_attn_t"].rearrange("(n p) c -> p n c", p=P)).then_inc(t_loaded, 16)
            for half in range(2):
                b = 2 * half
                for n in (0, 6, 2, 4, 1, 5, 3, 7):
                    sp.dma_start(y_all[:, n, b:b + 2], x_dram[:, n, b:b + 2]).then_inc(x_loaded[half][n], 16)
                if half == 0:
                    sp.dma_start(fwd[:, 2:4], d["fwd"][:, 2:4]).then_inc(fwd_loaded[1], 16)
                    sp.dma_start(fwd[:, 0:5:4], d["fwd"][:, 0:5:4]).then_inc(fwd_loaded[2], 16)
                    sp.dma_start(inv[:], d["inv"]).then_inc(inv_loaded, 16)
                l, w = half, f"L{half}_ffn_"
                sp.dma_start(w_sin[l][:], d[w + "w_shared_in"]).then_inc(weights_loaded[l], 16)
                sp.dma_start(w_rin[l][:], d[w + "w1_shared"]).then_inc(weights_loaded[l], 16)
                sp.dma_start(w_sout[l][:], d[w + "w_shared_out"]).then_inc(weights_loaded[l], 16)
                sp.dma_start(w_exp[l][:], d[w + "w2"].rearrange("e h c -> h e c")).then_inc(weights_loaded[l], 16)
                sp.dma_start(w_gate[l][:], d[w + "w_gate"]).then_inc(weights_loaded[l], 16)
                sp.dma_start(bias[l][:], d[w + "gate_bias"].partition_broadcast(P)).then_inc(weights_loaded[l], 16)

            for g in range(2):
                sp.sem_inc(tok4_free[g], 16)

            sp.sem_inc(dve_ln[1], AHEAD * LN_STEPS)
            sp.sem_inc(pool_ln[1], AHEAD * 3)
            sp.sem_inc(normed[1], AHEAD)

            def store(b):
                for g in range(2):
                    sp.wait_ge(normed[1], norm_number(4, b, g)[1] + 1)
                    if isinstance(b, int) and g == 1:
                        sp.wait_ge(normed_last, 1)
                    sp.dma_start(out_dram[:, b, g], tok4[:, g]).then_inc(tok4_free[g], 16)

            with sp.Fori(1, BATCH) as i:
                store(i - 1)
            store(BATCH - 1)
            for g in range(2):
                sp.wait_ge(tok4_free[g], 16 * (BATCH + 1))

        @block.tensor
        def _(pe):
            mm = nc.tensor.matmul

            def filter_block(i):
                k = ORDER[i]
                if i >= 2:
                    pe.wait_ge(t_kept, i - 1)
                for o in range(2):
                    for q in range(2):
                        last = mm(t_ps[i % 2][:, o * P:(o + 1) * P], fwd[:, k, 2 * o + q, :], t_u[:, k, q, :],
                                  start=(q == 0), stop=(q == 1))
                last.then_inc(t_block, 1)

            def forward_block(half, i):
                k = ORDER[i]
                pe.wait_ge(fwd_step[half], after(FWD, U_READY[k]))
                if half == 1 and i == 0:
                    pe.wait_ge(combined, VECTOR_OPS)
                    pe.wait_ge(weighed, SCALAR_OPS)
                if i >= 3:
                    pe.wait_ge(products, 24 * half + 4 * (i - 2))
                for o in range(2):
                    for q in range(2):
                        last = mm(x_ps[i % 3][o], fwd[:, k, 2 * o + q, :], u[k][q], start=(q == 0), stop=(q == 1))
                last.then_inc(x_block, 1)

            def inverse_block(half, i):
                k = ORDER[i]
                pe.wait_ge(spectra, 12 * half + 2 * (i + 1))
                if i == 0 and half == 1:
                    pe.wait_ge(h_done, 8)
                if i < 3:
                    pe.wait_ge(products, 24 * half + 4 * (i + 4))
                else:
                    pe.wait_ge(z_kept, 12 * half + 2 * (i - 2))
                for o in range(2):
                    for q in range(2):
                        last = mm(x_ps[i % 3][o], inv[:, k, 2 * o + q, :], spec[k][q], start=(q == 0), stop=(q == 1))
                last.then_inc(z_block, 1)

            def channels(norm, b, g):
                if norm == 1:
                    use = g if isinstance(b, int) and b == 0 else ch_use(b - 1)[1][g]
                else:
                    use = ch_use(b)[norm][g]
                if norm == 1:
                    pe.wait_ge(normed1, b * 2 + g + 1)
                else:
                    stage, n = norm_number(norm, b, g)
                    pe.wait_ge(normed[stage], n + 1)
                if not (isinstance(use, int) and use == 0):
                    pe.wait_ge(ch_copied, use)
                for t in range(TILES):
                    last = nc.tensor.transpose(to_ch[:, t * P:(t + 1) * P], (tok1, tok2, tok3)[norm - 1][:, g, t, :],
                                               ident[:])
                last.then_inc(ch_ready, 1)

            def to_tokens(zT, g, ready, count, read, value):
                pe.wait_ge(ready, count)
                pe.wait_ge(read, value)
                for t in range(TILES):
                    last = nc.tensor.transpose(to_tok[:, t * P:(t + 1) * P], zT[:, g, t * P:(t + 1) * P], ident[:])
                last.then_inc(tok_ready, 1)

            def logits(s, l, xT, use, read=None, value=None):
                pe.wait_ge(ch_copied, use)
                if read is not None:
                    pe.wait_ge(read, value)
                for t in range(2 * TILES):
                    last = mm(route_ps[:, t * EXPERTS:(t + 1) * EXPERTS],
                              xT[:, t // TILES, (t % TILES) * P:(t % TILES + 1) * P], w_gate[l][:],
                              start=True, stop=True)
                last.then_inc(logits_done, 1)

            def unit_read(n, u):
                pair, half, tile = (u - 2) // 4, (u - 2) // 2 % 2, u % 2
                if u < 2:
                    pe.wait_ge(combined, n * VECTOR_OPS + u + 1)
                elif half == 1 and pair in SCALAR_PAIRS:
                    pe.wait_ge(weighed, n * SCALAR_OPS + scalar_ops(pair, tile))
                else:
                    pe.wait_ge(combined, n * VECTOR_OPS + vector_ops(pair, half, tile))

            def hidden(s, l, xT, unit, use, last=None, odd=False):
                g, kind = unit // 2, unit % 2
                w = (w_sin[l], w_rin[l])[kind]
                gate_ps, up_ps = hidden_ps(unit, odd)
                pe.wait_ge(ch_copied, use)
                if unit == 2 or unit == 0 and not (isinstance(s, int) and s == 0):
                    pe.wait_ge(h_done, s * 4 + unit - 1)
                elif kind == 1 and isinstance(last, str) and last == "spectra":
                    pe.wait_ge(products, 48)
                    if unit == 3:
                        pe.wait_ge(h_done, s * 4 + 2)
                elif kind == 1 and isinstance(last, str):
                    pe.wait_ge(h_done, s * 4 + unit - 3)
                elif kind == 1 and last is not None:
                    unit_read(last, UNITS - 5 + unit)
                    unit_read(last, UNITS - 4 + unit)
                elif kind == 1:
                    pe.wait_ge(z_kept, 12 if isinstance(s, int) and s == 0 else 24)
                mm(gate_ps[:], w[:, 0:P], xT[:, g, :], start=True, stop=True).then_inc(gate_done, 1)
                mm(up_ps[:], w[:, P:2 * P], xT[:, g, :], start=True, stop=True).then_inc(up_done, 1)

            def experts(s, l, odd, hooks, after=None):
                pe.wait_ge(h_done, s * 4 + 4)
                unit = 0

                def bank(unit):
                    if unit >= 4:
                        unit_read(s, unit - 4)
                    elif after is not None:
                        pe.wait_ge(h_done, after * 4 + (2 if unit < 2 else 4))
                    else:
                        unit_read(s - 1, unit + UNITS - 4)
                    return o_ps[(unit + 2 * odd) % 4]

                for g in range(2):
                    o = bank(unit)
                    for t in range(TILES):
                        last = mm(o[:, t * P:(t + 1) * P], h_shared[l][:, g, t * P:(t + 1) * P], w_sout[l][:],
                                  start=True, stop=True)
                    last.then_inc(o_ready, 1)
                    unit += 1
                for pair in range(TILES):
                    if pair in hooks:
                        hooks[pair]()
                    for half in range(2):
                        w = w_exp[l][:, half * HEADS:(half + 1) * HEADS, :].rearrange("p e c -> p (e c)")
                        for tile in range(2):
                            g, t = pair // 2, 2 * (pair % 2) + tile
                            mm(bank(unit)[:], h_routed[l][:, g, t * P:(t + 1) * P], w,
                               start=True, stop=True).then_inc(o_ready, 1)
                            unit += 1

            def tokens3(i, g, s):
                if g == 0:
                    to_tokens(zT, 0, added, i * 2 + 1, dve_gate, s * GATE_STEPS + 1)
                else:
                    to_tokens(zT, 1, added, i * 2 + 2, normed[0], norm_number(3, i, 0)[1] + 1)

            def experts0(i):
                experts(s_next(i), 0, True, {0: lambda: channels(3, i, 0), 2: lambda: channels(3, i, 1)})
                logits(s_next(i) + 1, 1, x3T, ch_use(i)[3][1] + 1, normed[0], norm_number(3, i, 1)[1] + 1)

            def start():
                experts(0, 0, False, {2: lambda: channels(1, 1, 0), 3: lambda: channels(1, 1, 1)}, after=0)
                for n in range(BLOCKS):
                    forward_block(1, n)
                    if n in (1, 4):
                        channels(2, 0, n // 3)
                for unit in range(4):
                    hidden(1, 0, x1T, unit, ch_use(0)[1][1] + 1, last="spectra")
                logits(1, 0, x1T, ch_use(0)[1][1] + 1, dve_gate, 1)
                for n in range(BLOCKS):
                    inverse_block(1, n)
                    if n == 1:
                        tokens3(0, 0, 1)
                tokens3(0, 1, 1)
                pe.wait_ge(z_kept, 24)
                experts0(0)

            def body(i, more=True):
                ch = ch_use(i)
                for unit in range(4):
                    hidden(s_mid(i), 1, x3T, unit, i * 6 + 2, last=s_mid(i) - 1, odd=True)
                    if unit == 1:
                        channels(2, i, 0)
                if more:
                    channels(1, i + 1, 0)
                    for unit in range(4):
                        hidden(s_next(i), 0, x1T, unit, ch[1][unit // 2] + 1, last="hidden", odd=True)
                        if unit == 0:
                            channels(1, i + 1, 1)
                        if unit == 2:
                            channels(2, i, 1)
                    logits(s_next(i), 0, x1T, ch[1][1] + 1, dve_gate, s_mid(i) * GATE_STEPS + 1)
                s = s_next(i) if more else s_mid(i)
                hooks = {0: lambda: tokens3(i, 0, s), 2: lambda: tokens3(i, 1, s)}
                if not more:
                    def last_tokens():
                        tokens3(i, 1, s)
                        channels(3, i, 0)

                    hooks = {0: lambda: channels(2, i, 1), 1: hooks[0], 3: last_tokens}
                experts(s_mid(i), 1, False, hooks, after=s)
                if more:
                    experts0(i)

            pe.wait_ge(dve_t, len(T_DVE))
            for n in range(BLOCKS):
                pe.wait_ge(fwd_loaded[n // 2], 16)
                filter_block(n)
                forward_block(0, n)
            pe.wait_ge(inv_loaded, 16)
            for n in range(BLOCKS):
                inverse_block(0, n)
            pe.wait_ge(const_loaded, 16 * 3)
            channels(1, 0, 0)
            channels(1, 0, 1)
            pe.wait_ge(weights_loaded[0], 16 * 6)
            for unit in range(4):
                if unit == 2:
                    logits(0, 0, x1T, 2)
                hidden(0, 0, x1T, unit, 1 + unit // 2, odd=True)
            pe.wait_ge(weights_loaded[1], 16 * 6)
            start()
            with pe.Fori(1, BATCH - 1) as i:
                body(i)
            body(BATCH - 1, more=False)
            final, use = 2 * BATCH - 1, ch_use(BATCH - 1)[3][0]
            for unit in range(4):
                if unit == 2:
                    channels(3, BATCH - 1, 1)
                    logits(final, 1, x3T, use + 2, normed[0], norm_number(3, BATCH - 1, 1)[1] + 1)
                hidden(final, 1, x3T, unit, use + 1 + unit // 2, last=final - 1)
            experts(final, 1, True, {}, after=final)

        @block.scalar
        def _(act):
            act.dma_start(phazor[:], d["L1_attn_phazor"]).then_inc(param_loaded, 16)
            act.dma_start(phazor_init[:], d["L1_attn_phazor_init"]).then_inc(param_loaded, 16)
            act.dma_start(last[:, 0:1], d["L1_attn_last_conv_re"].rearrange("(p o) -> p o", o=1)).then_inc(param_loaded, 16)
            act.dma_start(last[:, 1:2], d["L1_attn_last_conv_im"].rearrange("(p o) -> p o", o=1)).then_inc(param_loaded, 16)
            act.dma_start(fwd[:, 1:6:4], d["fwd"][:, 1:6:4]).then_inc(fwd_loaded[0], 16)
            act.dma_start(bin0[:], d["bin0"]).then_inc(const_loaded, 16)
            act.dma_start(ident[:], d["ident"]).then_inc(const_loaded, 16)
            act.dma_start(rank[:], d["rank"]).then_inc(const_loaded, 16)

            for i, k in enumerate(ORDER[:-1]):
                act.wait_ge(t_block, i + 1)
                nc.scalar.activation(t_spec[:, k], t_ps[i % 2][:, 0:2 * P].rearrange("p (a c) -> p a c", a=2),
                                     ACT.Copy).then_inc(t_kept, 1)
            def keep_inverse(half, i):
                act.wait_ge(z_block, 6 * half + i + 1)
                for o in range(2):
                    nc.scalar.activation(z[ORDER[i]][o], x_ps[i % 3][o], ACT.Copy).then_inc(z_kept, 1)

            def normalise1(b, g):
                act.wait_ge(pool_ln1, (b + 1) * 3)
                for t in range(TILES):
                    chunk = g * TILES + t
                    last = nc.scalar.activation(tok1[:, g, t, :], y_all[:, chunk, b, :], ACT.Identity,
                                                bias=sh1[:, b, chunk:chunk + 1], scale=rs1[:, b, chunk:chunk + 1])
                last.then_inc(normed1, 1)

            def normalise(norm, b, g, tiles=TILES):
                stage, n = norm_number(norm, b, g)
                if norm == 4:
                    act.wait_ge(tok4_free[g], (b + 1) * 16)
                act.wait_ge(pool_ln[stage], (n + 1) * 3)
                for t in range(tiles):
                    source = {2: y[0][:, g, t, :], 3: to_tok[:, t * P:(t + 1) * P], 4: y[1][:, g, t, :]}[norm]
                    last = nc.scalar.activation((tok2, tok3, tok4)[norm - 2][:, g, t, :], source, ACT.Identity,
                                                bias=SH[stage][g][:, t:t + 1], scale=RS[stage][g][:, t:t + 1])
                last.then_inc(normed[stage], 1)

            def copy_channels(xT, g, use):
                act.wait_ge(ch_ready, use + 1)
                nc.scalar.activation(xT[:, g, :], to_ch[:], ACT.Copy).then_inc(ch_copied, 1)

            def silu(s, unit, odd=False, first=False):
                act.wait_ge(gate_done, s * 4 + unit + 1)
                if not (first and unit < 2):
                    act.wait_ge(h_done, s * 4 + unit - 1)
                nc.scalar.activation(sil[:, unit % 2, :], hidden_ps(unit, odd)[0][:], ACT.Silu).then_inc(silu_done, 1)

            def exponentials(s):
                act.wait_ge(dve_gate, s * GATE_STEPS + 3)
                nc.scalar.activation(expo[:], logit[:], ACT.Exp).then_inc(exp_done, 1)

            def weigh(s, l, odd, pair, first=False):
                turn = SCALAR_PAIRS.index(pair)
                act.wait_ge(dve_gate, (s + 1) * GATE_STEPS)
                if not (first and turn < 2):
                    act.wait_ge(y_done, s * len(SCALAR_PAIRS) + turn - 1)
                for tile in range(2):
                    act.wait_ge(o_ready, s * UNITS + 2 + 4 * pair + 2 + tile + 1)
                    for e in range(HEADS, EXPERTS):
                        nc.scalar.activation(part[:, (turn + odd * len(SCALAR_PAIRS)) % 2, e - HEADS, tile, :],
                                             expert_out(odd, 1, tile, e), ACT.Copy,
                                             scale=gate_w[l][:, 2 * pair + tile, e:e + 1]).then_inc(weighed, 1)

            def experts0(i, mid=True):
                s, ch = s_next(i), ch_use(i)
                weigh(s, 0, True, 0)
                copy_channels(x3T, 0, ch[3][0])
                weigh(s, 0, True, 1)
                if mid:
                    normalise(4, i - 1, 0)
                weigh(s, 0, True, 2)
                copy_channels(x3T, 1, ch[3][1])
                if mid:
                    normalise(4, i - 1, 1)
                weigh(s, 0, True, 3)
                normalise(2, i + 1, 0)

            def start():
                ch = ch_use(0)
                weigh(0, 0, False, 0, first=True)
                normalise1(1, 0)
                weigh(0, 0, False, 1, first=True)
                normalise1(1, 1)
                copy_channels(x1T, 0, ch[1][0])
                weigh(0, 0, False, 2)
                weigh(0, 0, False, 3)
                copy_channels(x1T, 1, ch[1][1])
                normalise(2, 0, 0)
                copy_channels(x2T, 0, ch[2][0])
                normalise(2, 0, 1)
                copy_channels(x2T, 1, ch[2][1])
                for unit in range(4):
                    silu(1, unit)
                exponentials(1)
                for n in range(BLOCKS):
                    keep_inverse(1, n)
                    if n == 3:
                        normalise(3, 0, 0)
                normalise(3, 0, 1)
                experts0(0, mid=False)

            def body(i, more=True):
                ch = ch_use(i)
                exponentials(s_mid(i))
                silu(s_mid(i), 0, odd=True)
                silu(s_mid(i), 1, odd=True)
                copy_channels(x2T, 0, ch[2][0])
                if more:
                    normalise1(i + 1, 0)
                silu(s_mid(i), 2, odd=True)
                silu(s_mid(i), 3, odd=True)
                if more:
                    copy_channels(x1T, 0, ch[1][0])
                    normalise1(i + 1, 1)
                    silu(s_next(i), 0, odd=True)
                    copy_channels(x1T, 1, ch[1][1])
                normalise(2, i, 1)
                if more:
                    silu(s_next(i), 1, odd=True)
                    silu(s_next(i), 2, odd=True)
                copy_channels(x2T, 1, ch[2][1])
                if more:
                    silu(s_next(i), 3, odd=True)
                    exponentials(s_next(i))
                weigh(s_mid(i), 1, False, 0)
                if more:
                    normalise(3, i, 0)
                weigh(s_mid(i), 1, False, 1)
                if not more:
                    normalise(3, i, 0)
                weigh(s_mid(i), 1, False, 2)
                if not more:
                    copy_channels(x3T, 0, ch[3][0])
                weigh(s_mid(i), 1, False, 3)
                normalise(3, i, 1)
                if more:
                    experts0(i)

            for n in range(BLOCKS):
                keep_inverse(0, n)
            normalise1(0, 0)
            normalise1(0, 1)
            copy_channels(x1T, 0, 0)
            copy_channels(x1T, 1, 1)
            silu(0, 0, odd=True, first=True)
            silu(0, 1, odd=True, first=True)
            exponentials(0)
            silu(0, 2, odd=True)
            silu(0, 3, odd=True)
            start()
            with act.Fori(1, BATCH - 1) as i:
                body(i)
            body(BATCH - 1, more=False)
            final, use = 2 * BATCH - 1, ch_use(BATCH - 1)[3][0]
            silu(final, 0)
            silu(final, 1)
            copy_channels(x3T, 1, use + 1)
            exponentials(final)
            silu(final, 2)
            silu(final, 3)
            for g in range(2):
                normalise(4, BATCH - 2, g)
            for pair in SCALAR_PAIRS:
                weigh(final, 1, True, pair)
            normalise(4, BATCH - 1, 0)
            normalise(4, BATCH - 1, 1, tiles=2)

        @block.gpsimd
        def _(pool):
            tt, ts_ = nc.gpsimd.tensor_tensor, nc.gpsimd.tensor_scalar
            nc.gpsimd.memset(half_neg[:], -0.5).then_inc(set_up, 1)
            nc.gpsimd.memset(eps[:], EPS).then_inc(set_up, 1)
            nc.gpsimd.memset(half_pos[:], 0.5).then_inc(set_up, 1)
            nc.gpsimd.memset(euler[:], float(np.e)).then_inc(set_up, 1)
            pool.wait_ge(param_loaded, 16 * 4)
            pool.wait_ge(set_up, 4)

            def step(ins, n):
                ins.then_inc(pool_col, 1)
                pool.wait_ge(pool_col, n)

            step(tt(col[:, 0:2], phazor[:], phazor[:], MUL), 1)
            step(tt(col[:, 2:3], col[:, 0:1], col[:, 1:2], ADD), 2)
            step(tt(col[:, 3:4], col[:, 2:3], half_pos[:, 0:1], ALU.pow), 3)
            step(tt(col[:, 4:5], col[:, 2:3], half_neg[:, 0:1], ALU.pow), 4)
            step(ts_(powers[:, 0, 0:2], phazor[:], col[:, 4:5], None, MUL), 5)
            step(ts_(col[:, 5:6], col[:, 3:4], -1.0, None, MUL), 6)
            step(tt(col[:, 6:7], euler[:, 0:1], col[:, 5:6], ALU.pow), 7)

            def tick(ins):
                tab.append(0)
                ins.then_inc(pool_tab, 1)

            tab = []
            zr, zi = powers[:, :, 0], powers[:, :, 1]
            tick(nc.gpsimd.memset(cosT[:, 0:1], 1.0))
            tick(nc.gpsimd.memset(sinT[:, 0:1], 0.0))
            for j in range(DOUBLINGS - 1):
                pool.wait_ge(pool_tab, len(tab))
                r, i_ = zr[:, j:j + 1], zi[:, j:j + 1]
                tick(tt(powers[:, j, 2:3], r, r, MUL))
                tick(tt(powers[:, j, 3:4], i_, i_, MUL))
                tick(ts_(powers[:, j + 1, 1:2], r, i_, 2.0, MUL, MUL))
                pool.wait_ge(pool_tab, len(tab))
                tick(tt(zr[:, j + 1:j + 2], powers[:, j, 2:3], powers[:, j, 3:4], SUB))
            for j in range(SMALL_TABLES):
                double_tables(nc.gpsimd, pool, pool_tab, tab, j)
            r, i_ = zr[:, 0:1], zi[:, 0:1]
            tick(tt(col[:, 8:9], last[:, 1:2], i_, MUL))
            tick(tt(col[:, 9:10], last[:, 1:2], r, MUL))
            tick(tt(col[:, 12:13], last[:, 0:1], r, MUL))
            tick(tt(col[:, 13:14], last[:, 0:1], i_, MUL))
            pool.wait_ge(pool_tab, len(tab))
            tick(tt(col[:, 10:11], col[:, 12:13], col[:, 8:9], SUB))
            tick(tt(col[:, 11:12], col[:, 13:14], col[:, 9:10], ADD))
            assert len(tab) == TAB_STEPS

            def product_sums(half, i):
                k = ORDER[i]
                pool.wait_ge(products, 24 * half + 4 * (i + 1))
                tt(spec[k][0], prod[i % 2][0], prod[i % 2][1], SUB).then_inc(spectra, 1)
                tt(spec[k][1], prod[i % 2][2], prod[i % 2][3], ADD).then_inc(spectra, 1)

            def inverse_share(half, part):
                (R0, R6), (R1, S1), (R2, S2), (R3, S3), (R4, S4), (R5, S5) = z
                a, aR, p, e, ep = work[0], work[10], work[4], work[8], work[11]
                w, gv, qm, um = prod[0][0], prod[0][1], prod[1][2], prod[1][3]
                y = [xy[:, n, half * HALF:(half + 1) * HALF] for n in range(CHUNKS)]
                done, kept = half * len(INV_POOL), 12 * half
                if part == 0:
                    pool.wait_ge(dve_inv, half * len(INV_DVE) + after(INV_DVE, "a"))
                    pool.wait_ge(z_kept, kept + 6)
                    tt(aR, a, R3, ADD).then_inc(pool_inv, 1)
                    pool.wait_ge(z_kept, kept + 10)
                    tt(p, R2, R4, ADD).then_inc(pool_inv, 1)
                if part == 1:
                    pool.wait_ge(z_kept, kept + 12)
                    tt(e, R0, R6, ADD).then_inc(pool_inv, 1)
                    pool.wait_ge(pool_inv, done + after(INV_POOL, "e"))
                    tt(ep, e, p, ADD).then_inc(pool_inv, 1)
                    pool.wait_ge(pool_inv, done + after(INV_POOL, "ep"))
                    tt(y[0], ep, aR, ADD).then_inc(pool_inv, 1)
                    tt(y[6], ep, aR, SUB).then_inc(pool_inv, 1)
                    pool.wait_ge(dve_inv, half * len(INV_DVE) + after(INV_DVE, "w"))
                    tt(y[4], w, gv, SUB).then_inc(pool_inv, 1)
                    pool.wait_ge(dve_inv, half * len(INV_DVE) + after(INV_DVE, "qm"))
                    tt(y[7], qm, um, ADD).then_inc(pool_inv, 1)

            def scale_shift1(b):
                pool.wait_ge(dve_ln1, (b + 1) * LN1_STEPS)
                tt(ve1[:, b], vr1[:, b], eps[:], ADD).then_inc(pool_ln1, 1)
                pool.wait_ge(pool_ln1, b * 3 + 1)
                tt(rs1[:, b], ve1[:, b], half_neg[:], ALU.pow).then_inc(pool_ln1, 1)
                pool.wait_ge(pool_ln1, b * 3 + 2)
                tt(sh1[:, b], nm1[:, b], rs1[:, b], MUL).then_inc(pool_ln1, 1)

            def scale_shift(norm, b, g):
                stage, n = norm_number(norm, b, g)
                if not early(n):
                    pool.wait_ge(normed[stage], n - 1)
                pool.wait_ge(dve_ln[stage], (n + 1) * LN_STEPS)
                tt(VE[stage][g][:], VR[stage][g][:], eps[:, 0:TILES], ADD).then_inc(pool_ln[stage], 1)
                pool.wait_ge(pool_ln[stage], n * 3 + 1)
                tt(RS[stage][g][:], VE[stage][g][:], half_neg[:, 0:TILES], ALU.pow).then_inc(pool_ln[stage], 1)
                pool.wait_ge(pool_ln[stage], n * 3 + 2)
                tt(SH[stage][g][:], NM[stage][g][:], RS[stage][g][:], MUL).then_inc(pool_ln[stage], 1)

            def add_parts(s, l, odd, pair):
                turn = SCALAR_PAIRS.index(pair)
                p, done = part[:, (turn + odd * len(SCALAR_PAIRS)) % 2], (s * len(SCALAR_PAIRS) + turn) * 2
                pool.wait_ge(weighed, s * SCALAR_OPS + scalar_ops(pair, 1))
                tt(p[:, 0:2], p[:, 0:2], p[:, 2:4], ADD).then_inc(part_added, 1)
                pool.wait_ge(part_added, done + 1)
                tt(p[:, 0], p[:, 0], p[:, 1], ADD).then_inc(part_added, 1)
                pool.wait_ge(part_added, done + 2)
                pool.wait_ge(combined, s * VECTOR_OPS + vector_ops(pair, 0, 1))
                out_ = y[l][:, pair // 2, 2 * (pair % 2):2 * (pair % 2) + 2, :]
                tt(out_, out_, p[:, 0], ADD).then_inc(y_done, 1)

            def drive_state(i, g, use, first=False):
                lo, hi = g * GROUP, (g + 1) * GROUP
                pool.wait_ge(ch_copied, use)
                if first:
                    pool.wait_ge(dve_tab, DVE_TAB_STEPS)
                else:
                    pool.wait_ge(added, i * 2)
                tt(drive[0][:, lo:hi], x2T[:, g, :], in_re[:, lo:hi], MUL).then_inc(driven, 1)
                tt(drive[1][:, lo:hi], x2T[:, g, :], in_im[:, lo:hi], MUL).then_inc(driven, 1)

            def turn_state(i, g):
                lo, hi = g * GROUP, (g + 1) * GROUP
                pool.wait_ge(scanned, i * 4 + 2 * g + 2)
                tt(drive[0][:, lo:hi], state[0][:, lo:hi], cosT[:, lo:hi], MUL).then_inc(turned, 1)
                tt(drive[1][:, lo:hi], state[1][:, lo:hi], sinT[:, lo:hi], MUL).then_inc(turned, 1)

            def experts0(i, mid=True):
                add_parts(s_next(i), 0, True, 0)
                if mid:
                    scale_shift(4, i - 1, 0)
                add_parts(s_next(i), 0, True, 1)
                if mid:
                    scale_shift(4, i - 1, 1)
                else:
                    scale_shift1(2)
                add_parts(s_next(i), 0, True, 2)
                scale_shift(2, i + 1, 0)
                add_parts(s_next(i), 0, True, 3)
                if not mid:
                    scale_shift1(3)

            def start():
                add_parts(0, 0, False, 0)
                add_parts(0, 0, False, 1)
                add_parts(0, 0, False, 2)
                scale_shift(2, 0, 0)
                add_parts(0, 0, False, 3)
                for n in range(BLOCKS):
                    product_sums(1, n)
                    if n == 1:
                        scale_shift(2, 0, 1)
                    if n == 3:
                        drive_state(0, 0, ch_use(0)[2][0] + 1, first=True)
                drive_state(0, 1, ch_use(0)[2][1] + 1, first=True)
                turn_state(0, 0)
                turn_state(0, 1)
                scale_shift(3, 0, 0)
                inverse_share(1, 0)
                scale_shift(3, 0, 1)
                inverse_share(1, 1)
                experts0(0, mid=False)

            def body(i, more=True):
                ch = ch_use(i)
                drive_state(i, 0, ch[2][0] + 1)
                scale_shift(2, i, 1)
                turn_state(i, 0)
                drive_state(i, 1, ch[2][1] + 1)
                if not more:
                    add_parts(s_mid(i), 1, False, 0)
                turn_state(i, 1)
                scale_shift(3, i, 0)
                if more:
                    add_parts(s_mid(i), 1, False, 0)
                add_parts(s_mid(i), 1, False, 1)
                add_parts(s_mid(i), 1, False, 2)
                scale_shift(3, i, 1)
                add_parts(s_mid(i), 1, False, 3)
                if more:
                    experts0(i)
                else:
                    scale_shift(4, i - 1, 0)
                    scale_shift(4, i - 1, 1)

            for n in range(BLOCKS):
                product_sums(0, n)
            for step in range(2):
                inverse_share(0, step)
            scale_shift1(0)
            scale_shift1(1)
            for quarter in range(3):
                forward_transform(nc.gpsimd, pool, 1, quarter)
            start()
            with pool.Fori(1, BATCH - 1) as i:
                body(i)
            body(BATCH - 1, more=False)
            final = 2 * BATCH - 1
            for pair in range(3):
                add_parts(final, 1, True, pair)
            for g in range(2):
                scale_shift(4, BATCH - 1, g)

        @block.vector
        def _(dve):
            tt, ts_, stt = nc.vector.tensor_tensor, nc.vector.tensor_scalar, nc.vector.scalar_tensor_tensor

            t = [t_in[:, n, :] for n in range(4)]
            A, C, Em, Ep = (t_w[:, i, :] for i in range(4))
            U = [[t_u[:, k, i, :] for i in range(2)] for k in range(BLOCKS)]
            dve.wait_ge(t_loaded, 16)
            ts_(t[0][0:1, :], t[0][0:1, :], 1.0, None, ADD).then_inc(dve_t, 1)
            dve.wait_ge(dve_t, after(T_DVE, "delta"))
            tt(U[3][0], t[0], t[2], SUB).then_inc(dve_t, 1)
            tt(U[3][1], t[1], t[3], SUB).then_inc(dve_t, 1)
            stt(A, t[2], 0.5, t[0], MUL, ADD).then_inc(dve_t, 1)
            dve.wait_ge(dve_t, after(T_DVE, "A"))
            stt(U[1][0], t[1], ROOT, A, MUL, ADD).then_inc(dve_t, 1)
            stt(U[5][0], t[1], -ROOT, A, MUL, ADD).then_inc(dve_t, 1)
            stt(C, t[1], 0.5, t[3], MUL, ADD).then_inc(dve_t, 1)
            dve.wait_ge(dve_t, after(T_DVE, "C"))
            stt(U[1][1], t[2], ROOT, C, MUL, ADD).then_inc(dve_t, 1)
            stt(U[5][1], t[2], -ROOT, C, MUL, ADD).then_inc(dve_t, 1)
            tt(Em, t[0], t[3], SUB).then_inc(dve_t, 1)
            tt(Ep, t[0], t[3], ADD).then_inc(dve_t, 1)
            tt(U[4][1], t[1], t[2], SUB).then_inc(dve_t, 1)
            tt(U[2][1], t[1], t[2], ADD).then_inc(dve_t, 1)
            dve.wait_ge(dve_t, after(T_DVE, "Fp"))
            stt(U[2][0], U[4][1], 0.5, Em, MUL, ADD).then_inc(dve_t, 1)
            stt(U[4][0], U[2][1], -0.5, Ep, MUL, ADD).then_inc(dve_t, 1)
            tt(U[0][0], Ep, U[2][1], ADD).then_inc(dve_t, 1)
            tt(U[0][1], Em, U[4][1], SUB).then_inc(dve_t, 1)

            def keep_filter0():
                i = BLOCKS - 1
                dve.wait_ge(t_block, i + 1)
                dve.wait_ge(const_loaded, 16 * 3)
                tr, ti = t_ps[i % 2][:, 0:P], t_ps[i % 2][:, P:2 * P]
                nc.vector.tensor_copy(t_spec[:, 0, 0, :], tr).then_inc(dve_t0, 1)
                ts_(t_spec[:, 0, 1, :], ti, bin0[:, 1:2], None, MUL).then_inc(dve_t0, 1)
                ts_(t_spec0[:, 1, :], ti, bin0[:, 0:1], None, MUL).then_inc(dve_t0, 1)
                dve.wait_ge(dve_t0, 3)
                stt(t_spec0[:, 0, :], tr, bin0[:, 1:2], t_spec0[:, 1, :], MUL, ADD).then_inc(dve_t0, 1)
                dve.wait_ge(dve_t0, 4)

            def multiply_spectra(half, i):
                k = ORDER[i]

                def wide(ap):
                    return ap.unsqueeze(1).to_broadcast([P, 2, P])

                if half == 0 and k != 0:
                    dve.wait_ge(t_kept, i + 1)
                dve.wait_ge(x_block, 6 * half + i + 1)
                if half == 1 or i >= 2:
                    dve.wait_ge(spectra, 12 * half + 2 * (i - 1))
                xr, xi = (x_ps[i % 3][o].rearrange("p (b c) -> p b c", b=2) for o in range(2))
                tr, ti = wide(t_spec[:, k, 0, :]), wide(t_spec[:, k, 1, :])
                t4 = wide(t_spec0[:, 0, :]) if k == 0 else tr
                pr = [q.rearrange("p (b c) -> p b c", b=2) for q in prod[i % 2]]
                tt(pr[0], xr, tr, MUL).then_inc(products, 1)
                tt(pr[1], xi, ti, MUL).then_inc(products, 1)
                tt(pr[2], xr, ti, MUL).then_inc(products, 1)
                tt(pr[3], xi, t4, MUL).then_inc(products, 1)

            def inverse_transform(half, part):
                (R0, R6), (R1, S1), (R2, S2), (R3, S3), (R4, S4), (R5, S5) = z
                a, rm, cc, sm, p, m, uu, v, e, o, aR, ep, t1, t2, f, g_ = work
                w, gv, q, r, qr, s_, qm, um = prod[0] + prod[1]
                y = [xy[:, n, half * HALF:(half + 1) * HALF] for n in range(CHUNKS)]
                kept = 12 * half

                def own(name):
                    dve.wait_ge(dve_inv, half * len(INV_DVE) + after(INV_DVE, name))

                def pools(name):
                    dve.wait_ge(pool_inv, half * len(INV_POOL) + after(INV_POOL, name))

                if part == 0:
                    dve.wait_ge(z_kept, kept + 4)
                    tt(a, R1, R5, ADD).then_inc(dve_inv, 1)
                    tt(rm, R1, R5, SUB).then_inc(dve_inv, 1)
                    tt(cc, S1, S5, ADD).then_inc(dve_inv, 1)
                    tt(sm, S1, S5, SUB).then_inc(dve_inv, 1)
                    dve.wait_ge(z_kept, kept + 6)
                    dve.wait_ge(spectra, 12 * half + 12)
                    own("cc")
                    tt(t2, cc, S3, SUB).then_inc(dve_inv, 1)
                    stt(r, cc, 0.5, S3, MUL, ADD).then_inc(dve_inv, 1)
                    stt(g_, a, 0.5, R3, MUL, SUB).then_inc(dve_inv, 1)
                    dve.wait_ge(z_kept, kept + 10)
                    tt(v, S2, S4, SUB).then_inc(dve_inv, 1)
                    tt(uu, S2, S4, ADD).then_inc(dve_inv, 1)
                    own("v")
                    tt(gv, g_, v, ADD).then_inc(dve_inv, 1)
                    tt(m, R2, R4, SUB).then_inc(dve_inv, 1)
                    own("u")
                    stt(s_, rm, ROOT, uu, MUL, ADD).then_inc(dve_inv, 1)
                    stt(um, rm, -ROOT, uu, MUL, ADD).then_inc(dve_inv, 1)
                if part == 1:
                    dve.wait_ge(z_kept, kept + 12)
                    tt(o, R0, R6, SUB).then_inc(dve_inv, 1)
                    own("o")
                    stt(q, m, 0.5, o, MUL, ADD).then_inc(dve_inv, 1)
                    tt(t1, o, m, SUB).then_inc(dve_inv, 1)
                    own("t1")
                    tt(y[3], t1, t2, ADD).then_inc(dve_inv, 1)
                    pools("e")
                    stt(f, p, -0.5, e, MUL, ADD).then_inc(dve_inv, 1)
                    own("f")
                    stt(w, sm, ROOT, f, MUL, ADD).then_inc(dve_inv, 1)
                    own("w")
                    tt(y[2], w, gv, ADD).then_inc(dve_inv, 1)
                    tt(qr, q, r, ADD).then_inc(dve_inv, 1)
                    tt(qm, q, r, SUB).then_inc(dve_inv, 1)
                    own("qr")
                    tt(y[1], qr, s_, ADD).then_inc(dve_inv, 1)
                    tt(y[5], qr, s_, SUB).then_inc(dve_inv, 1)

            def moments1(b):
                stats, sums = stats1[:, b * NT:(b + 1) * NT], sums1[:, b * NT:(b + 1) * NT]
                for n in range(NT):
                    nc.vector.bn_stats(stats[:, n, :], y_all[:, n, b, :]).then_inc(dve_ln1, 1)
                even, odd = stats[:, :, 1:3], stats[:, :, 4:6]
                done = b * LN1_STEPS + NT
                dve.wait_ge(dve_ln1, done)
                tt(sums, even, odd, ADD).then_inc(dve_ln1, 1)
                tt(dm1[:, b], even[:, :, 0], odd[:, :, 0], SUB).then_inc(dve_ln1, 1)
                dve.wait_ge(dve_ln1, done + 1)
                ts_(nm1[:, b], sums[:, :, 0], -0.5, None, MUL).then_inc(dve_ln1, 1)
                dve.wait_ge(dve_ln1, done + 2)
                stt(qm1[:, b], dm1[:, b], 0.25, dm1[:, b], MUL, MUL).then_inc(dve_ln1, 1)
                dve.wait_ge(dve_ln1, done + 4)
                stt(vr1[:, b], sums[:, :, 1], 1.0 / P, qm1[:, b], MUL, ADD).then_inc(dve_ln1, 1)

            def moments(norm, b, g, s=None):
                stage, n = norm_number(norm, b, g)
                if norm == 3:
                    dve.wait_ge(tok_ready, b * 2 + g + 1)
                else:
                    dve.wait_ge(y_done, s * len(SCALAR_PAIRS) + sum(p // 2 <= g for p in SCALAR_PAIRS))
                    if g == 1:
                        dve.wait_ge(combined, (s + 1) * VECTOR_OPS)
                for t_ in range(TILES):
                    if norm == 3:
                        source = to_tok[:, t_ * P:(t_ + 1) * P]
                    else:
                        source = y[norm // 2 - 1][:, g, t_, :]
                    nc.vector.bn_stats(NB[stage][g][:, t_, :], source).then_inc(dve_ln[stage], 1)
                done = n * LN_STEPS
                even, odd = NB[stage][g][:, :, 1:3], NB[stage][g][:, :, 4:6]
                dve.wait_ge(dve_ln[stage], done + 4)
                tt(SM[stage][g][:], even, odd, ADD).then_inc(dve_ln[stage], 1)
                tt(DM[stage][g][:], even[:, :, 0], odd[:, :, 0], SUB).then_inc(dve_ln[stage], 1)
                if not early(n):
                    dve.wait_ge(pool_ln[stage], (n - 1) * 3)
                dve.wait_ge(dve_ln[stage], done + 5)
                ts_(NM[stage][g][:], SM[stage][g][:, :, 0], -0.5, None, MUL).then_inc(dve_ln[stage], 1)
                dve.wait_ge(dve_ln[stage], done + 6)
                stt(QM[stage][g][:], DM[stage][g][:], 0.25, DM[stage][g][:], MUL, MUL).then_inc(dve_ln[stage], 1)
                dve.wait_ge(dve_ln[stage], done + 8)
                stt(VR[stage][g][:], SM[stage][g][:, :, 1], 1.0 / P, QM[stage][g][:], MUL,
                    ADD).then_inc(dve_ln[stage], 1)

            def spread(ap):
                return ap.unsqueeze(2).to_broadcast([P, NT, EXPERTS])

            def route_shift(s, l):
                dve.wait_ge(logits_done, s + 1)
                tt(logit[:], route_ps[:, 0:NT * EXPERTS].rearrange("p (a e) -> p a e", a=NT),
                   bias[l][:].unsqueeze(1).to_broadcast([P, NT, EXPERTS]), ADD).then_inc(dve_gate, 1)
                dve.wait_ge(dve_gate, s * GATE_STEPS + 1)
                nc.vector.tensor_reduce(peak[:], logit[:], AX.X, ALU.max).then_inc(dve_gate, 1)
                dve.wait_ge(dve_gate, s * GATE_STEPS + 2)
                tt(logit[:], logit[:], spread(peak[:]), SUB).then_inc(dve_gate, 1)

            def route_softmax(s):
                dve.wait_ge(exp_done, s + 1)
                nc.vector.tensor_reduce(total[:], expo[:], AX.X, ADD).then_inc(dve_gate, 1)
                dve.wait_ge(dve_gate, s * GATE_STEPS + 4)
                nc.vector.reciprocal(rtotal[:], total[:]).then_inc(dve_gate, 1)
                dve.wait_ge(dve_gate, s * GATE_STEPS + 5)
                tt(prob[:], expo[:], spread(rtotal[:]), MUL).then_inc(dve_gate, 1)
                dve.wait_ge(dve_gate, s * GATE_STEPS + 6)
                nc.vector.tensor_reduce(peak2[:], prob[:], AX.X, ALU.max).then_inc(dve_gate, 1)

            def route_pick(s, i, values):
                done = s * GATE_STEPS + 7 + 6 * i
                dve.wait_ge(dve_gate, done)
                tt(key[:], values[:], spread(peak2[:]), ALU.is_equal).then_inc(dve_gate, 1)
                dve.wait_ge(dve_gate, done + 1)
                tt(key[:], key[:], rank[:], MUL).then_inc(dve_gate, 1)
                dve.wait_ge(dve_gate, done + 2)
                nc.vector.tensor_reduce(top[:], key[:], AX.X, ALU.max).then_inc(dve_gate, 1)
                dve.wait_ge(dve_gate, done + 3)
                tt(pick[i][:], key[:], spread(top[:]), ALU.is_equal).then_inc(dve_gate, 1)

            def route_rest(s):
                dve.wait_ge(dve_gate, s * GATE_STEPS + 11)
                stt(rest[:], pick[0][:], -2.0, prob[:], MUL, ADD).then_inc(dve_gate, 1)
                dve.wait_ge(dve_gate, s * GATE_STEPS + 12)
                nc.vector.tensor_reduce(peak2[:], rest[:], AX.X, ALU.max).then_inc(dve_gate, 1)

            def route_weights(s, l):
                dve.wait_ge(dve_gate, s * GATE_STEPS + 17)
                tt(key[:], pick[0][:], pick[1][:], ADD).then_inc(dve_gate, 1)
                dve.wait_ge(dve_gate, s * GATE_STEPS + 18)
                tt(gate_w[l][:], key[:], prob[:], MUL).then_inc(dve_gate, 1)

            def route(s, l, part):
                if part == 0:
                    route_softmax(s)
                elif part == 1:
                    route_pick(s, 0, prob)
                elif part == 2:
                    route_rest(s)
                elif part == 3:
                    route_pick(s, 1, rest)
                elif part == 4:
                    route_weights(s, l)

            def hidden(s, l, unit, odd=False):
                g, kind = unit // 2, unit % 2
                dve.wait_ge(silu_done, s * 4 + unit + 1)
                dve.wait_ge(up_done, s * 4 + unit + 1)
                dst = (h_shared, h_routed)[kind][l]
                tt(dst[:, g, :], hidden_ps(unit, odd)[1][:], sil[:, kind, :], MUL).then_inc(h_done, 1)

            def start_sum(s, l, odd, g, x, norm=None):
                dve.wait_ge(o_ready, s * UNITS + g + 1)
                if norm is not None:
                    dve.wait_ge(normed[norm[0]], norm[1] + 1)
                tt(y[l][:, g], o_ps[(g + 2 * odd) % 4][:].rearrange("p (t c) -> p t c", t=TILES), x[:, g],
                   ADD).then_inc(combined, 1)

            def combine(s, l, odd, pair):
                if pair == 0:
                    dve.wait_ge(dve_gate, (s + 1) * GATE_STEPS)
                done = vector_pair(pair)
                for half in range(1 if pair in SCALAR_PAIRS else 2):
                    for e in range(half * HEADS, (half + 1) * HEADS):
                        for tile in range(2):
                            if e % HEADS == 0:
                                dve.wait_ge(o_ready, s * UNITS + 2 + 4 * pair + 2 * half + tile + 1)
                            if e == 0:
                                dve.wait_ge(combined, s * VECTOR_OPS + 2)
                            else:
                                dve.wait_ge(combined, s * VECTOR_OPS + done - 1)
                            sum_ = y[l][:, pair // 2, 2 * (pair % 2) + tile, :]
                            stt(sum_, expert_out(odd, half, tile, e), gate_w[l][:, 2 * pair + tile, e:e + 1], sum_,
                                MUL, ADD).then_inc(combined, 1)
                            done += 1

            def add_last_parts(s):
                p, done = part[:, (SCALAR_PAIRS.index(3) + len(SCALAR_PAIRS)) % 2], (s + 1) * 2 * len(SCALAR_PAIRS) - 2
                dve.wait_ge(y_done, (s + 1) * len(SCALAR_PAIRS) - 1)
                for tile in range(2):
                    dve.wait_ge(weighed, s * SCALAR_OPS + scalar_ops(3, tile))
                    tt(p[:, 0:2, tile], p[:, 0:2, tile], p[:, 2:4, tile], ADD).then_inc(part_added, 1)
                    dve.wait_ge(part_added, done + 3 * tile + 1)
                    tt(p[:, 0, tile], p[:, 0, tile], p[:, 1, tile], ADD).then_inc(part_added, 1)
                    dve.wait_ge(part_added, done + 3 * tile + 2)
                    dve.wait_ge(combined, s * VECTOR_OPS + vector_ops(3, 0, tile))
                    out_ = y[1][:, 1, 2 + tile, :]
                    tt(out_, out_, p[:, 0, tile], ADD).then_inc((part_added, y_done)[tile], 1)
                dve.wait_ge(part_added, done + 3)

            def normalise_last(b):
                stage, n = norm_number(4, b, 1)
                dve.wait_ge(tok4_free[1], (b + 1) * 16)
                dve.wait_ge(pool_ln[stage], (n + 1) * 3)
                for t_ in range(2, TILES):
                    last = ts_(tok4[:, 1, t_, :], y[1][:, 1, t_, :], RS[stage][1][:, t_:t_ + 1],
                               SH[stage][1][:, t_:t_ + 1], MUL, ADD)
                last.then_inc(normed_last, 1)

            def scan_state(i, g):
                lo, hi = g * GROUP, (g + 1) * GROUP
                for part in range(2):
                    dve.wait_ge(driven, i * 4 + 2 * g + part + 1)
                    start = col[:, 10 + part:11 + part] if g == 0 else state[part][:, lo - 1:lo]
                    nc.vector.tensor_tensor_scan(state[part][:, lo:hi], col[:, 6:7].to_broadcast([P, GROUP]),
                                                 drive[part][:, lo:hi], start, MUL, ADD).then_inc(scanned, 1)

            def add_state(i, g):
                lo, hi = g * GROUP, (g + 1) * GROUP
                dve.wait_ge(turned, i * 4 + 2 * g + 2)
                tt(drive[0][:, lo:hi], drive[0][:, lo:hi], drive[1][:, lo:hi], SUB).then_inc(summed, 1)
                dve.wait_ge(summed, i * 2 + g + 1)
                tt(zT[:, g, :], drive[0][:, lo:hi], x2T[:, g, :], ADD).then_inc(added, 1)

            table_steps = []

            def table_tick(ins):
                table_steps.append(0)
                ins.then_inc(dve_tab, 1)

            def large_tables():
                dve.wait_ge(pool_tab, TAB_STEPS)
                for j in range(SMALL_TABLES, DOUBLINGS):
                    double_tables(nc.vector, dve, dve_tab, table_steps, j)

            def input_factors(step):
                tmp = table_tmp
                pr, pi = phazor_init[:, 0:1], phazor_init[:, 1:2]
                if step == 0:
                    dve.wait_ge(dve_tab, len(table_steps))
                    table_tick(ts_(in_re[:], cosT[:], pr, None, MUL))
                elif step == 1:
                    table_tick(ts_(in_im[:], cosT[:], pi, None, MUL))
                else:
                    table_tick(ts_(tmp, sinT[:], pr, None, MUL))
                    dve.wait_ge(dve_tab, len(table_steps) - 2)
                    table_tick(stt(in_re[:], sinT[:], pi, in_re[:], MUL, ADD))
                    dve.wait_ge(dve_tab, len(table_steps) - 1)
                    table_tick(tt(in_im[:], in_im[:], tmp, SUB))
                    assert len(table_steps) == DVE_TAB_STEPS, len(table_steps)

            def experts0(i, mid=True):
                s = s_next(i)
                for g in range(2):
                    start_sum(s, 0, True, g, tok1, norm_number(2, i, g))
                combine(s, 0, True, 0)
                if mid:
                    moments(4, i - 1, 0, s_mid(i))
                else:
                    inverse_transform(1, 1)
                combine(s, 0, True, 1)
                if mid:
                    moments(4, i - 1, 1, s_mid(i))
                else:
                    dve.wait_ge(pool_inv, 2 * len(INV_POOL))
                    dve.wait_ge(dve_inv, 2 * len(INV_DVE))
                    moments1(2)
                combine(s, 0, True, 2)
                if not mid:
                    moments1(3)
                moments(2, i + 1, 0, s)
                combine(s, 0, True, 3)
                route_shift(s + 1, 1)

            def start():
                for g in range(2):
                    start_sum(0, 0, False, g, tok1)
                combine(0, 0, False, 0)
                input_factors(0)
                combine(0, 0, False, 1)
                input_factors(1)
                combine(0, 0, False, 2)
                forward_transform(nc.vector, dve, 1, 3)
                moments(2, 0, 0, 0)
                combine(0, 0, False, 3)
                input_factors(2)
                for n in range(BLOCKS):
                    multiply_spectra(1, n)
                    if n == 1:
                        moments(2, 0, 1, 0)
                for unit in range(4):
                    hidden(1, 0, unit)
                    if unit == 1:
                        scan_state(0, 0)
                route_shift(1, 0)
                scan_state(0, 1)
                add_state(0, 0)
                route(1, 0, 0)
                add_state(0, 1)
                moments(3, 0, 0)
                for part in range(1, 5):
                    route(1, 0, part)
                inverse_transform(1, 0)
                moments(3, 0, 1)
                experts0(0, mid=False)

            def body(i, more=True):
                hidden(s_mid(i), 1, 0, odd=True)
                hidden(s_mid(i), 1, 1, odd=True)
                moments(2, i, 1, s_mid(i) - 1)
                hidden(s_mid(i), 1, 2, odd=True)
                route(s_mid(i), 1, 0)
                route(s_mid(i), 1, 1)
                hidden(s_mid(i), 1, 3, odd=True)
                scan_state(i, 0)
                route(s_mid(i), 1, 2)
                if more:
                    hidden(s_next(i), 0, 0, odd=True)
                route(s_mid(i), 1, 3)
                if more:
                    hidden(s_next(i), 0, 1, odd=True)
                route(s_mid(i), 1, 4)
                if more:
                    add_state(i, 0)
                    hidden(s_next(i), 0, 2, odd=True)
                    scan_state(i, 1)
                    hidden(s_next(i), 0, 3, odd=True)
                    route_shift(s_next(i), 0)
                for g in range(2):
                    start_sum(s_mid(i), 1, False, g, tok3, norm_number(4, i - 2, g))
                if more:
                    moments(3, i, 0)
                combine(s_mid(i), 1, False, 0)
                if more:
                    add_state(i, 1)
                    route(s_next(i), 0, 0)
                else:
                    add_state(i, 0)
                    scan_state(i, 1)
                combine(s_mid(i), 1, False, 1)
                if more:
                    route(s_next(i), 0, 1)
                    route(s_next(i), 0, 2)
                else:
                    moments(3, i, 0)
                    add_state(i, 1)
                combine(s_mid(i), 1, False, 2)
                moments(3, i, 1)
                combine(s_mid(i), 1, False, 3)
                if more:
                    route(s_next(i), 0, 3)
                    route(s_next(i), 0, 4)
                    experts0(i)
                else:
                    moments(4, i - 1, 0, s_mid(i))

            for quarter in range(4):
                forward_transform(nc.vector, dve, 0, quarter)
            for n in range(BLOCKS):
                if n == BLOCKS - 1:
                    keep_filter0()
                multiply_spectra(0, n)
            for step in range(2):
                inverse_transform(0, step)
            dve.wait_ge(pool_inv, len(INV_POOL))
            dve.wait_ge(dve_inv, len(INV_DVE))
            moments1(0)
            moments1(1)
            large_tables()
            dve.wait_ge(weights_loaded[0], 16 * 6)
            hidden(0, 0, 0, odd=True)
            hidden(0, 0, 1, odd=True)
            route_shift(0, 0)
            for step in range(5):
                if step == 2:
                    hidden(0, 0, 2, odd=True)
                    hidden(0, 0, 3, odd=True)
                route(0, 0, step)
            dve.wait_ge(weights_loaded[1], 16 * 6)
            start()
            with dve.Fori(1, BATCH - 1) as i:
                body(i)
            body(BATCH - 1, more=False)
            final = 2 * BATCH - 1
            hidden(final, 1, 0)
            hidden(final, 1, 1)
            moments(4, BATCH - 2, 1, final - 1)
            route_shift(final, 1)
            route(final, 1, 0)
            route(final, 1, 1)
            hidden(final, 1, 2)
            hidden(final, 1, 3)
            route(final, 1, 2)
            route(final, 1, 3)
            route(final, 1, 4)
            for g in range(2):
                start_sum(final, 1, True, g, tok3, norm_number(4, BATCH - 2, g))
            for pair in range(4):
                combine(final, 1, True, pair)
                if pair == 2:
                    moments(4, BATCH - 1, 0, final)
            add_last_parts(final)
            moments(4, BATCH - 1, 1, final)
            normalise_last(BATCH - 1)


INPUTS = ["L0_attn_x", "L0_attn_t", "L0_ffn_w_shared_in", "L0_ffn_w_shared_out", "L0_ffn_w1_shared", "L0_ffn_w2",
          "L0_ffn_w_gate", "L0_ffn_gate_bias", "L1_attn_phazor", "L1_attn_phazor_init", "L1_attn_last_conv_re",
          "L1_attn_last_conv_im", "L1_ffn_w_shared_in", "L1_ffn_w_shared_out", "L1_ffn_w1_shared", "L1_ffn_w2",
          "L1_ffn_w_gate", "L1_ffn_gate_bias"]


def kernel(**inputs):
    import concourse.bacc as bacc
    from concourse.bass_utils import run_bass_kernel_spmd

    nc = bacc.Bacc("TRN2", target_bir_lowering=False, num_devices=1)
    arrays, aps = {}, {}
    for name, value in [(n, inputs[n]) for n in INPUTS] + list(constants().items()):
        a = np.ascontiguousarray(value)
        arrays[f"in_{name}"] = a
        aps[name] = nc.dram_tensor(f"in_{name}", a.shape, mybir.dt.from_np(a.dtype), kind="ExternalInput").ap()
    out = nc.dram_tensor("out_0", (BATCH, TIME, P), F32, kind="ExternalOutput").ap()
    build(nc, aps, out)
    r = run_bass_kernel_spmd(nc, [arrays], core_ids=[0])
    return r.results[0]["out_0"]
```
